# Optimizing a Trainium2 kernel written in Bass

```python
import numpy as np
import jax
import jax.numpy as jnp

def _softmax(x, axis=-1):
    return jax.nn.softmax(x, axis=axis)

def _gelu(x):
    return jax.nn.gelu(x, approximate=True)

def _silu(x):
    return jax.nn.silu(x)

def _sigmoid(x):
    return jax.nn.sigmoid(x)

def _layernorm(x, axis=-1, eps=1e-05):
    m = jnp.mean(x, axis=axis, keepdims=True)
    v = jnp.var(x, axis=axis, keepdims=True)
    return (x - m) / jnp.sqrt(v + eps)

def _scatter_add(tgt, idx, src, axis=0):
    return tgt.at[idx].add(src)

def _segment_sum(src, seg, n):
    return jax.ops.segment_sum(src, seg, n)
kernel_name = 'mk_sandwich_d1_jaxref_r4_2f2326'

def setup_inputs(seed: int=0):
    np.random.seed(seed)
    _w = jnp.asarray

    def _L0_attn_setup():
        import jax, jax.numpy as jnp
        import numpy as np
        from jax import lax
        SHIFT = 1
        GAMMA = 0.25

        def q_shift_1d(x, shift=SHIFT, gamma=GAMMA):
            B, T, C = x.shape
            c1 = int(C * gamma)
            c2 = int(C * gamma * 2)
            fwd = jnp.pad(x[:, :T - shift, :c1], ((0, 0), (shift, 0), (0, 0)))
            bwd = jnp.pad(x[:, shift:, c1:c2], ((0, 0), (0, shift), (0, 0)))
            return jnp.concatenate([fwd, bwd, x[:, :, c2:]], axis=-1)

        def wkv_scan(w, u, k, v):
            B, T, C = k.shape
            ew = jnp.exp(w)

            def step(carry, kv):
                a, b = carry
                kt, vt = kv
                eku = jnp.exp(u + kt)
                out = (a + eku * vt) / (b + eku)
                ek = jnp.exp(kt)
                return ((a * ew + ek * vt, b * ew + ek), out)
            k_t = jnp.moveaxis(k, 1, 0)
            v_t = jnp.moveaxis(v, 1, 0)
            init = (jnp.zeros((B, C), k.dtype), jnp.zeros((B, C), k.dtype))
            _, ys = lax.scan(step, init, (k_t, v_t))
            return jnp.moveaxis(ys, 0, 1)
        key = jax.random.key(seed)
        ks = jax.random.split(key, 10)
        B, T, C = (8, 1024, 256)
        s = 1.0 / np.sqrt(C)
        return {'x': jax.random.normal(ks[0], (B, T, C), jnp.float32), 'Wk': jax.random.normal(ks[1], (C, C), jnp.float32) * s, 'Wv': jax.random.normal(ks[2], (C, C), jnp.float32) * s, 'Wr': jax.random.normal(ks[3], (C, C), jnp.float32) * s, 'Wo': jax.random.normal(ks[4], (C, C), jnp.float32) * s, 'spatial_decay': jax.random.normal(ks[5], (C,), jnp.float32), 'spatial_first': jax.random.normal(ks[6], (C,), jnp.float32), 'mix_k': jax.random.uniform(ks[7], (C,), jnp.float32), 'mix_v': jax.random.uniform(ks[8], (C,), jnp.float32), 'mix_r': jax.random.uniform(ks[9], (C,), jnp.float32)}
    _L0_attn_in = _L0_attn_setup()

    def _L0_ffn_setup():
        import jax, jax.numpy as jnp
        import numpy as np
        DIM = 256
        INTER = 256
        E = 8
        TOPK = 2
        ROUTE_SCALE = 1.0
        SHARED_INTER = 512
        B, S = (4, 512)

        def _moe_forward(x, gate_w, gate_b, w1, b1, w3, b3, w2, b2, ws1, bs1, ws3, bs3, ws2, bs2):
            Bq, Sq, D = x.shape
            xt = x.reshape(-1, D)
            logits = (xt @ gate_w.T + gate_b).astype(jnp.float32)
            scores = jax.nn.softmax(logits, axis=-1)
            top_w, top_i = jax.lax.top_k(scores, TOPK)
            weights = (top_w * ROUTE_SCALE).astype(x.dtype)
            gate_dense = jnp.sum(jax.nn.one_hot(top_i, E, dtype=x.dtype) * weights[..., None], axis=1)

            def expert(w1e, b1e, w3e, b3e, w2e, b2e):
                h = jax.nn.silu(xt @ w1e.T + b1e) * (xt @ w3e.T + b3e)
                return h @ w2e.T + b2e
            outs = jax.vmap(expert)(w1, b1, w3, b3, w2, b2)
            y = jnp.einsum('etd,te->td', outs, gate_dense)
            z = jax.nn.silu(xt @ ws1.T + bs1) * (xt @ ws3.T + bs3) @ ws2.T + bs2
            return (y + z).reshape(Bq, Sq, D)
        key = jax.random.key(seed)
        ks = jax.random.split(key, 10)

        def w(k, shape, scale=0.02):
            return jax.random.normal(k, shape, jnp.float32) * scale
        return {'x': jax.random.normal(ks[0], (B, S, DIM), jnp.float32), 'gate_w': w(ks[1], (E, DIM)), 'gate_b': jnp.zeros((E,), jnp.float32), 'w1': w(ks[2], (E, INTER, DIM)), 'b1': jnp.zeros((E, INTER), jnp.float32), 'w3': w(ks[3], (E, INTER, DIM)), 'b3': jnp.zeros((E, INTER), jnp.float32), 'w2': w(ks[4], (E, DIM, INTER)), 'b2': jnp.zeros((E, DIM), jnp.float32), 'ws1': w(ks[5], (SHARED_INTER, DIM)), 'bs1': jnp.zeros((SHARED_INTER,), jnp.float32), 'ws3': w(ks[6], (SHARED_INTER, DIM)), 'bs3': jnp.zeros((SHARED_INTER,), jnp.float32), 'ws2': w(ks[7], (DIM, SHARED_INTER)), 'bs2': jnp.zeros((DIM,), jnp.float32)}
    _L0_ffn_in = _L0_ffn_setup()
    _d = {'L0_attn_x': _L0_attn_in['x'], 'L0_attn_Wk': _L0_attn_in['Wk'], 'L0_attn_Wv': _L0_attn_in['Wv'], 'L0_attn_Wr': _L0_attn_in['Wr'], 'L0_attn_Wo': _L0_attn_in['Wo'], 'L0_attn_spatial_decay': _L0_attn_in['spatial_decay'], 'L0_attn_spatial_first': _L0_attn_in['spatial_first'], 'L0_attn_mix_k': _L0_attn_in['mix_k'], 'L0_attn_mix_v': _L0_attn_in['mix_v'], 'L0_attn_mix_r': _L0_attn_in['mix_r'], 'L0_ffn_gate_w': _L0_ffn_in['gate_w'], 'L0_ffn_gate_b': _L0_ffn_in['gate_b'], 'L0_ffn_w1': _L0_ffn_in['w1'], 'L0_ffn_b1': _L0_ffn_in['b1'], 'L0_ffn_w3': _L0_ffn_in['w3'], 'L0_ffn_b3': _L0_ffn_in['b3'], 'L0_ffn_w2': _L0_ffn_in['w2'], 'L0_ffn_b2': _L0_ffn_in['b2'], 'L0_ffn_ws1': _L0_ffn_in['ws1'], 'L0_ffn_bs1': _L0_ffn_in['bs1'], 'L0_ffn_ws3': _L0_ffn_in['ws3'], 'L0_ffn_bs3': _L0_ffn_in['bs3'], 'L0_ffn_ws2': _L0_ffn_in['ws2'], 'L0_ffn_bs2': _L0_ffn_in['bs2']}
    _x0 = _d['L0_attn_x']
    _d['L0_attn_x'] = jax.random.normal(jax.random.fold_in(jax.random.key(seed), 1), (16, 512, 256), dtype=_x0.dtype)
    del _x0
    return _d

def reference(L0_attn_x, L0_attn_Wk, L0_attn_Wv, L0_attn_Wr, L0_attn_Wo, L0_attn_spatial_decay, L0_attn_spatial_first, L0_attn_mix_k, L0_attn_mix_v, L0_attn_mix_r, L0_ffn_gate_w, L0_ffn_gate_b, L0_ffn_w1, L0_ffn_b1, L0_ffn_w3, L0_ffn_b3, L0_ffn_w2, L0_ffn_b2, L0_ffn_ws1, L0_ffn_bs1, L0_ffn_ws3, L0_ffn_bs3, L0_ffn_ws2, L0_ffn_bs2):

    def _L0_attn_ref(x, Wk, Wv, Wr, Wo, spatial_decay, spatial_first, mix_k, mix_v, mix_r):
        import jax, jax.numpy as jnp
        import numpy as np
        from jax import lax
        SHIFT = 1
        GAMMA = 0.25

        def q_shift_1d(x, shift=SHIFT, gamma=GAMMA):
            B, T, C = x.shape
            c1 = int(C * gamma)
            c2 = int(C * gamma * 2)
            fwd = jnp.pad(x[:, :T - shift, :c1], ((0, 0), (shift, 0), (0, 0)))
            bwd = jnp.pad(x[:, shift:, c1:c2], ((0, 0), (0, shift), (0, 0)))
            return jnp.concatenate([fwd, bwd, x[:, :, c2:]], axis=-1)

        def wkv_scan(w, u, k, v):
            B, T, C = k.shape
            ew = jnp.exp(w)

            def step(carry, kv):
                a, b = carry
                kt, vt = kv
                eku = jnp.exp(u + kt)
                out = (a + eku * vt) / (b + eku)
                ek = jnp.exp(kt)
                return ((a * ew + ek * vt, b * ew + ek), out)
            k_t = jnp.moveaxis(k, 1, 0)
            v_t = jnp.moveaxis(v, 1, 0)
            init = (jnp.zeros((B, C), k.dtype), jnp.zeros((B, C), k.dtype))
            _, ys = lax.scan(step, init, (k_t, v_t))
            return jnp.moveaxis(ys, 0, 1)
        B, T, C = x.shape
        xx = q_shift_1d(x)
        xk = x * mix_k + xx * (1.0 - mix_k)
        xv = x * mix_v + xx * (1.0 - mix_v)
        xr = x * mix_r + xx * (1.0 - mix_r)
        k = jnp.einsum('btc,oc->bto', xk, Wk)
        v = jnp.einsum('btc,oc->bto', xv, Wv)
        r = jnp.einsum('btc,oc->bto', xr, Wr)
        sr = jax.nn.sigmoid(r)
        wkv_out = wkv_scan(spatial_decay / T, spatial_first / T, k, v)
        return jnp.einsum('btc,oc->bto', sr * wkv_out, Wo)

    def _L0_ffn_ref(x, gate_w, gate_b, w1, b1, w3, b3, w2, b2, ws1, bs1, ws3, bs3, ws2, bs2):
        import jax, jax.numpy as jnp
        import numpy as np
        DIM = 256
        INTER = 256
        E = 8
        TOPK = 2
        ROUTE_SCALE = 1.0
        SHARED_INTER = 512
        B, S = (4, 512)

        def _moe_forward(x, gate_w, gate_b, w1, b1, w3, b3, w2, b2, ws1, bs1, ws3, bs3, ws2, bs2):
            Bq, Sq, D = x.shape
            xt = x.reshape(-1, D)
            logits = (xt @ gate_w.T + gate_b).astype(jnp.float32)
            scores = jax.nn.softmax(logits, axis=-1)
            top_w, top_i = jax.lax.top_k(scores, TOPK)
            weights = (top_w * ROUTE_SCALE).astype(x.dtype)
            gate_dense = jnp.sum(jax.nn.one_hot(top_i, E, dtype=x.dtype) * weights[..., None], axis=1)

            def expert(w1e, b1e, w3e, b3e, w2e, b2e):
                h = jax.nn.silu(xt @ w1e.T + b1e) * (xt @ w3e.T + b3e)
                return h @ w2e.T + b2e
            outs = jax.vmap(expert)(w1, b1, w3, b3, w2, b2)
            y = jnp.einsum('etd,te->td', outs, gate_dense)
            z = jax.nn.silu(xt @ ws1.T + bs1) * (xt @ ws3.T + bs3) @ ws2.T + bs2
            return (y + z).reshape(Bq, Sq, D)
        return _moe_forward(x, gate_w, gate_b, w1, b1, w3, b3, w2, b2, ws1, bs1, ws3, bs3, ws2, bs2)
    x = L0_attn_x
    x = x + _layernorm(_L0_attn_ref(_layernorm(x, axis=-1), L0_attn_Wk, L0_attn_Wv, L0_attn_Wr, L0_attn_Wo, L0_attn_spatial_decay, L0_attn_spatial_first, L0_attn_mix_k, L0_attn_mix_v, L0_attn_mix_r), axis=-1)
    x = x + _layernorm(_L0_ffn_ref(_layernorm(x, axis=-1), L0_ffn_gate_w, L0_ffn_gate_b, L0_ffn_w1, L0_ffn_b1, L0_ffn_w3, L0_ffn_b3, L0_ffn_w2, L0_ffn_b2, L0_ffn_ws1, L0_ffn_bs1, L0_ffn_ws3, L0_ffn_bs3, L0_ffn_ws2, L0_ffn_bs2), axis=-1)
    return x

_drawn_inputs = setup_inputs


def setup_inputs(seed=0):
    import zlib

    import numpy as np

    out = dict(_drawn_inputs(seed))
    spreads = {'L0_ffn_gate_b': (0.0, 0.1),
     'L0_ffn_b1': (0.0, 0.8),
     'L0_ffn_b3': (0.0, 0.8),
     'L0_ffn_b2': (0.0, 0.1),
     'L0_ffn_bs1': (0.0, 0.1),
     'L0_ffn_bs3': (0.0, 0.1),
     'L0_ffn_bs2': (0.0, 0.1)}
    factors = {'L0_attn_spatial_first': 200.0}
    for name, (base, spread) in spreads.items():
        noise = np.random.default_rng([zlib.crc32(name.encode()), seed]).standard_normal(out[name].shape)
        drawn = base * np.exp(spread * noise) if base else spread * noise
        out[name] = jnp.asarray(drawn.astype(out[name].dtype))
    for name, factor in factors.items():
        out[name] = (out[name] * factor).astype(out[name].dtype)
    return out
```

```python
from contextlib import ExitStack

import concourse.bass as bass
from concourse import mybir

F32 = mybir.dt.float32
F32R = mybir.dt.float32r
ALU = mybir.AluOpType
ACT = mybir.ActivationFunctionType

P = 128
EPS = 1e-5


def inside(s, n):
    return not isinstance(s, int) or 0 <= s < n


def wait(eng, sem, count):
    if not isinstance(count, int) or count > 0:
        eng.wait_ge(sem, count)


def hold(pool, scratch, held, step, *waits):
    for sem, count in waits:
        wait(pool, sem, count)
    wait(pool, held, step)
    pool.tensor_tensor(scratch[:, 0:1], scratch[:, 1:2], scratch[:, 1:2], ALU.add).then_inc(held, 1)


SCALES = 4
HALF, PER_ROW, EPSILON, MINUS_HALF = range(4)


def scale_constants(pool, consts, row, ready):
    for k, v in ((HALF, 0.5), (PER_ROW, 1.0 / row), (EPSILON, EPS), (MINUS_HALF, -0.5)):
        pool.memset(consts[:, k, :], v).then_inc(ready, 1)
    pool.wait_ge(ready, 4)


def layernorm_scales(pool, consts, stats, sums, half_diff, var, mean, rstd, ordered, s, ready):
    pool.tensor_tensor(sums[:, :, :], stats[:, :, 1:3], stats[:, :, 4:6], ALU.add)
    pool.tensor_tensor(half_diff[:, :], stats[:, :, 1], stats[:, :, 4], ALU.subtract).then_inc(ordered, 1)
    pool.wait_ge(ordered, s * SCALES + 1)
    pool.tensor_tensor(mean[:, :], sums[:, :, 0], consts[:, HALF, :], ALU.mult)
    pool.tensor_tensor(half_diff[:, :], half_diff[:, :], consts[:, HALF, :], ALU.mult)
    pool.tensor_tensor(var[:, :], sums[:, :, 1], consts[:, PER_ROW, :], ALU.mult).then_inc(ordered, 1)
    pool.wait_ge(ordered, s * SCALES + 2)
    pool.tensor_tensor(half_diff[:, :], half_diff[:, :], half_diff[:, :], ALU.mult)
    pool.tensor_tensor(var[:, :], var[:, :], consts[:, EPSILON, :], ALU.add).then_inc(ordered, 1)
    pool.wait_ge(ordered, s * SCALES + 3)
    pool.tensor_tensor(var[:, :], var[:, :], half_diff[:, :], ALU.add).then_inc(ordered, 1)
    pool.wait_ge(ordered, s * SCALES + 4)
    pool.tensor_tensor(rstd[:, :], var[:, :], consts[:, MINUS_HALF, :], ALU.pow).then_inc(ready, 1)


def landed(s, parity, dmas=1):
    return (s - parity + 2) * (8 * dmas)


def steps(eng, body, first, loop_first, loop_end, end):
    for i in range(first, loop_first):
        body(i, i % 2)
    with eng.Fori(loop_first // 2, loop_end // 2) as pair:
        body(pair * 2, 0)
        body(pair * 2 + 1, 1)
    for i in range(loop_end, end):
        body(i, i % 2)


def time_mix(nc, x, attn_w, mix, decay, first, ident, ffn_w, x1_dram, xf_dram, ffn_hi, ffn_lo, slots_x):
    SEQS, T, C = x.shape
    SUBS = T // P
    CC = C // P
    SHIFTED = C // 4
    assert CC == 2 and SUBS == 4 and 2 * SHIFTED == P and T == 512 and SEQS % 2 == 0
    K, V, R = range(3)
    HERE, SHIFT, REST = range(3)

    with ExitStack() as ctx:
        def sb(name, shape, dt=F32):
            return ctx.enter_context(nc.sbuf_tensor(name, shape, dt))

        def psum(name, shape):
            return ctx.enter_context(nc.psum_tensor(name, shape, F32))

        def sem(name):
            return ctx.enter_context(nc.semaphore(name))

        eye = sb("eye", [P, P])
        w_raw = sb("w_raw", [P, 4, CC, C])
        w_mixed = sb("w_mixed", [P, 3, 3, C])
        w_hi = sb("w_hi", [P, 3, 3, C], F32R)
        w_lo = sb("w_lo", [P, 3, 3, C], F32R)
        wo_hi = sb("wo_hi", [P, CC, C], F32R)
        wo_lo = sb("wo_lo", [P, CC, C], F32R)
        mix_c = sb("mix_c", [P, 3, CC])
        unmix = sb("unmix", [P, 3, CC])
        both = sb("both", [P, 3, CC])
        decay_c = sb("decay_c", [P, CC])
        first_c = sb("first_c", [P, CC])
        ew = sb("ew", [P, CC])
        u = sb("u", [P, CC])
        scale_c = sb("scale_c", [P, 4, SUBS])

        x_in = [sb(f"x_in{p}", [P, SUBS, C]) for p in range(2)]
        x_res = [sb(f"x_res{p}", [P, SUBS, C]) for p in range(2)]
        xn = sb("xn", [P, SUBS, C])
        z_hi = [sb(f"z_hi{p}", [P, CC, T], F32R) for p in range(2)]
        z_lo = [sb(f"z_lo{p}", [P, CC, T], F32R) for p in range(2)]
        zs_hi = [sb(f"zs_hi{p}", [P, T], F32R) for p in range(2)]
        zs_lo = [sb(f"zs_lo{p}", [P, T], F32R) for p in range(2)]
        ek = [sb(f"ek{c}", [P, T]) for c in range(CC)]
        eku = [sb(f"eku{c}", [P, T]) for c in range(CC)]
        er = [sb(f"er{c}", [P, T]) for c in range(CC)]
        ekv = [sb(f"ekv{c}", [P, T]) for c in range(CC)]
        a_sum = [sb(f"a_sum{c}", [P, T + 1]) for c in range(CC)]
        b_sum = [sb(f"b_sum{c}", [P, T + 1]) for c in range(CC)]
        num = [sb(f"num{c}", [P, T]) for c in range(CC)]
        den = [sb(f"den{c}", [P, T]) for c in range(CC)]
        g = [sb(f"g{c}", [P, T]) for c in range(CC)]
        g_hi = [sb(f"g_hi{p}", [P, CC, T], F32R) for p in range(2)]
        g_lo = [sb(f"g_lo{p}", [P, CC, T], F32R) for p in range(2)]
        on = sb("on", [P, SUBS, C])
        x1 = [sb(f"x1{p}", [P, SUBS, C]) for p in range(2)]
        xf = [sb(f"xf{p}", [P, SUBS, C]) for p in range(2)]
        piece = ffn_w.shape[1] // SEQS
        fw = [sb(f"fw{p}", [P, piece]) for p in range(2)]
        fw_hi = [sb(f"fw_hi{p}", [P, piece], F32R) for p in range(2)]
        fw_lo = [sb(f"fw_lo{p}", [P, piece], F32R) for p in range(2)]
        clear_rows = slots_x.shape[0] // SEQS // P
        zeros = sb("zeros", [P, clear_rows * C])
        LN_X, LN_O, LN_X1 = range(3)
        stats = [[sb(f"stats{k}{p}", [P, SUBS, 6]) for p in range(2)] for k in range(3)]
        sums = [[sb(f"sums{k}{p}", [P, SUBS, 2]) for p in range(2)] for k in range(3)]
        half_diff = [[sb(f"half_diff{k}{p}", [P, SUBS]) for p in range(2)] for k in range(3)]
        var = [[sb(f"var{k}{p}", [P, SUBS]) for p in range(2)] for k in range(3)]
        mean = [[sb(f"mean{k}{p}", [P, SUBS]) for p in range(2)] for k in range(3)]
        rstd = [[sb(f"rstd{k}{p}", [P, SUBS]) for p in range(2)] for k in range(3)]

        k_ps = [psum(f"k_ps{c}", [P, T]) for c in range(CC)]
        v_ps = [psum(f"v_ps{c}", [P, T]) for c in range(CC)]
        r_ps = [psum(f"r_ps{c}", [P, T]) for c in range(CC)]
        turn_ps = psum("turn_ps", [P, CC, T])
        o_ps = turn_ps[:, :, :].rearrange("p a (b n) -> p (a b) n", n=C)

        consts_in = sem("consts_in")
        consts_done = sem("consts_done")
        w_in = sem("w_in")
        zs_cleared = sem("zs_cleared")
        mixes_ready = sem("mixes_ready")
        mixed_ready = sem("mixed_ready")
        w_ready = sem("w_ready")
        u_ready = sem("u_ready")
        ew_ready = sem("ew_ready")
        x_loaded = [sem(f"x_loaded{p}") for p in range(2)]
        res_loaded = [sem(f"res_loaded{p}") for p in range(2)]
        stats_ready = [sem(f"stats_ready{k}") for k in range(3)]
        scales_ordered = [sem(f"scales_ordered{k}") for k in range(3)]
        rstd_ready = [sem(f"rstd_ready{k}") for k in range(3)]
        xn_ready = sem("xn_ready")
        turned = sem("turned")
        zhi_ready = sem("zhi_ready")
        zlo_ready = sem("zlo_ready")
        zs_ready = [sem(f"zs_ready{p}") for p in range(2)]
        kvr_done = sem("kvr_done")
        exps_ready = sem("exps_ready")
        ekv_ready = sem("ekv_ready")
        v_used = sem("v_used")
        scans_ready = sem("scans_ready")
        num_ready = sem("num_ready")
        bd_ready = sem("bd_ready")
        den_ready = sem("den_ready")
        rec_ready = sem("rec_ready")
        g_ready = sem("g_ready")
        ghi_ready = sem("ghi_ready")
        glo_ready = sem("glo_ready")
        o_done = sem("o_done")
        on_ready = sem("on_ready")
        x1_ready = sem("x1_ready")
        xf_ready = sem("xf_ready")
        x1_stored = [sem(f"x1_stored{p}") for p in range(2)]
        xf_stored = [sem(f"xf_stored{p}") for p in range(2)]
        fw_loaded = [sem(f"fw_loaded{p}") for p in range(2)]
        fw_stored = [sem(f"fw_stored{p}") for p in range(2)]
        fwhi_ready = sem("fwhi_ready")
        fwlo_ready = sem("fwlo_ready")
        zeros_ready = sem("zeros_ready")
        cleared = sem("cleared")
        block = ctx.enter_context(nc.Block())

        LOOP = (4, SEQS - 2)

        @block.sync
        def _(sp):
            sp.dma_start(eye[:, :], ident).then_inc(consts_in, 16)
            sp.dma_start(mix_c[:, :, :], mix).then_inc(consts_in, 16)
            sp.dma_start(decay_c[:, :], decay).then_inc(consts_in, 16)
            sp.dma_start(first_c[:, :], first).then_inc(consts_in, 16)
            sp.dma_start(w_raw[:, :, :, :], attn_w).then_inc(w_in, 16)

            def body(i, par):
                n = i + 2
                if inside(n, SEQS):
                    wait(sp, xn_ready, n - 1)
                    sp.dma_start(x_in[par][:, :, :], x[n, :, :].rearrange("(j p) c -> p j c", p=P))\
                        .then_inc(x_loaded[par], 16)
                s = i + 1
                if inside(s, SEQS):
                    q = 1 - par
                    for ready, z, zs in ((zhi_ready, z_hi[q][:, 0, :].bitcast(F32), zs_hi[q][:, :].bitcast(F32)),
                                         (zlo_ready, z_lo[q][:, 0, :].bitcast(F32), zs_lo[q][:, :].bitcast(F32))):
                        sp.wait_ge(ready, s + 1)
                        sp.dma_start(zs[0:SHIFTED, 1:T], z[0:SHIFTED, 0:T - 1]).then_inc(zs_ready[q], 16)
                        sp.dma_start(zs[SHIFTED:P, 0:T - 1], z[SHIFTED:P, 1:T]).then_inc(zs_ready[q], 16)
                if inside(i, SEQS):
                    wait(sp, x1_ready, i - 1)
                    sp.dma_start(x_res[par][:, :, :], x[i, :, :].rearrange("(j p) c -> p j c", p=P))\
                        .then_inc(res_loaded[par], 16)
                if inside(i, SEQS):
                    if isinstance(i, int) and i == 0:
                        sp.wait_ge(zeros_ready, 1)
                    sp.dma_start(slots_x[bass.ds(i * (clear_rows * P), clear_rows * P), :]
                                 .rearrange("(p r) c -> p (r c)", p=P), zeros[:, :]).then_inc(cleared, 16)
                    wait(sp, fwlo_ready, i - 1)
                    sp.dma_start(fw[par][:, :], ffn_w[:, bass.ds(i * piece, piece)]).then_inc(fw_loaded[par], 16)
                s = i - 1
                if inside(s, SEQS):
                    sp.wait_ge(x1_ready, s + 1)
                    sp.dma_start(x1_dram[s, :, :].rearrange("(j p) c -> p j c", p=P), x1[1 - par][:, :, :])\
                        .then_inc(x1_stored[1 - par], 16)
                s = i - 1
                if inside(s, SEQS):
                    q = 1 - par
                    sp.wait_ge(fwlo_ready, s + 1)
                    sp.dma_start(ffn_hi[:, bass.ds(s * piece, piece)], fw_hi[q][:, :].bitcast(F32))\
                        .then_inc(fw_stored[q], 16)
                    sp.dma_start(ffn_lo[:, bass.ds(s * piece, piece)], fw_lo[q][:, :].bitcast(F32))\
                        .then_inc(fw_stored[q], 16)
                s = i - 2
                if inside(s, SEQS):
                    sp.wait_ge(xf_ready, s + 1)
                    sp.dma_start(xf_dram[s, :, :].rearrange("(j p) c -> p j c", p=P), xf[par][:, :, :])\
                        .then_inc(xf_stored[par], 16)

            steps(sp, body, -2, *LOOP, SEQS + 2)
            sp.wait_ge(cleared, 16 * SEQS)
            for p in range(2):
                sp.wait_ge(fw_stored[p], 16 * SEQS)
                sp.wait_ge(x1_stored[p], 16 * (SEQS // 2))
                sp.wait_ge(xf_stored[p], 16 * (SEQS // 2))

        @block.tensor
        def _(pe):
            pe.wait_ge(consts_in, 64)

            def turn(s, p):
                if not inside(s, SEQS):
                    return
                pe.wait_ge(xn_ready, s + 1)
                wait(pe, on_ready, s - 2)
                for c in range(CC):
                    for j in range(SUBS):
                        last = pe.transpose(turn_ps[:, c, j * P:(j + 1) * P], xn[:, j, c * P:(c + 1) * P], eye[:, :])
                last.then_inc(turned, 1)

            def kvr(s, p, c):
                if not inside(s, SEQS):
                    return
                if c == 0:
                    if isinstance(s, int) and s == 0:
                        pe.wait_ge(w_ready, 1)
                    pe.wait_ge(zhi_ready, s + 1)
                    pe.wait_ge(zlo_ready, s + 1)
                    pe.wait_ge(zs_ready[p], landed(s, p, 4))
                wait(pe, exps_ready, 6 * s + 3 * c - 3)
                wait(pe, v_used, 2 * s + c - 1)
                for which, out in ((K, k_ps[c]), (V, v_ps[c]), (R, r_ps[c])):
                    n = 0
                    for part, hi, lo in ((HERE, z_hi[p][:, 0, :], z_lo[p][:, 0, :]),
                                         (REST, z_hi[p][:, 1, :], z_lo[p][:, 1, :]),
                                         (SHIFT, zs_hi[p][:, :], zs_lo[p][:, :])):
                        for w, z in ((w_hi, hi), (w_hi, lo), (w_lo, hi)):
                            last = pe.matmul(out[:, :], w[:, which, part, c * P:(c + 1) * P], z,
                                             start=(n == 0), stop=(n == 8))
                            n += 1
                last.then_inc(kvr_done, 1)

            def project(s, p):
                if not inside(s, SEQS):
                    return
                pe.wait_ge(glo_ready, 2 * s + 2)
                wait(pe, zlo_ready, min(s + 3, SEQS) if isinstance(s, int) else s + 3)
                wait(pe, on_ready, s)
                for j in range(SUBS):
                    n = 0
                    for c in range(CC):
                        for a, w in ((g_hi, wo_hi), (g_lo, wo_hi), (g_hi, wo_lo)):
                            last = pe.matmul(o_ps[:, j, :], a[p][:, c, j * P:(j + 1) * P], w[:, c, :],
                                             start=(n == 0), stop=(n == 5))
                            n += 1
                last.then_inc(o_done, 1)

            def body(i, par):
                kvr(i, par, 0)
                turn(i + 1, 1 - par)
                kvr(i, par, 1)
                project(i - 1, 1 - par)

            steps(pe, body, -1, *LOOP, SEQS + 1)

        @block.scalar
        def _(act):
            act.wait_ge(consts_in, 64)
            act.activation(ew[:, :], decay_c[:, :], ACT.Exp, scale=1.0 / T).then_inc(ew_ready, 1)
            act.wait_ge(u_ready, 1)

            def exps(s, c):
                if not inside(s, SEQS):
                    return
                act.wait_ge(kvr_done, 2 * s + c + 1)
                wait(act, den_ready, 2 * s + c - 1)
                act.activation(ek[c][:, :], k_ps[c][:, :], ACT.Exp).then_inc(exps_ready, 1)
                act.activation(eku[c][:, :], k_ps[c][:, :], ACT.Exp, bias=u[:, c:c + 1]).then_inc(exps_ready, 1)
                act.activation(er[c][:, :], r_ps[c][:, :], ACT.Exp, scale=-1.0).then_inc(exps_ready, 1)

            def high(s, p):
                if not inside(s, SEQS):
                    return
                act.wait_ge(turned, s + 1)
                wait(act, kvr_done, 2 * s - 2)
                act.activation(z_hi[p][:, :, :], turn_ps[:, :, :], ACT.Copy).then_inc(zhi_ready, 1)

            def g_high(s, p, c):
                if not inside(s, SEQS):
                    return
                act.wait_ge(g_ready, 2 * s + c + 1)
                wait(act, o_done, s - 1)
                act.activation(g_hi[p][:, c, :], g[c][:, :], ACT.Copy).then_inc(ghi_ready, 1)

            def split_high(s, p):
                if not inside(s, SEQS):
                    return
                act.wait_ge(fw_loaded[p], landed(s, p))
                wait(act, fw_stored[p], landed(s - 2, p, 2))
                act.activation(fw_hi[p][:, :], fw[p][:, :], ACT.Copy).then_inc(fwhi_ready, 1)

            def body(i, par):
                exps(i, 0)
                high(i + 1, 1 - par)
                exps(i, 1)
                g_high(i, par, 0)
                split_high(i, par)
                g_high(i, par, 1)

            steps(act, body, -1, *LOOP, SEQS)

        @block.vector
        def _(dve):
            for p in range(2):
                dve.memset(zs_hi[p][0:SHIFTED, 0:1].bitcast(F32), 0.0)
                dve.memset(zs_hi[p][SHIFTED:P, T - 1:T].bitcast(F32), 0.0)
                dve.memset(zs_lo[p][0:SHIFTED, 0:1].bitcast(F32), 0.0)
                dve.memset(zs_lo[p][SHIFTED:P, T - 1:T].bitcast(F32), 0.0)
            for c in range(CC):
                dve.memset(a_sum[c][:, 0:1], 0.0)
                last = dve.memset(b_sum[c][:, 0:1], 0.0)
            last.then_inc(zs_cleared, 1)
            dve.wait_ge(consts_in, 64)
            dve.tensor_scalar(u[:, :], first_c[:, :], 1.0 / T, None, ALU.mult).then_inc(u_ready, 1)
            dve.tensor_scalar(unmix[:, :, :], mix_c[:, :, :], -1.0, 1.0, ALU.mult, ALU.add).then_inc(mixes_ready, 1)
            dve.wait_ge(mixes_ready, 1)
            dve.tensor_tensor(both[:, :, :], mix_c[:, :, :], unmix[:, :, :], ALU.add).then_inc(mixes_ready, 1)
            dve.wait_ge(mixes_ready, 2)
            dve.wait_ge(w_in, 16)
            for which in (K, V, R):
                for part, c, by in ((HERE, 0, mix_c), (SHIFT, 0, unmix), (REST, 1, both)):
                    last = dve.tensor_scalar(w_mixed[:, which, part, :], w_raw[:, which, c, :],
                                             by[:, which, c:c + 1], None, ALU.mult)
            last.then_inc(mixed_ready, 1)
            dve.wait_ge(mixed_ready, 1)
            dve.tensor_copy(w_hi[:, :, :, :], w_mixed[:, :, :, :])
            dve.tensor_copy(wo_hi[:, :, :], w_raw[:, 3, :, :]).then_inc(mixed_ready, 1)
            dve.wait_ge(mixed_ready, 2)
            dve.tensor_tensor(w_lo[:, :, :, :], w_mixed[:, :, :, :], w_hi[:, :, :, :].bitcast(F32), ALU.subtract)
            dve.tensor_tensor(wo_lo[:, :, :], w_raw[:, 3, :, :], wo_hi[:, :, :].bitcast(F32), ALU.subtract)\
                .then_inc(w_ready, 1)
            dve.wait_ge(ew_ready, 1)

            def moments(k, s, p, src):
                for j in range(SUBS):
                    last = dve.bn_stats(stats[k][p][:, j, :], src[:, j, :])
                last.then_inc(stats_ready[k], 1)

            def normalise(k, s, p, out, src):
                dve.wait_ge(rstd_ready[k], s + 1)
                for j in range(SUBS):
                    last = dve.tensor_scalar(out[:, j, :], src[:, j, :], mean[k][p][:, j:j + 1],
                                             rstd[k][p][:, j:j + 1], ALU.subtract, ALU.mult)
                return last

            def moments_x(s, p):
                if inside(s, SEQS):
                    dve.wait_ge(x_loaded[p], landed(s, p))
                    moments(LN_X, s, p, x_in[p])

            def normalise_x(s, p):
                if inside(s, SEQS):
                    wait(dve, turned, s)
                    normalise(LN_X, s, p, xn, x_in[p]).then_inc(xn_ready, 1)

            def low(s, p):
                if inside(s, SEQS):
                    dve.wait_ge(zhi_ready, s + 1)
                    dve.tensor_tensor(z_lo[p][:, :, :], turn_ps[:, :, :], z_hi[p][:, :, :].bitcast(F32),
                                      ALU.subtract).then_inc(zlo_ready, 1)

            def scans(s, c):
                if not inside(s, SEQS):
                    return
                dve.wait_ge(exps_ready, 6 * s + 3 * c + 2)
                dve.tensor_tensor(ekv[c][:, :], ek[c][:, :], v_ps[c][:, :], ALU.mult).then_inc(ekv_ready, 1)
                dve.tensor_tensor(num[c][:, :], eku[c][:, :], v_ps[c][:, :], ALU.mult).then_inc(v_used, 1)
                wait(dve, bd_ready, 2 * s + c - 1)
                dve.tensor_tensor_scan(b_sum[c][:, 1:T + 1], ew[:, c:c + 1].to_broadcast([P, T]), ek[c][:, :],
                                       0.0, ALU.mult, ALU.add)
                dve.wait_ge(ekv_ready, 2 * s + c + 1)
                dve.tensor_tensor_scan(a_sum[c][:, 1:T + 1], ew[:, c:c + 1].to_broadcast([P, T]), ekv[c][:, :],
                                       0.0, ALU.mult, ALU.add).then_inc(scans_ready, 1)

            def gate(s, c):
                if not inside(s, SEQS):
                    return
                dve.wait_ge(exps_ready, 6 * s + 3 * c + 3)
                dve.wait_ge(bd_ready, 2 * s + c + 1)
                dve.scalar_tensor_tensor(out=den[c][:, :], in0=er[c][:, :], scalar=1.0, in1=den[c][:, :],
                                         op0=ALU.add, op1=ALU.mult).then_inc(den_ready, 1)
                dve.wait_ge(den_ready, 2 * s + c + 1)
                dve.reciprocal(den[c][:, :], den[c][:, :]).then_inc(rec_ready, 1)
                dve.wait_ge(rec_ready, 2 * s + c + 1)
                wait(dve, glo_ready, 2 * s + c - 1)
                dve.tensor_tensor(g[c][:, :], num[c][:, :], den[c][:, :], ALU.mult).then_inc(g_ready, 1)

            def moments_o(s, p):
                if inside(s, SEQS):
                    dve.wait_ge(o_done, s + 1)
                    moments(LN_O, s, p, o_ps)

            def normalise_o(s, p):
                if inside(s, SEQS):
                    wait(dve, x1_ready, s)
                    normalise(LN_O, s, p, on, o_ps).then_inc(on_ready, 1)

            def moments_x1(s, p):
                if inside(s, SEQS):
                    dve.wait_ge(x1_ready, s + 1)
                    moments(LN_X1, s, p, x1[p])

            def normalise_x1(s, p):
                if inside(s, SEQS):
                    wait(dve, xf_stored[p], landed(s - 2, p))
                    normalise(LN_X1, s, p, xf[p], x1[p]).then_inc(xf_ready, 1)

            def body(i, par):
                moments_x(i + 1, 1 - par)
                moments_x1(i - 2, par)
                scans(i, 0)
                normalise_x(i + 1, 1 - par)
                normalise_x1(i - 2, par)
                gate(i, 0)
                low(i + 1, 1 - par)
                scans(i, 1)
                moments_o(i - 1, 1 - par)
                gate(i, 1)
                normalise_o(i - 1, 1 - par)

            steps(dve, body, -1, *LOOP, SEQS + 2)

        @block.gpsimd
        def _(pool):
            scale_constants(pool, scale_c, C, consts_done)
            pool.wait_ge(zs_cleared, 1)
            pool.memset(zeros[:, :], 0.0).then_inc(zeros_ready, 1)

            def inverse_std(k, s, p):
                if not inside(s, SEQS):
                    return
                pool.wait_ge(stats_ready[k], s + 1)
                layernorm_scales(pool, scale_c, stats[k][p], sums[k][p], half_diff[k][p], var[k][p], mean[k][p],
                                 rstd[k][p], scales_ordered[k], s, rstd_ready[k])

            def running_sums(s, c):
                if not inside(s, SEQS):
                    return
                pool.wait_ge(scans_ready, 2 * s + c + 1)
                pool.tensor_tensor(num[c][:, :], num[c][:, :], a_sum[c][:, 0:T], ALU.add)
                wait(pool, g_ready, 2 * s + c - 1)
                pool.tensor_tensor(den[c][:, :], b_sum[c][:, 0:T], eku[c][:, :], ALU.add).then_inc(bd_ready, 1)

            def g_low(s, p, c):
                if not inside(s, SEQS):
                    return
                pool.wait_ge(ghi_ready, 2 * s + c + 1)
                pool.tensor_tensor(g_lo[p][:, c, :], g[c][:, :], g_hi[p][:, c, :].bitcast(F32), ALU.subtract)\
                    .then_inc(glo_ready, 1)

            def add_x(s, p):
                if not inside(s, SEQS):
                    return
                pool.wait_ge(on_ready, s + 1)
                pool.wait_ge(res_loaded[p], landed(s, p))
                wait(pool, x1_stored[p], landed(s - 2, p))
                wait(pool, xf_ready, s - 1)
                pool.tensor_tensor(x1[p][:, :, :], on[:, :, :], x_res[p][:, :, :], ALU.add).then_inc(x1_ready, 1)

            def split_low(s, p):
                if not inside(s, SEQS):
                    return
                pool.wait_ge(fwhi_ready, s + 1)
                pool.tensor_tensor(fw_lo[p][:, :], fw[p][:, :], fw_hi[p][:, :].bitcast(F32), ALU.subtract)\
                    .then_inc(fwlo_ready, 1)

            def body(i, par):
                inverse_std(LN_X, i + 1, 1 - par)
                inverse_std(LN_X1, i - 2, par)
                running_sums(i, 0)
                g_low(i, par, 0)
                running_sums(i, 1)
                inverse_std(LN_O, i - 1, 1 - par)
                g_low(i, par, 1)
                add_x(i - 1, 1 - par)
                split_low(i, par)

            steps(pool, body, -1, *LOOP, SEQS + 2)


def swiglu(nc, name, tiles, parts, src, dst, w_hi, w_lo, biases, ident, route=None, expert_of=None):
    C = src.shape[1]
    CC, SUBS = C // P, 4
    T = SUBS * P
    INNER = parts * P
    W13, W2 = 2 * CC * INNER, parts * C
    WSETS = 2 if expert_of is not None else 1
    E = 8

    with ExitStack() as ctx:
        def sb(label, shape, dt=F32):
            return ctx.enter_context(nc.sbuf_tensor(f"{name}_{label}", shape, dt))

        def psum(label, shape):
            return ctx.enter_context(nc.psum_tensor(f"{name}_{label}", shape, F32))

        def sem(label):
            return ctx.enter_context(nc.semaphore(f"{name}_{label}"))

        eye = sb("eye", [P, P])
        w13_hi = [sb(f"w13_hi{p}", [P, 2, CC, INNER], F32R) for p in range(WSETS)]
        w13_lo = [sb(f"w13_lo{p}", [P, 2, CC, INNER], F32R) for p in range(WSETS)]
        w2_hi = [sb(f"w2_hi{p}", [P, parts, C], F32R) for p in range(WSETS)]
        w2_lo = [sb(f"w2_lo{p}", [P, parts, C], F32R) for p in range(WSETS)]
        bias = [sb(f"bias{p}", [P, 2, parts]) for p in range(WSETS)]
        x_in = [sb(f"x_in{p}", [P, SUBS, C]) for p in range(2)]
        z_hi = [sb(f"z_hi{p}", [P, CC, T], F32R) for p in range(2)]
        z_lo = [sb(f"z_lo{p}", [P, CC, T], F32R) for p in range(2)]
        act_h = [sb(f"act_h{p}", [P, T]) for p in range(2)]
        h = [sb(f"h{p}", [P, T]) for p in range(2)]
        h_hi = [sb(f"h_hi{p}", [P, parts, T], F32R) for p in range(2)]
        h_lo = [sb(f"h_lo{p}", [P, parts, T], F32R) for p in range(2)]
        y = [sb(f"y{p}", [P, SUBS, C]) for p in range(2)]
        turn_ps = psum("turn_ps", [P, CC, T])
        h1_ps = [psum(f"h1_ps{p}", [P, T]) for p in range(2)]
        h3_ps = [psum(f"h3_ps{p}", [P, T]) for p in range(2)]
        y_ps = psum("y_ps", [P, SUBS, C])
        if route:
            gw = sb("gw", [P, CC, E])
            gw_hi = sb("gw_hi", [P, CC, E], F32R)
            gw_lo = sb("gw_lo", [P, CC, E], F32R)
            gb = sb("gb", [P, E])
            logits_ps = turn_ps[:, 0, 0:SUBS * E].rearrange("p (j e) -> p j e", e=E)

        eye_in = sem("eye_in")
        w13_loaded = [sem(f"w13_loaded{p}") for p in range(WSETS)]
        w2_loaded = [sem(f"w2_loaded{p}") for p in range(WSETS)]
        x_loaded = [sem(f"x_loaded{p}") for p in range(2)]
        turned = sem("turned")
        zhi_ready = sem("zhi_ready")
        zlo_ready = sem("zlo_ready")
        h13_done = sem("h13_done")
        silu_ready = sem("silu_ready")
        h_ready = sem("h_ready")
        hhi_ready = sem("hhi_ready")
        hlo_ready = sem("hlo_ready")
        y_done = sem("y_done")
        y_read = sem("y_read")
        y_stored = [sem(f"y_stored{p}") for p in range(2)]
        if route:
            gw_in = sem("gw_in")
            gw_ready = sem("gw_ready")
            logits_done = sem("logits_done")
            logits_read = sem("logits_read")
        block = ctx.enter_context(nc.Block())
        LOOP = (4, tiles - 2)

        def words(ap):
            return ap.bitcast(F32)

        def rows(dram, i):
            return dram[bass.ds(i * T, T), :].rearrange("(j p) c -> p j c", p=P)

        @block.sync
        def _(sp):
            sp.dma_start(eye[:, :], ident).then_inc(eye_in, 16)
            if route:
                sp.dma_start(gw[:, :, :], route["w"]).then_inc(gw_in, 16)
                sp.dma_start(gb[:, :], route["b"].to_broadcast([P, E])).then_inc(gw_in, 16)

            def load_w13(p, at):
                for dram, to in ((w_hi, w13_hi[p]), (w_lo, w13_lo[p])):
                    sp.dma_start(words(to[:, :, :, :].rearrange("p a b n -> p (a b n)")),
                                 dram[:, bass.ds(at, W13)]).then_inc(w13_loaded[p], 16)

            def load_w2(p, at):
                for dram, to in ((w_hi, w2_hi[p]), (w_lo, w2_lo[p])):
                    sp.dma_start(words(to[:, :, :].rearrange("p a n -> p (a n)")),
                                 dram[:, bass.ds(at + W13, W2)]).then_inc(w2_loaded[p], 16)

            if expert_of is None:
                load_w13(0, 0)
                load_w2(0, 0)
                sp.dma_start(bias[0][:, :, :], biases).then_inc(w13_loaded[0], 16)

            def body(i, par):
                n = i + 2
                if inside(n, tiles):
                    wait(sp, turned, n - 1)
                    sp.dma_start(x_in[par][:, :, :], rows(src, n)).then_inc(x_loaded[par], 16)
                n = i + 1
                if expert_of is not None and inside(n, tiles):
                    p = 1 - par
                    e = sp.value_load(expert_of[0:1, bass.ds(n, 1)], min_val=0, max_val=E - 1)
                    wait(sp, h13_done, (n - 1) * parts)
                    wait(sp, h_ready, (n - 1) * parts)
                    load_w13(p, e * (W13 + W2))
                    sp.dma_start(bias[p][:, :, :], biases[bass.ds(e, 1), :, :, :].rearrange("a p b c -> p (a b) c"))\
                        .then_inc(w13_loaded[p], 16)
                    wait(sp, y_done, n - 1)
                    load_w2(p, e * (W13 + W2))
                s = i - 1
                if inside(s, tiles):
                    sp.wait_ge(y_read, s + 1)
                    sp.dma_start(rows(dst, s), y[1 - par][:, :, :]).then_inc(y_stored[1 - par], 16)

            steps(sp, body, -2, *LOOP, tiles + 1)
            for p in range(2):
                sp.wait_ge(y_stored[p], 16 * (tiles // 2))

        @block.tensor
        def _(pe):
            pe.wait_ge(eye_in, 16)

            def turn(s, p):
                if not inside(s, tiles):
                    return
                pe.wait_ge(x_loaded[p], landed(s, p))
                wait(pe, zlo_ready, s)
                if route:
                    wait(pe, logits_read, s)
                for c in range(CC):
                    for j in range(SUBS):
                        last = pe.transpose(turn_ps[:, c, j * P:(j + 1) * P],
                                            x_in[p][:, j, c * P:(c + 1) * P], eye[:, :])
                last.then_inc(turned, 1)

            def logits(s, p):
                if not inside(s, tiles):
                    return
                if isinstance(s, int) and s == 0:
                    pe.wait_ge(gw_ready, 2)
                pe.wait_ge(zlo_ready, s + 1)
                for j in range(SUBS):
                    n = 0
                    for c in range(CC):
                        for a, w in ((z_hi, gw_hi), (z_lo, gw_hi), (z_hi, gw_lo)):
                            last = pe.matmul(logits_ps[:, j, :], a[p][:, c, j * P:(j + 1) * P], w[:, c, :],
                                             start=(n == 0), stop=(n == 5))
                            n += 1
                last.then_inc(logits_done, 1)

            def inner(s, p, q):
                if not inside(s, tiles):
                    return
                w = p % WSETS
                if q == 0:
                    pe.wait_ge(zlo_ready, s + 1)
                    if expert_of is not None:
                        pe.wait_ge(w13_loaded[w], landed(s, p, 3))
                    elif isinstance(s, int) and s == 0:
                        pe.wait_ge(w13_loaded[w], 48)
                wait(pe, silu_ready, s * parts + q - 1)
                wait(pe, h_ready, s * parts + q - 1)
                for which, out in ((0, h1_ps[q % 2]), (1, h3_ps[q % 2])):
                    n = 0
                    for c in range(CC):
                        for a, b in ((w13_hi, z_hi), (w13_hi, z_lo), (w13_lo, z_hi)):
                            last = pe.matmul(out[:, :], a[w][:, which, c, q * P:(q + 1) * P], b[p][:, c, :],
                                             start=(n == 0), stop=(n == 5))
                            n += 1
                last.then_inc(h13_done, 1)

            def outer(s, p):
                if not inside(s, tiles):
                    return
                w = p % WSETS
                pe.wait_ge(hlo_ready, (s + 1) * parts)
                wait(pe, y_read, s)
                if expert_of is not None:
                    pe.wait_ge(w2_loaded[w], landed(s, p, 2))
                elif isinstance(s, int) and s == 0:
                    pe.wait_ge(w2_loaded[w], 32)
                for j in range(SUBS):
                    n = 0
                    for q in range(parts):
                        for a, b in ((h_hi, w2_hi), (h_lo, w2_hi), (h_hi, w2_lo)):
                            last = pe.matmul(y_ps[:, j, :], a[p][:, q, j * P:(j + 1) * P], b[w][:, q, :],
                                             start=(n == 0), stop=(n == 3 * parts - 1))
                            n += 1
                last.then_inc(y_done, 1)

            def body(i, par):
                inner(i, par, 0)
                outer(i - 1, 1 - par)
                turn(i + 1, 1 - par)
                for q in range(1, parts):
                    inner(i, par, q)
                if route:
                    logits(i + 1, 1 - par)

            steps(pe, body, -1, *LOOP, tiles + 1)

        @block.scalar
        def _(act):
            act.wait_ge(w13_loaded[0], 48)

            def high(s, p):
                if not inside(s, tiles):
                    return
                act.wait_ge(turned, s + 1)
                wait(act, h13_done, (s - 1) * parts)
                if route:
                    wait(act, logits_done, s - 1)
                act.activation(z_hi[p][:, :, :], turn_ps[:, :, :], ACT.Copy).then_inc(zhi_ready, 1)

            def silu(s, p, q):
                if not inside(s, tiles):
                    return
                w = p % WSETS
                act.wait_ge(h13_done, s * parts + q + 1)
                wait(act, h_ready, s * parts + q - 1)
                act.activation(act_h[q % 2][:, :], h1_ps[q % 2][:, :], ACT.Silu, bias=bias[w][:, 0, q:q + 1])\
                    .then_inc(silu_ready, 1)

            def h_high(s, p, q):
                if not inside(s, tiles):
                    return
                act.wait_ge(h_ready, s * parts + q + 1)
                wait(act, y_done, s - 1)
                act.activation(h_hi[p][:, q, :], h[q % 2][:, :], ACT.Copy).then_inc(hhi_ready, 1)

            def body(i, par):
                silu(i, par, 0)
                high(i + 1, 1 - par)
                for q in range(1, parts):
                    silu(i, par, q)
                    h_high(i, par, q - 1)
                h_high(i, par, parts - 1)

            steps(act, body, -1, *LOOP, tiles)

        @block.vector
        def _(dve):
            if route:
                dve.wait_ge(gw_in, 32)
                dve.tensor_copy(gw_hi[:, :, :], gw[:, :, :]).then_inc(gw_ready, 1)
                dve.wait_ge(gw_ready, 1)
                dve.tensor_tensor(gw_lo[:, :, :], gw[:, :, :], words(gw_hi[:, :, :]), ALU.subtract)\
                    .then_inc(gw_ready, 1)

            def low(s, p):
                if inside(s, tiles):
                    dve.wait_ge(zhi_ready, s + 1)
                    dve.tensor_tensor(z_lo[p][:, :, :], turn_ps[:, :, :], words(z_hi[p][:, :, :]), ALU.subtract)\
                        .then_inc(zlo_ready, 1)

            def read_logits(s, p):
                if inside(s, tiles):
                    dve.wait_ge(logits_done, s + 1)
                    to = route["logits"][:, bass.ds(s * SUBS, SUBS), :]
                    dve.tensor_tensor(to, logits_ps, gb[:, None, :].to_broadcast([P, SUBS, E]), ALU.add)\
                        .then_inc(logits_read, 1)

            def product(s, p, q):
                if not inside(s, tiles):
                    return
                w = p % WSETS
                dve.wait_ge(silu_ready, s * parts + q + 1)
                wait(dve, hlo_ready, s * parts + q - 1)
                dve.scalar_tensor_tensor(out=h[q % 2][:, :], in0=h3_ps[q % 2][:, :], scalar=bias[w][:, 1, q:q + 1],
                                         in1=act_h[q % 2][:, :], op0=ALU.add, op1=ALU.mult).then_inc(h_ready, 1)

            def read_y(s, p):
                if inside(s, tiles):
                    dve.wait_ge(y_done, s + 1)
                    wait(dve, y_stored[p], landed(s - 2, p))
                    dve.tensor_copy(y[p][:, :, :], y_ps[:, :, :]).then_inc(y_read, 1)

            def body(i, par):
                product(i, par, 0)
                read_y(i - 1, 1 - par)
                low(i + 1, 1 - par)
                for q in range(1, parts):
                    product(i, par, q)
                if route:
                    read_logits(i + 1, 1 - par)

            steps(dve, body, -1, *LOOP, tiles + 1)

        @block.gpsimd
        def _(pool):
            def h_low(s, p, q):
                if not inside(s, tiles):
                    return
                pool.wait_ge(hhi_ready, s * parts + q + 1)
                pool.tensor_tensor(h_lo[p][:, q, :], h[q % 2][:, :], words(h_hi[p][:, q, :]), ALU.subtract)\
                    .then_inc(hlo_ready, 1)

            def body(i, par):
                for q in range(parts):
                    h_low(i, par, q)

            steps(pool, body, 0, *LOOP, tiles)


def routing(nc, logits, gates, slot, expert_of, tri, ones, limits, rank_start, SLOT_TILE):
    _, NT, E = logits.shape
    TILES = expert_of.shape[1]
    STEPS = limits.shape[1]

    with ExitStack() as ctx:
        def sb(label, shape, dt=F32):
            return ctx.enter_context(nc.sbuf_tensor(f"r_{label}", shape, dt))

        def sem(label):
            return ctx.enter_context(nc.semaphore(f"r_{label}"))

        tri_s = sb("tri", [P, P])
        ones_s = sb("ones", [P, P])
        limits_s = sb("limits", [P, STEPS])
        start_s = sb("rank_start", [P, E])
        top = sb("top", [P, NT])
        prob = sb("prob", [P, NT, E])
        ge = sb("ge", [P, NT, E])
        rank = sb("rank", [P, NT, E])
        mask = sb("mask", [P, NT, E])
        before = sb("before", [P, E, NT + 1])
        over = sb("over", [P, E, STEPS])
        used = sb("used", [P, E])
        ends = sb("ends", [P, E + 1])
        pos = sb("pos", [P, NT, E])
        chosen = sb("chosen", [P, NT, E])
        picked = sb("picked", [P, NT, E])
        slot_f = sb("slot_f", [P, NT])
        past = sb("past", [1, TILES, E])
        number = sb("number", [1, TILES])
        rank_ps = ctx.enter_context(nc.psum_tensor("r_rank_ps", [P, NT, E], F32))
        total_ps = ctx.enter_context(nc.psum_tensor("r_total_ps", [P, NT, E], F32))

        in_ready = sem("in_ready")
        mask_ready = sem("mask_ready")
        counted = sem("counted")
        shifted_ready = sem("shifted_ready")
        exp_ready = sem("exp_ready")
        chain = sem("chain")
        block = ctx.enter_context(nc.Block())

        @block.sync
        def _(sp):
            sp.dma_start(tri_s[:, :], tri).then_inc(in_ready, 16)
            sp.dma_start(ones_s[:, :], ones).then_inc(in_ready, 16)
            sp.dma_start(limits_s[:, :], limits.to_broadcast([P, STEPS])).then_inc(in_ready, 16)
            sp.dma_start(start_s[:, :], rank_start.to_broadcast([P, E])).then_inc(in_ready, 16)

        @block.scalar
        def _(act):
            act.wait_ge(shifted_ready, 1)
            act.activation(prob[:, :, :], prob[:, :, :], ACT.Exp).then_inc(exp_ready, 1)

        @block.tensor
        def _(pe):
            pe.wait_ge(in_ready, 64)
            pe.wait_ge(mask_ready, 1)
            flat = mask[:, :, :].rearrange("p t e -> p (t e)")
            pe.matmul(rank_ps[:, :, :].rearrange("p t e -> p (t e)"), tri_s[:, :], flat, start=True, stop=True)
            pe.matmul(total_ps[:, :, :].rearrange("p t e -> p (t e)"), ones_s[:, :], flat, start=True, stop=True)\
                .then_inc(counted, 1)

        @block.vector
        def _(dve):
            count = [0]

            def then(ins):
                count[0] += 1
                ins.then_inc(chain, 1)
                dve.wait_ge(chain, count[0])

            def wide(v):
                return v[:, :, None].to_broadcast([P, NT, E])

            dve.wait_ge(in_ready, 64)
            then(dve.tensor_reduce(top[:, :], logits[:, :, :], mybir.AxisListType.X, ALU.max))
            dve.tensor_tensor(prob[:, :, :], logits[:, :, :], wide(top), ALU.subtract).then_inc(shifted_ready, 1)
            dve.wait_ge(exp_ready, 1)
            then(dve.tensor_reduce(top[:, :], prob[:, :, :], mybir.AxisListType.X, ALU.add))
            then(dve.reciprocal(top[:, :], top[:, :]))
            then(dve.tensor_tensor(prob[:, :, :], prob[:, :, :], wide(top), ALU.mult))
            then(dve.tensor_copy(rank[:, :, :], start_s[:, None, :].to_broadcast([P, NT, E])))
            for d in range(1, E):
                then(dve.tensor_tensor(ge[:, :, 0:E - d], prob[:, :, 0:E - d], prob[:, :, d:E], ALU.is_ge))
                then(dve.tensor_tensor(rank[:, :, d:E], rank[:, :, d:E], ge[:, :, 0:E - d], ALU.add))
                then(dve.tensor_tensor(rank[:, :, 0:E - d], rank[:, :, 0:E - d], ge[:, :, 0:E - d], ALU.subtract))
            dve.tensor_scalar(mask[:, :, :], rank[:, :, :], 2.0, None, ALU.is_lt).then_inc(mask_ready, 1)
            dve.wait_ge(mask_ready, 1)
            dve.memset(before[:, :, 0:1], 0.0)
            dve.memset(ends[:, 0:1], 0.0)
            dve.memset(gates["all"][:, :, E:E + 1], 1.0)
            then(dve.tensor_tensor(gates["all"][:, :, 0:E], mask[:, :, :], prob[:, :, :], ALU.mult))
            dve.wait_ge(counted, 1)
            then(dve.tensor_copy(ge[:, :, :], total_ps[:, :, :]))
            for e in range(E):
                last = dve.tensor_tensor_scan(before[:, e, 1:NT + 1], ones_s[:, 0:1].to_broadcast([P, NT]),
                                              ge[:, :, e], 0.0, ALU.mult, ALU.add)
            then(last)
            then(dve.tensor_tensor(over[:, :, :], before[:, :, NT:NT + 1].to_broadcast([P, E, STEPS]),
                                   limits_s[:, None, :].to_broadcast([P, E, STEPS]), ALU.is_gt))
            then(dve.tensor_reduce(used[:, :], over[:, :, :], mybir.AxisListType.X, ALU.add))
            then(dve.tensor_tensor_scan(ends[:, 1:E + 1], ones_s[:, 0:E], used[:, :], 0.0, ALU.mult, ALU.add))
            for t in range(TILES):
                last = dve.tensor_scalar(past[:, t, :], ends[0:1, 1:E + 1], float(t), None, ALU.is_le)
            then(last)
            then(dve.tensor_reduce(number[:, :], past[:, :, :], mybir.AxisListType.X, ALU.add))
            then(dve.tensor_scalar(expert_of[:, :], number[:, :], float(E - 1), None, ALU.min))
            then(dve.tensor_tensor(pos[:, :, :], rank_ps[:, :, :],
                                   before[:, :, 0:NT].rearrange("p e t -> p t e"), ALU.add))
            then(dve.tensor_scalar(used[:, :], ends[:, 0:E], float(SLOT_TILE), None, ALU.mult))
            then(dve.tensor_tensor(pos[:, :, :], pos[:, :, :], used[:, None, :].to_broadcast([P, NT, E]), ALU.add))
            for k in range(2):
                then(dve.tensor_scalar(chosen[:, :, :], rank[:, :, :], float(k), None, ALU.is_equal))
                then(dve.tensor_tensor(picked[:, :, :], chosen[:, :, :], pos[:, :, :], ALU.mult))
                then(dve.tensor_reduce(slot_f[:, :], picked[:, :, :], mybir.AxisListType.X, ALU.add))
                then(dve.tensor_copy(slot[k][:, :], slot_f[:, :]))
                then(dve.tensor_tensor(picked[:, :, :], chosen[:, :, :], prob[:, :, :], ALU.mult))
                then(dve.tensor_reduce(gates[k][:, :], picked[:, :, :], mybir.AxisListType.X, ALU.add))


def dispatch(nc, xf_dram, slot, slots_x):
    C = xf_dram.shape[1]
    SUBS = 4
    T = SUBS * P
    tiles = xf_dram.shape[0] // T
    with ExitStack() as ctx:
        def sem(label):
            return ctx.enter_context(nc.semaphore(f"d_{label}"))

        x_in = [[ctx.enter_context(nc.sbuf_tensor(f"d_x_in{p}{j}", [P, C], F32)) for j in range(SUBS)] for p in range(2)]
        at = [[[ctx.enter_context(nc.sbuf_tensor(f"d_at{p}{j}{k}", [P, 1], mybir.dt.uint32)) for k in range(2)]
               for j in range(SUBS)] for p in range(2)]
        scratch = ctx.enter_context(nc.sbuf_tensor("d_scratch", [P, 2], F32))
        x_loaded = [sem(f"x_loaded{p}") for p in range(2)]
        at_ready = sem("at_ready")
        scratch_ready = sem("scratch_ready")
        held = sem("held")
        sent = [sem(f"sent{p}") for p in range(2)]
        block = ctx.enter_context(nc.Block())
        LOOP = (2, tiles)

        @block.sync
        def _(sp):
            def body(i, par):
                wait(sp, sent[par], landed(i - 2, par, 2 * SUBS))
                for j in range(SUBS):
                    sp.dma_start(x_in[par][j][:, :], xf_dram[bass.ds(i * T + j * P, P), :]).then_inc(x_loaded[par], 16)

            steps(sp, body, 0, *LOOP, tiles)

        @block.vector
        def _(dve):
            def body(i, par):
                wait(dve, sent[par], landed(i - 2, par, 2 * SUBS))
                for j in range(SUBS):
                    for k in range(2):
                        last = dve.tensor_copy(at[par][j][k][:, :], slot[k][:, bass.ds(i * SUBS + j, 1)])
                last.then_inc(at_ready, 1)

            steps(dve, body, 0, *LOOP, tiles)

        @block.gpsimd
        def _(pool):
            pool.memset(scratch[:, :], 0.0).then_inc(scratch_ready, 1)
            pool.wait_ge(scratch_ready, 1)

            def body(i, par):
                hold(pool, scratch, held, i, (x_loaded[par], landed(i, par, SUBS)), (at_ready, i + 1))
                for j in range(SUBS):
                    for k in range(2):
                        pool.indirect_dma_start(out=slots_x[:, :], out_offset=bass.IndirectOffsetOnAxis(ap=at[par][j][k][:, :], axis=0),
                                                in_=x_in[par][j][:, :], in_offset=None).then_inc(sent[par], 16)

            steps(pool, body, 0, *LOOP, tiles)
            for p in range(2):
                pool.wait_ge(sent[p], landed(tiles - 2 + p, p, 2 * SUBS))


def combine(nc, x1_dram, shared, slots_y, slot, gates, out_biases, ident, out):
    C = x1_dram.shape[1]
    SUBS = 4
    T = SUBS * P
    tiles = x1_dram.shape[0] // T
    G = gates["all"].shape[2]
    with ExitStack() as ctx:
        def sb(label, shape, dt=F32):
            return ctx.enter_context(nc.sbuf_tensor(f"c_{label}", shape, dt))

        def sem(label):
            return ctx.enter_context(nc.semaphore(f"c_{label}"))

        eye = sb("eye", [P, P])
        b_out = sb("b_out", [G, C])
        scale_c = sb("scale_c", [P, 4, SUBS])
        scratch = sb("scratch", [P, 2])
        at = [[[sb(f"at{p}{j}{k}", [P, 1], mybir.dt.uint32) for k in range(2)] for j in range(SUBS)] for p in range(2)]
        ye = [[[sb(f"ye{p}{j}{k}", [P, C]) for k in range(2)] for j in range(SUBS)] for p in range(2)]
        ys = [sb(f"ys{p}", [P, SUBS, C]) for p in range(2)]
        x1 = [sb(f"x1{p}", [P, SUBS, C]) for p in range(2)]
        gt = [sb(f"gt{p}", [G, T]) for p in range(2)]
        gate_now = [sb(f"gate_now{p}", [P, 2, SUBS]) for p in range(2)]
        acc = [sb(f"acc{p}", [P, SUBS, C]) for p in range(2)]
        stats = [sb(f"stats{p}", [P, SUBS, 6]) for p in range(2)]
        sums = [sb(f"sums{p}", [P, SUBS, 2]) for p in range(2)]
        half_diff = [sb(f"half_diff{p}", [P, SUBS]) for p in range(2)]
        var = [sb(f"var{p}", [P, SUBS]) for p in range(2)]
        mean = [sb(f"mean{p}", [P, SUBS]) for p in range(2)]
        rstd = [sb(f"rstd{p}", [P, SUBS]) for p in range(2)]
        res = [sb(f"res{p}", [P, SUBS, C]) for p in range(2)]
        gt_ps = [ctx.enter_context(nc.psum_tensor(f"c_gt_ps{p}", [P, T], F32)) for p in range(2)]
        b_ps = [ctx.enter_context(nc.psum_tensor(f"c_b_ps{p}", [P, SUBS, C], F32)) for p in range(2)]

        consts_in = sem("consts_in")
        scale_c_ready = sem("scale_c_ready")
        scratch_ready = sem("scratch_ready")
        held = sem("held")
        at_ready = sem("at_ready")
        gathered = [sem(f"gathered{p}") for p in range(2)]
        loaded = [sem(f"loaded{p}") for p in range(2)]
        gt_turned = sem("gt_turned")
        gt_ready = sem("gt_ready")
        b_done = sem("b_done")
        sum_b = sem("sum_b")
        sum_0 = sem("sum_0")
        sum_1 = sem("sum_1")
        stats_ready = sem("stats_ready")
        scales_ordered = sem("scales_ordered")
        rstd_ready = sem("rstd_ready")
        normed = sem("normed")
        res_ready = sem("res_ready")
        stored = [sem(f"stored{p}") for p in range(2)]
        block = ctx.enter_context(nc.Block())
        LOOP = (4, tiles - 2)

        def rows(dram, i):
            return dram[bass.ds(i * T, T), :].rearrange("(j p) c -> p j c", p=P)

        @block.sync
        def _(sp):
            sp.dma_start(eye[:, :], ident).then_inc(consts_in, 16)
            sp.dma_start(b_out[:, :], out_biases).then_inc(consts_in, 16)

            def body(i, par):
                if inside(i, tiles):
                    wait(sp, res_ready, i - 1)
                    sp.dma_start(ys[par][:, :, :], rows(shared, i)).then_inc(loaded[par], 16)
                    sp.dma_start(x1[par][:, :, :], rows(x1_dram, i)).then_inc(loaded[par], 16)
                s = i - 1
                if inside(s, tiles):
                    sp.wait_ge(res_ready, s + 1)
                    sp.dma_start(rows(out, s), res[1 - par][:, :, :]).then_inc(stored[1 - par], 16)

            steps(sp, body, 0, *LOOP, tiles + 1)
            for p in range(2):
                sp.wait_ge(stored[p], 16 * (tiles // 2))

        @block.tensor
        def _(pe):
            pe.wait_ge(consts_in, 32)

            def turn(s, p):
                if not inside(s, tiles):
                    return
                pe.wait_ge(at_ready, s + 1)
                wait(pe, gt_ready, s - 1)
                for j in range(SUBS):
                    last = pe.transpose(gt_ps[p][0:G, j * P:(j + 1) * P], gates["now"][p][:, j, :], eye[:, :])
                last.then_inc(gt_turned, 1)

            def bias(s, p):
                if not inside(s, tiles):
                    return
                pe.wait_ge(gt_ready, s + 1)
                wait(pe, sum_b, s - 1)
                for j in range(SUBS):
                    last = pe.matmul(b_ps[p][:, j, :], gt[p][:, j * P:(j + 1) * P], b_out[:, :],
                                     start=True, stop=True)
                last.then_inc(b_done, 1)

            def body(i, par):
                turn(i + 1, 1 - par)
                bias(i, par)

            steps(pe, body, -1, *LOOP, tiles)

        @block.scalar
        def _(act):
            def body(i, par):
                act.wait_ge(gt_turned, i + 1)
                wait(act, b_done, i - 1)
                act.activation(gt[par][:, :], gt_ps[par][0:G, :], ACT.Copy).then_inc(gt_ready, 1)

            steps(act, body, 0, *LOOP, tiles)

        @block.vector
        def _(dve):
            def fetch(s, p):
                if not inside(s, tiles):
                    return
                wait(dve, gathered[p], landed(s - 2, p, 2 * SUBS))
                wait(dve, gt_turned, s - 1)
                for j in range(SUBS):
                    for k in range(2):
                        dve.tensor_copy(at[p][j][k][:, :], slot[k][:, bass.ds(s * SUBS + j, 1)])
                for k in range(2):
                    dve.tensor_copy(gate_now[p][:, k, :], gates[k][:, bass.ds(s * SUBS, SUBS)])
                dve.tensor_copy(gates["now"][p][:, :, :], gates["all"][:, bass.ds(s * SUBS, SUBS), :])\
                    .then_inc(at_ready, 1)

            def add(s, p):
                if not inside(s, tiles):
                    return
                dve.wait_ge(b_done, s + 1)
                dve.wait_ge(loaded[p], landed(s, p, 2))
                dve.tensor_tensor(acc[p][:, :, :], b_ps[p][:, :, :], ys[p][:, :, :], ALU.add).then_inc(sum_b, 1)
                dve.wait_ge(sum_b, s + 1)
                dve.wait_ge(gathered[p], landed(s, p, 2 * SUBS))
                dve.wait_ge(at_ready, s + 1)
                for k, done in ((0, sum_0), (1, sum_1)):
                    for j in range(SUBS):
                        last = dve.scalar_tensor_tensor(out=acc[p][:, j, :], in0=ye[p][j][k][:, :],
                                                        scalar=gate_now[p][:, k, j:j + 1], in1=acc[p][:, j, :],
                                                        op0=ALU.mult, op1=ALU.add)
                    last.then_inc(done, 1)
                    dve.wait_ge(done, s + 1)
                for j in range(SUBS):
                    last = dve.bn_stats(stats[p][:, j, :], acc[p][:, j, :])
                last.then_inc(stats_ready, 1)

            def finish(s, p):
                if not inside(s, tiles):
                    return
                dve.wait_ge(rstd_ready, s + 1)
                for j in range(SUBS):
                    last = dve.tensor_scalar(acc[p][:, j, :], acc[p][:, j, :], mean[p][:, j:j + 1],
                                             rstd[p][:, j:j + 1], ALU.subtract, ALU.mult)
                last.then_inc(normed, 1)
                dve.wait_ge(normed, s + 1)
                wait(dve, stored[p], landed(s - 2, p))
                dve.tensor_tensor(res[p][:, :, :], acc[p][:, :, :], x1[p][:, :, :], ALU.add).then_inc(res_ready, 1)

            def body(i, par):
                fetch(i + 1, 1 - par)
                add(i, par)
                finish(i - 1, 1 - par)

            steps(dve, body, -1, *LOOP, tiles + 1)

        @block.gpsimd
        def _(pool):
            scale_constants(pool, scale_c, C, scale_c_ready)
            pool.memset(scratch[:, :], 0.0).then_inc(scratch_ready, 1)
            pool.wait_ge(scratch_ready, 1)

            def gather(s, p):
                if not inside(s, tiles):
                    return
                hold(pool, scratch, held, s, (at_ready, s + 1), (sum_1, s - 1))
                for j in range(SUBS):
                    for k in range(2):
                        pool.indirect_dma_start(out=ye[p][j][k][:, :], out_offset=None, in_=slots_y[:, :],
                                                in_offset=bass.IndirectOffsetOnAxis(ap=at[p][j][k][:, :], axis=0))\
                            .then_inc(gathered[p], 16)

            def inverse_std(s, p):
                if not inside(s, tiles):
                    return
                pool.wait_ge(stats_ready, s + 1)
                layernorm_scales(pool, scale_c, stats[p], sums[p], half_diff[p], var[p], mean[p], rstd[p],
                                 scales_ordered, s, rstd_ready)

            def body(i, par):
                gather(i + 1, 1 - par)
                inverse_std(i, par)

            steps(pool, body, -1, *LOOP, tiles)


SLOT_TILE = 512


def sandwich(nc, x, attn_w, mix, decay, first, ident, tri, ones, limits, rank_start, ffn_w, expert_biases,
             shared_biases, gate_w, gate_b, out_biases, out):
    B, T, C = x.shape
    TOKENS = B * T
    E = gate_w.shape[2]
    EXPERTS_W = 6 * C * (C // P) // 2
    MAX_TILES = (2 * TOKENS + E * (SLOT_TILE - 1)) // SLOT_TILE
    TILES = MAX_TILES + MAX_TILES % 2
    COLS = ffn_w.shape[1]

    x1_dram = nc.dram_tensor("x1_dram", (B, T, C), F32, kind="Internal").ap()
    xf_dram = nc.dram_tensor("xf_dram", (B, T, C), F32, kind="Internal").ap()
    ffn_hi = nc.dram_tensor("ffn_hi", (P, COLS), F32, kind="Internal").ap()
    ffn_lo = nc.dram_tensor("ffn_lo", (P, COLS), F32, kind="Internal").ap()
    slots_x = nc.dram_tensor("slots_x", (TILES * SLOT_TILE, C), F32, kind="Internal").ap()
    slots_y = nc.dram_tensor("slots_y", (TILES * SLOT_TILE, C), F32, kind="Internal").ap()
    shared_y = nc.dram_tensor("shared_y", (TOKENS, C), F32, kind="Internal").ap()
    tokens = "b t c -> (b t) c"

    time_mix(nc, x, attn_w, mix, decay, first, ident, ffn_w, x1_dram, xf_dram, ffn_hi, ffn_lo, slots_x)
    with ExitStack() as ctx:
        def sb(label, shape, dt=F32):
            return ctx.enter_context(nc.sbuf_tensor(label, shape, dt))

        NT = TOKENS // P
        logits = sb("logits", [P, NT, E])
        gates = {0: sb("gate0", [P, NT]), 1: sb("gate1", [P, NT]), "all": sb("gates_all", [P, NT, E + 1]),
                 "now": [sb(f"gates_now{p}", [P, 4, E + 1]) for p in range(2)]}
        slot = [sb(f"slot{k}", [P, NT], mybir.dt.uint32) for k in range(2)]
        expert_of = sb("expert_of", [1, TILES], mybir.dt.int32)
        shared_at = E * EXPERTS_W
        swiglu(nc, "sh", TOKENS // 512, 4, xf_dram.rearrange(tokens), shared_y, ffn_hi[:, shared_at:COLS],
               ffn_lo[:, shared_at:COLS], shared_biases, ident, route={"w": gate_w, "b": gate_b, "logits": logits})
        routing(nc, logits, gates, slot, expert_of, tri, ones, limits, rank_start, SLOT_TILE)
        dispatch(nc, xf_dram.rearrange(tokens), slot, slots_x)
        swiglu(nc, "ex", TILES, 2, slots_x, slots_y, ffn_hi[:, 0:shared_at], ffn_lo[:, 0:shared_at],
               expert_biases, ident, expert_of=expert_of)
        combine(nc, x1_dram.rearrange(tokens), shared_y, slots_y, slot, gates, out_biases, ident,
                out.rearrange(tokens))


def kernel(**inputs):
    import numpy as _np
    import concourse.bacc as _bacc
    from concourse import mybir as _mybir
    from concourse.bass_utils import run_bass_kernel_spmd as _run

    def get(name):
        return _np.asarray(inputs["L0_" + name])

    def chunked(w):
        n, m = w.shape
        return w.T.reshape(m // 128, 128, n).transpose(1, 0, 2)

    def columns(v):
        return v.reshape(-1, 128).T

    w1, w3, w2 = get("ffn_w1"), get("ffn_w3"), get("ffn_w2")
    ffn = [chunked(w[e]).reshape(128, -1) for e in range(w1.shape[0]) for w in (w1, w3, w2)]
    ffn += [chunked(get(n)).reshape(128, -1) for n in ("ffn_ws1", "ffn_ws3", "ffn_ws2")]
    tokens, slot_tile = get("attn_x").shape[0] * get("attn_x").shape[1], 512
    arrays = {
        "x": get("attn_x"),
        "attn_w": _np.stack([chunked(get(n)) for n in ("attn_Wk", "attn_Wv", "attn_Wr", "attn_Wo")], 1),
        "mix": _np.stack([columns(get(n)) for n in ("attn_mix_k", "attn_mix_v", "attn_mix_r")], 1),
        "decay": columns(get("attn_spatial_decay")),
        "first": columns(get("attn_spatial_first")),
        "ident": _np.eye(128, dtype=_np.float32),
        "tri": _np.triu(_np.ones((128, 128), _np.float32), 1),
        "ones": _np.ones((128, 128), _np.float32),
        "limits": _np.arange(0, tokens, slot_tile, dtype=_np.float32)[None],
        "rank_start": _np.arange(7, -1, -1, dtype=_np.float32)[None],
        "ffn_w": _np.concatenate(ffn, 1),
        "expert_biases": _np.stack([_np.stack([columns(b[e]) for b in (get("ffn_b1"), get("ffn_b3"))], 1)
                                    for e in range(w1.shape[0])], 0),
        "shared_biases": _np.stack([columns(get("ffn_bs1")), columns(get("ffn_bs3"))], 1),
        "gate_w": chunked(get("ffn_gate_w")),
        "gate_b": get("ffn_gate_b")[None],
        "out_biases": _np.concatenate([get("ffn_b2"), get("ffn_bs2")[None]], 0),
    }
    nc = _bacc.Bacc("TRN2", target_bir_lowering=False, num_devices=1)
    args = {}
    for name in arrays:
        a = arrays[name] = _np.ascontiguousarray(arrays[name])
        args[name] = nc.dram_tensor(name, a.shape, _mybir.dt.from_np(a.dtype), kind="ExternalInput").ap()
    args["out"] = nc.dram_tensor("out", arrays["x"].shape, _mybir.dt.float32, kind="ExternalOutput").ap()
    sandwich(nc, **args)
    r = _run(nc, [arrays], core_ids=[0])
    return r.results[0]["out"]
```

```python
from contextlib import ExitStack

import concourse.bass as bass
from concourse import mybir

F32 = mybir.dt.float32
F32R = mybir.dt.float32r
ALU = mybir.AluOpType
ACT = mybir.ActivationFunctionType

P = 128
EPS = 1e-5
NOBODY = 1e9


def inside(s, n):
    return not isinstance(s, int) or 0 <= s < n


def wait(eng, sem, count):
    if not isinstance(count, int) or count > 0:
        eng.wait_ge(sem, count)


def hold(pool, scratch, held, step, *waits):
    for sem, count in waits:
        wait(pool, sem, count)
    wait(pool, held, step)
    pool.tensor_tensor(scratch[:, 0:1], scratch[:, 1:2], scratch[:, 1:2], ALU.add).then_inc(held, 1)


SCALES = 4
HALF, PER_ROW, EPSILON, MINUS_HALF = range(4)


def scale_constants(pool, consts, row, ready):
    for k, v in ((HALF, 0.5), (PER_ROW, 1.0 / row), (EPSILON, EPS), (MINUS_HALF, -0.5)):
        pool.memset(consts[:, k, :], v).then_inc(ready, 1)
    pool.wait_ge(ready, 4)


def layernorm_scales(pool, consts, stats, sums, half_diff, var, mean, rstd, ordered, s, ready, negative=False):
    pool.tensor_tensor(sums[:, :, :], stats[:, :, 1:3], stats[:, :, 4:6], ALU.add)
    pool.tensor_tensor(half_diff[:, :], stats[:, :, 1], stats[:, :, 4], ALU.subtract).then_inc(ordered, 1)
    pool.wait_ge(ordered, s * SCALES + 1)
    pool.tensor_tensor(mean[:, :], sums[:, :, 0], consts[:, MINUS_HALF if negative else HALF, :], ALU.mult)
    pool.tensor_tensor(half_diff[:, :], half_diff[:, :], consts[:, HALF, :], ALU.mult)
    pool.tensor_tensor(var[:, :], sums[:, :, 1], consts[:, PER_ROW, :], ALU.mult).then_inc(ordered, 1)
    pool.wait_ge(ordered, s * SCALES + 2)
    pool.tensor_tensor(half_diff[:, :], half_diff[:, :], half_diff[:, :], ALU.mult)
    pool.tensor_tensor(var[:, :], var[:, :], consts[:, EPSILON, :], ALU.add).then_inc(ordered, 1)
    pool.wait_ge(ordered, s * SCALES + 3)
    pool.tensor_tensor(var[:, :], var[:, :], half_diff[:, :], ALU.add).then_inc(ordered, 1)
    pool.wait_ge(ordered, s * SCALES + 4)
    pool.tensor_tensor(rstd[:, :], var[:, :], consts[:, MINUS_HALF, :], ALU.pow).then_inc(ready, 1)


def landed(s, parity, dmas=1):
    return (s - parity + 2) * (8 * dmas)


def steps(eng, body, first, loop_first, loop_end, end):
    for i in range(first, loop_first):
        body(i, i % 2)
    with eng.Fori(loop_first // 2, loop_end // 2) as pair:
        body(pair * 2, 0)
        body(pair * 2 + 1, 1)
    for i in range(loop_end, end):
        body(i, i % 2)


def split_weights(nc, attn_w, mix, ffn_w, gate_w, w_hi, w_lo, wo_hi, wo_lo, w13, w2, gw):
    K, V, R = range(3)
    HERE, SHIFT, REST = range(3)
    CC, C = attn_w.shape[2:]
    W13 = w13["hi"].shape[1] * w13["hi"].shape[2] * w13["hi"].shape[3]

    with ExitStack() as ctx:
        def sb(name, shape, dt=F32):
            return ctx.enter_context(nc.sbuf_tensor(f"w_{name}", shape, dt))

        def sem(name):
            return ctx.enter_context(nc.semaphore(f"w_{name}"))

        w_raw = sb("raw", [P, 4, CC, C])
        w_mixed = sb("mixed", [P, 3, 3, C])
        ffn_raw = sb("ffn_raw", [P, ffn_w.shape[1]])
        gw_raw = sb("gw_raw", list(gate_w.shape))
        mix_c = sb("mix_c", [P, 3, CC])
        unmix = sb("unmix", [P, 3, CC])
        both = sb("both", [P, 3, CC])
        mix_in = sem("mix_in")
        w_in = sem("w_in")
        ffn_in = sem("ffn_in")
        mixes_ready = sem("mixes_ready")
        mixed_ready = sem("mixed_ready")
        hi_ready = sem("hi_ready")
        ffn_hi_ready = sem("ffn_hi_ready")
        block = ctx.enter_context(nc.Block())

        def words(ap):
            return ap.bitcast(F32)

        def flat(w):
            return w.rearrange("p a b n -> p (a b n)") if len(w.shape) == 4 else w.rearrange("p a n -> p (a n)")

        @block.sync
        def _(sp):
            sp.dma_start(mix_c[:, :, :], mix).then_inc(mix_in, 16)
            sp.dma_start(w_raw[:, :, :, :], attn_w).then_inc(w_in, 16)
            sp.dma_start(ffn_raw[:, :], ffn_w).then_inc(ffn_in, 16)
            sp.dma_start(gw_raw[:, :, :], gate_w).then_inc(ffn_in, 16)

        @block.scalar
        def _(act):
            act.wait_ge(ffn_in, 32)
            act.activation(flat(w13["hi"][:, :, :, :]), ffn_raw[:, 0:W13], ACT.Copy).then_inc(ffn_hi_ready, 1)
            act.activation(flat(w2["hi"][:, :, :]), ffn_raw[:, W13:], ACT.Copy).then_inc(ffn_hi_ready, 1)
            act.activation(gw["hi"][:, :, :], gw_raw[:, :, :], ACT.Copy).then_inc(ffn_hi_ready, 1)
            act.wait_ge(mixed_ready, 1)
            act.activation(w_hi[:, :, :, :], w_mixed[:, :, :, :], ACT.Copy).then_inc(hi_ready, 1)
            act.activation(wo_hi[:, :, :], w_raw[:, 3, :, :], ACT.Copy).then_inc(hi_ready, 1)

        @block.gpsimd
        def _(pool):
            pool.wait_ge(ffn_hi_ready, 3)
            pool.tensor_tensor(flat(w2["lo"][:, :, :]), ffn_raw[:, W13:], words(flat(w2["hi"][:, :, :])), ALU.subtract)
            pool.tensor_tensor(gw["lo"][:, :, :], gw_raw[:, :, :], words(gw["hi"][:, :, :]), ALU.subtract)

        @block.vector
        def _(dve):
            dve.wait_ge(mix_in, 16)
            dve.tensor_scalar(unmix[:, :, :], mix_c[:, :, :], -1.0, 1.0, ALU.mult, ALU.add).then_inc(mixes_ready, 1)
            dve.wait_ge(mixes_ready, 1)
            dve.tensor_tensor(both[:, :, :], mix_c[:, :, :], unmix[:, :, :], ALU.add).then_inc(mixes_ready, 1)
            dve.wait_ge(mixes_ready, 2)
            dve.wait_ge(w_in, 16)
            for which in (K, V, R):
                for part, c, by in ((HERE, 0, mix_c), (SHIFT, 0, unmix), (REST, 1, both)):
                    last = dve.tensor_scalar(w_mixed[:, which, part, :], w_raw[:, which, c, :],
                                             by[:, which, c:c + 1], None, ALU.mult)
            last.then_inc(mixed_ready, 1)
            dve.wait_ge(ffn_hi_ready, 1)
            dve.tensor_tensor(flat(w13["lo"][:, :, :, :]), ffn_raw[:, 0:W13], words(flat(w13["hi"][:, :, :, :])),
                              ALU.subtract)
            dve.wait_ge(hi_ready, 2)
            dve.tensor_tensor(w_lo[:, :, :, :], w_mixed[:, :, :, :], words(w_hi[:, :, :, :]), ALU.subtract)
            dve.tensor_tensor(wo_lo[:, :, :], w_raw[:, 3, :, :], words(wo_hi[:, :, :]), ALU.subtract)


def first_pass(nc, x, attn_w, mix, decay, first, ident, ffn_w, shared_biases, gate_w, logits, x1_dram, xf_dram,
               shared_y, slots_x):
    SEQS, T, C = x.shape
    SUBS = T // P
    ROW = slots_x.shape[1]
    CC = C // P
    SHIFTED = C // 4
    Q = shared_biases.shape[2]
    E = gate_w.shape[2]
    assert CC == 2 and SUBS == 4 and 2 * SHIFTED == P and T == 512 and SEQS % 2 == 0 and Q == 4
    K, V, R = range(3)
    HERE, SHIFT, REST = range(3)

    with ExitStack() as ctx:
        def sb(name, shape, dt=F32):
            return ctx.enter_context(nc.sbuf_tensor(f"f_{name}", shape, dt))

        def psum(name, shape):
            return ctx.enter_context(nc.psum_tensor(f"f_{name}", shape, F32))

        def sem(name):
            return ctx.enter_context(nc.semaphore(f"f_{name}"))

        w_hi = sb("w_hi", [P, 3, 3, C], F32R)
        w_lo = sb("w_lo", [P, 3, 3, C], F32R)
        wo_hi = sb("wo_hi", [P, CC, C], F32R)
        wo_lo = sb("wo_lo", [P, CC, C], F32R)
        w13 = {h: sb(f"w13_{h}", [P, 2, CC, Q * P], F32R) for h in ("hi", "lo")}
        w2 = {h: sb(f"w2_{h}", [P, Q, C], F32R) for h in ("hi", "lo")}
        gw = {h: sb(f"gw_{h}", [P, CC, E], F32R) for h in ("hi", "lo")}
        split_weights(nc, attn_w, mix, ffn_w, gate_w, w_hi, w_lo, wo_hi, wo_lo, w13, w2, gw)

        eye = sb("eye", [P, P])
        bias = sb("bias", [P, 2, Q])
        decay_c = sb("decay_c", [P, CC])
        first_c = sb("first_c", [P, CC])
        ew = sb("ew", [P, CC])
        u = sb("u", [P, CC])
        scale_c = sb("scale_c", [P, 4, SUBS])

        x_in = [sb(f"x_in{p}", [P, SUBS, C]) for p in range(2)]
        x_res = [sb(f"x_res{p}", [P, SUBS, C]) for p in range(2)]
        xn = sb("xn", [P, SUBS, C])
        z_hi = sb("z_hi", [P, CC, T], F32R)
        z_lo = sb("z_lo", [P, CC, T], F32R)
        zs_hi = sb("zs_hi", [P, T], F32R)
        zs_lo = sb("zs_lo", [P, T], F32R)
        ek = [sb(f"ek{c}", [P, T]) for c in range(CC)]
        eku = [sb(f"eku{c}", [P, T]) for c in range(CC)]
        er = [sb(f"er{c}", [P, T]) for c in range(CC)]
        ekv = [sb(f"ekv{c}", [P, T]) for c in range(CC)]
        a_sum = [sb(f"a_sum{c}", [P, T + 1]) for c in range(CC)]
        b_sum = [sb(f"b_sum{c}", [P, T + 1]) for c in range(CC)]
        num = [sb(f"num{c}", [P, T]) for c in range(CC)]
        den = [sb(f"den{c}", [P, T]) for c in range(CC)]
        g = [sb(f"g{c}", [P, T]) for c in range(CC)]
        g_hi = sb("g_hi", [P, CC, T], F32R)
        g_lo = sb("g_lo", [P, CC, T], F32R)
        on = sb("on", [P, SUBS, C])
        x1 = [sb(f"x1{p}", [P, SUBS, C]) for p in range(2)]
        xf = sb("xf", [P, SUBS, C])
        clear_rows = slots_x.shape[0] // SEQS // P
        zeros = sb("zeros", [P, 1, ROW])
        f_hi = [sb(f"f_hi{p}", [P, CC, T], F32R) for p in range(2)]
        f_lo = [sb(f"f_lo{p}", [P, CC, T], F32R) for p in range(2)]
        act_h = [sb(f"act_h{p}", [P, T]) for p in range(2)]
        h = [sb(f"h{p}", [P, T]) for p in range(2)]
        h_hi = sb("h_hi", [P, Q, T], F32R)
        h_lo = sb("h_lo", [P, Q, T], F32R)
        y = [sb(f"y{half}", [P, SUBS // 2, C]) for half in range(2)]
        LN_X, LN_O, LN_X1 = range(3)
        stats = [[sb(f"stats{k}{p}", [P, SUBS, 6]) for p in range(2)] for k in range(3)]
        sums = [[sb(f"sums{k}{p}", [P, SUBS, 2]) for p in range(2)] for k in range(3)]
        half_diff = [[sb(f"half_diff{k}{p}", [P, SUBS]) for p in range(2)] for k in range(3)]
        var = [[sb(f"var{k}{p}", [P, SUBS]) for p in range(2)] for k in range(3)]
        mean = [[sb(f"mean{k}{p}", [P, SUBS]) for p in range(2)] for k in range(3)]
        rstd = [[sb(f"rstd{k}{p}", [P, SUBS]) for p in range(2)] for k in range(3)]
        offset = [sb(f"offset{p}", [P, SUBS]) for p in range(2)]

        k_ps = psum("k_ps", [P, T])
        v_ps = psum("v_ps", [P, T])
        r_ps = psum("r_ps", [P, T])
        h1_ps = psum("h1_ps", [P, T])
        h3_ps = psum("h3_ps", [P, T])
        turn_ps = psum("turn_ps", [P, CC, T])
        o_ps = turn_ps[:, :, :].rearrange("p a (b n) -> p (a b) n", n=C)
        shared_ps = psum("shared_ps", [P, T])
        y_ps = shared_ps[:, :].rearrange("p (j n) -> p j n", n=C)
        logits_ps = shared_ps[:, 0:SUBS * E].rearrange("p (j e) -> p j e", e=E)

        consts_in = sem("consts_in")
        consts_done = sem("consts_done")
        zs_cleared = sem("zs_cleared")
        u_ready = sem("u_ready")
        ew_ready = sem("ew_ready")
        x_loaded = [sem(f"x_loaded{p}") for p in range(2)]
        res_loaded = [sem(f"res_loaded{p}") for p in range(2)]
        stats_ready = [sem(f"stats_ready{k}") for k in range(3)]
        scales_ordered = [sem(f"scales_ordered{k}") for k in range(3)]
        rstd_ready = [sem(f"rstd_ready{k}") for k in range(3)]
        offset_ready = sem("offset_ready")
        xn_ready = sem("xn_ready")
        turned = sem("turned")
        zhi_ready = sem("zhi_ready")
        zlo_ready = sem("zlo_ready")
        zs_ready = sem("zs_ready")
        kvr_done = sem("kvr_done")
        exps_ready = sem("exps_ready")
        ekv_ready = sem("ekv_ready")
        v_used = sem("v_used")
        scans_ready = sem("scans_ready")
        bd_ready = sem("bd_ready")
        den_ready = sem("den_ready")
        rec_ready = sem("rec_ready")
        g_ready = sem("g_ready")
        ghi_ready = sem("ghi_ready")
        glo_ready = sem("glo_ready")
        o_done = sem("o_done")
        on_ready = sem("on_ready")
        x1_ready = sem("x1_ready")
        xf_ready = sem("xf_ready")
        x1_stored = [sem(f"x1_stored{p}") for p in range(2)]
        xf_stored = sem("xf_stored")
        f_turned = sem("f_turned")
        fhi_ready = sem("fhi_ready")
        flo_ready = sem("flo_ready")
        inner_done = sem("inner_done")
        silu_ready = sem("silu_ready")
        h_ready = sem("h_ready")
        hhi_ready = sem("hhi_ready")
        hlo_ready = sem("hlo_ready")
        y_done = sem("y_done")
        y_read = sem("y_read")
        y_stored = [sem(f"y_stored{half}") for half in range(2)]
        logits_done = sem("logits_done")
        logits_read = sem("logits_read")
        zeros_ready = sem("zeros_ready")
        cleared = sem("cleared")
        block = ctx.enter_context(nc.Block())

        LOOP = (6, SEQS - 2)
        END = SEQS + 4

        def by_tiles(rows):
            return rows.rearrange("(j p) c -> p j c", p=P)

        @block.sync
        def _(sp):
            sp.dma_start(eye[:, :], ident).then_inc(consts_in, 16)
            sp.dma_start(decay_c[:, :], decay).then_inc(consts_in, 16)
            sp.dma_start(first_c[:, :], first).then_inc(consts_in, 16)
            sp.dma_start(bias[:, :, :], shared_biases).then_inc(consts_in, 16)

            def body(i, par):
                s = i - 4
                if inside(s, SEQS):
                    for half in range(2):
                        sp.wait_ge(y_read, 2 * s + half + 1)
                        at = (s * 2 + half) * (T // 2)
                        sp.dma_start(by_tiles(shared_y[bass.ds(at, T // 2), :]), y[half][:, :, :])\
                            .then_inc(y_stored[half], 16)
                n = i + 2
                if inside(n, SEQS):
                    wait(sp, xn_ready, n - 1)
                    sp.dma_start(x_in[par][:, :, :], by_tiles(x[n, :, :])).then_inc(x_loaded[par], 16)
                if inside(i, SEQS):
                    wait(sp, x1_ready, i - 1)
                    sp.dma_start(x_res[par][:, :, :], by_tiles(x[i, :, :])).then_inc(res_loaded[par], 16)
                    if isinstance(i, int) and i == 0:
                        sp.wait_ge(zeros_ready, 2)
                    sp.dma_start(slots_x[bass.ds(i * (clear_rows * P), clear_rows * P), :]
                                 .rearrange("(r p) c -> p r c", p=P),
                                 zeros[:, :, :].to_broadcast([P, clear_rows, ROW])).then_inc(cleared, 16)
                s = i - 2
                if inside(s, SEQS):
                    sp.wait_ge(xf_ready, s + 1)
                    sp.dma_start(by_tiles(xf_dram[s, :, :]), xf[:, :, :]).then_inc(xf_stored, 16)
                s = i - 1
                if inside(s, SEQS):
                    sp.wait_ge(x1_ready, s + 1)
                    sp.dma_start(by_tiles(x1_dram[s, :, :]), x1[1 - par][:, :, :]).then_inc(x1_stored[1 - par], 16)
                s = i + 1
                if inside(s, SEQS):
                    for ready, z, zs in ((zhi_ready, z_hi[:, 0, :].bitcast(F32), zs_hi[:, :].bitcast(F32)),
                                         (zlo_ready, z_lo[:, 0, :].bitcast(F32), zs_lo[:, :].bitcast(F32))):
                        sp.wait_ge(ready, s + 1)
                        sp.dma_start(zs[0:SHIFTED, 1:T], z[0:SHIFTED, 0:T - 1]).then_inc(zs_ready, 16)
                        sp.dma_start(zs[SHIFTED:P, 0:T - 1], z[SHIFTED:P, 1:T]).then_inc(zs_ready, 16)

            steps(sp, body, -2, *LOOP, END)
            sp.wait_ge(cleared, 16 * SEQS)
            sp.wait_ge(xf_stored, 16 * SEQS)
            for p in range(2):
                sp.wait_ge(x1_stored[p], 16 * (SEQS // 2))
                sp.wait_ge(y_stored[p], 16 * SEQS)

        @block.tensor
        def _(pe):
            pe.wait_ge(consts_in, 64)

            def turn(s):
                if not inside(s, SEQS):
                    return
                pe.wait_ge(xn_ready, s + 1)
                wait(pe, on_ready, min(s - 1, SEQS) if isinstance(s, int) else s - 1)
                for c in range(CC):
                    for j in range(SUBS):
                        last = pe.transpose(turn_ps[:, c, j * P:(j + 1) * P], xn[:, j, c * P:(c + 1) * P], eye[:, :])
                last.then_inc(turned, 1)

            def kvr(s, c):
                if not inside(s, SEQS):
                    return
                if c == 0:
                    pe.wait_ge(zhi_ready, s + 1)
                    pe.wait_ge(zlo_ready, s + 1)
                    pe.wait_ge(zs_ready, 64 * (s + 1))
                wait(pe, exps_ready, 6 * s + 3 * c)
                wait(pe, v_used, 2 * s + c)
                for which, out in ((K, k_ps), (V, v_ps), (R, r_ps)):
                    n = 0
                    for part, hi, lo in ((HERE, z_hi[:, 0, :], z_lo[:, 0, :]),
                                         (REST, z_hi[:, 1, :], z_lo[:, 1, :]),
                                         (SHIFT, zs_hi[:, :], zs_lo[:, :])):
                        for w, z in ((w_hi, hi), (w_hi, lo), (w_lo, hi)):
                            last = pe.matmul(out[:, :], w[:, which, part, c * P:(c + 1) * P], z,
                                             start=(n == 0), stop=(n == 8))
                            n += 1
                last.then_inc(kvr_done, 1)

            def project(s):
                if not inside(s, SEQS):
                    return
                pe.wait_ge(glo_ready, 2 * s + 2)
                wait(pe, zlo_ready, min(s + 2, SEQS) if isinstance(s, int) else s + 2)
                for j in range(SUBS):
                    n = 0
                    for c in range(CC):
                        for a, w in ((g_hi, wo_hi), (g_lo, wo_hi), (g_hi, wo_lo)):
                            last = pe.matmul(o_ps[:, j, :], a[:, c, j * P:(j + 1) * P], w[:, c, :],
                                             start=(n == 0), stop=(n == 5))
                            n += 1
                last.then_inc(o_done, 1)

            def turn_xf(s, c):
                if not inside(s, SEQS):
                    return
                if c == 0:
                    pe.wait_ge(xf_ready, s + 1)
                    wait(pe, logits_read, s)
                    if not isinstance(s, int) or s > 0:
                        pe.wait_ge(flo_ready, 2 * s)
                else:
                    pe.wait_ge(flo_ready, 2 * s + 1)
                for j in range(SUBS):
                    last = pe.transpose(shared_ps[:, j * P:(j + 1) * P], xf[:, j, c * P:(c + 1) * P], eye[:, :])
                last.then_inc(f_turned, 1)

            def route(s, p):
                if not inside(s, SEQS):
                    return
                pe.wait_ge(flo_ready, 2 * s + 2)
                wait(pe, y_read, 2 * s)
                for j in range(SUBS):
                    n = 0
                    for c in range(CC):
                        for a, w in ((f_hi, gw["hi"]), (f_lo, gw["hi"]), (f_hi, gw["lo"])):
                            last = pe.matmul(logits_ps[:, j, :], a[p][:, c, j * P:(j + 1) * P], w[:, c, :],
                                             start=(n == 0), stop=(n == 5))
                            n += 1
                last.then_inc(logits_done, 1)

            def inner(s, p, q):
                if not inside(s, SEQS):
                    return
                if q == 0:
                    pe.wait_ge(flo_ready, 2 * s + 2)
                wait(pe, silu_ready, s * Q + q)
                wait(pe, h_ready, s * Q + q)
                for which, out in ((0, h1_ps), (1, h3_ps)):
                    n = 0
                    for c in range(CC):
                        for a, b in ((w13["hi"], f_hi), (w13["hi"], f_lo), (w13["lo"], f_hi)):
                            last = pe.matmul(out[:, :], a[:, which, c, q * P:(q + 1) * P], b[p][:, c, :],
                                             start=(n == 0), stop=(n == 5))
                            n += 1
                last.then_inc(inner_done, 1)

            def outer(s, half):
                if not inside(s, SEQS):
                    return
                if half == 0:
                    pe.wait_ge(hlo_ready, (s + 1) * Q)
                    pe.wait_ge(flo_ready, min(2 * s + 4, 2 * SEQS) if isinstance(s, int) else 2 * s + 4)
                else:
                    pe.wait_ge(y_read, 2 * s + 1)
                for j in range(SUBS // 2):
                    n = 0
                    at = (half * (SUBS // 2) + j) * P
                    for q in range(Q):
                        for a, b in ((h_hi, w2["hi"]), (h_lo, w2["hi"]), (h_hi, w2["lo"])):
                            last = pe.matmul(y_ps[:, j, :], a[:, q, at:at + P], b[:, q, :],
                                             start=(n == 0), stop=(n == 3 * Q - 1))
                            n += 1
                last.then_inc(y_done, 1)

            def body(i, par):
                kvr(i, 0)
                project(i - 1)
                outer(i - 4, 0)
                kvr(i, 1)
                inner(i - 3, 1 - par, 0)
                outer(i - 4, 1)
                inner(i - 3, 1 - par, 1)
                turn(i + 1)
                route(i - 3, 1 - par)
                inner(i - 3, 1 - par, 2)
                turn_xf(i - 2, 0)
                inner(i - 3, 1 - par, 3)
                turn_xf(i - 2, 1)

            steps(pe, body, -1, *LOOP, END)

        @block.scalar
        def _(act):
            act.wait_ge(consts_in, 64)
            act.activation(ew[:, :], decay_c[:, :], ACT.Exp, scale=1.0 / T).then_inc(ew_ready, 1)
            act.wait_ge(u_ready, 1)

            def exps(s, c):
                if not inside(s, SEQS):
                    return
                act.wait_ge(kvr_done, 2 * s + c + 1)
                wait(act, den_ready, 2 * s + c - 1)
                act.activation(ek[c][:, :], k_ps[:, :], ACT.Exp).then_inc(exps_ready, 1)
                act.activation(eku[c][:, :], k_ps[:, :], ACT.Exp, bias=u[:, c:c + 1]).then_inc(exps_ready, 1)
                act.activation(er[c][:, :], r_ps[:, :], ACT.Exp, scale=-1.0).then_inc(exps_ready, 1)

            def high(s):
                if not inside(s, SEQS):
                    return
                act.wait_ge(turned, s + 1)
                wait(act, kvr_done, 2 * s)
                if not isinstance(s, int) or s > 0:
                    act.wait_ge(zs_ready, 64 * s)
                act.activation(z_hi[:, :, :], turn_ps[:, :, :], ACT.Copy).then_inc(zhi_ready, 1)

            def g_high(s, c):
                if not inside(s, SEQS):
                    return
                act.wait_ge(g_ready, 2 * s + c + 1)
                wait(act, o_done, s)
                act.activation(g_hi[:, c, :], g[c][:, :], ACT.Copy).then_inc(ghi_ready, 1)

            def normalise_x1(s, p):
                if not inside(s, SEQS):
                    return
                act.wait_ge(offset_ready, s + 1)
                if not isinstance(s, int) or s > 0:
                    act.wait_ge(xf_stored, 16 * s)
                    act.wait_ge(f_turned, 2 * s)
                for j in range(SUBS):
                    last = act.activation(xf[:, j, :], x1[p][:, j, :], ACT.Identity, bias=offset[p][:, j:j + 1],
                                          scale=rstd[LN_X1][p][:, j:j + 1])
                last.then_inc(xf_ready, 1)

            def f_high(s, p, c):
                if not inside(s, SEQS):
                    return
                act.wait_ge(f_turned, 2 * s + c + 1)
                wait(act, inner_done, (s - 1) * Q)
                wait(act, logits_done, s - 1)
                act.activation(f_hi[p][:, c, :], shared_ps[:, :], ACT.Copy).then_inc(fhi_ready, 1)

            def silu(s, q):
                if not inside(s, SEQS):
                    return
                act.wait_ge(inner_done, s * Q + q + 1)
                wait(act, h_ready, s * Q + q - 1)
                act.activation(act_h[q % 2][:, :], h1_ps[:, :], ACT.Silu, bias=bias[:, 0, q:q + 1])\
                    .then_inc(silu_ready, 1)

            def h_high(s, q):
                if not inside(s, SEQS):
                    return
                act.wait_ge(h_ready, s * Q + q + 1)
                wait(act, y_done, 2 * s)
                act.activation(h_hi[:, q, :], h[q % 2][:, :], ACT.Copy).then_inc(hhi_ready, 1)

            def read_y(s, half):
                if not inside(s, SEQS):
                    return
                act.wait_ge(y_done, 2 * s + half + 1)
                if not isinstance(s, int) or s > 0:
                    act.wait_ge(y_stored[half], 16 * s)
                act.activation(y[half][:, :, :], y_ps, ACT.Copy).then_inc(y_read, 1)

            def body(i, par):
                h_high(i - 4, 3)
                f_high(i - 3, 1 - par, 1)
                exps(i, 0)
                read_y(i - 4, 0)
                normalise_x1(i - 2, par)
                g_high(i, 0)
                exps(i, 1)
                silu(i - 3, 0)
                read_y(i - 4, 1)
                h_high(i - 3, 0)
                silu(i - 3, 1)
                high(i + 1)
                h_high(i - 3, 1)
                silu(i - 3, 2)
                g_high(i, 1)
                f_high(i - 2, par, 0)
                h_high(i - 3, 2)
                silu(i - 3, 3)

            steps(act, body, -1, *LOOP, END)

        @block.vector
        def _(dve):
            dve.memset(zs_hi[0:SHIFTED, 0:1].bitcast(F32), 0.0)
            dve.memset(zs_hi[SHIFTED:P, T - 1:T].bitcast(F32), 0.0)
            dve.memset(zs_lo[0:SHIFTED, 0:1].bitcast(F32), 0.0)
            dve.memset(zs_lo[SHIFTED:P, T - 1:T].bitcast(F32), 0.0)
            for c in range(CC):
                dve.memset(a_sum[c][:, 0:1], 0.0)
                last = dve.memset(b_sum[c][:, 0:1], 0.0)
            last.then_inc(zs_cleared, 1)
            dve.wait_ge(consts_in, 64)
            dve.tensor_scalar(u[:, :], first_c[:, :], 1.0 / T, None, ALU.mult).then_inc(u_ready, 1)
            dve.wait_ge(ew_ready, 1)

            def moments(k, s, p, src):
                for j in range(SUBS):
                    last = dve.bn_stats(stats[k][p][:, j, :], src[:, j, :])
                last.then_inc(stats_ready[k], 1)

            def normalise(k, s, p, out, src):
                dve.wait_ge(rstd_ready[k], s + 1)
                for j in range(SUBS):
                    last = dve.tensor_scalar(out[:, j, :], src[:, j, :], mean[k][p][:, j:j + 1],
                                             rstd[k][p][:, j:j + 1], ALU.subtract, ALU.mult)
                return last

            def moments_x(s, p):
                if inside(s, SEQS):
                    dve.wait_ge(x_loaded[p], landed(s, p))
                    moments(LN_X, s, p, x_in[p])

            def normalise_x(s, p):
                if inside(s, SEQS):
                    wait(dve, turned, s)
                    normalise(LN_X, s, p, xn, x_in[p]).then_inc(xn_ready, 1)

            def low(s):
                if inside(s, SEQS):
                    dve.wait_ge(zhi_ready, s + 1)
                    dve.tensor_tensor(z_lo[:, :, :], turn_ps[:, :, :], z_hi[:, :, :].bitcast(F32),
                                      ALU.subtract).then_inc(zlo_ready, 1)

            def scans(s, c):
                if not inside(s, SEQS):
                    return
                dve.wait_ge(exps_ready, 6 * s + 3 * c + 2)
                dve.tensor_tensor(ekv[c][:, :], ek[c][:, :], v_ps[:, :], ALU.mult).then_inc(ekv_ready, 1)
                dve.tensor_tensor(num[c][:, :], eku[c][:, :], v_ps[:, :], ALU.mult).then_inc(v_used, 1)
                wait(dve, bd_ready, 2 * s + c - 1)
                dve.tensor_tensor_scan(b_sum[c][:, 1:T + 1], ew[:, c:c + 1].to_broadcast([P, T]), ek[c][:, :],
                                       0.0, ALU.mult, ALU.add)
                dve.wait_ge(ekv_ready, 2 * s + c + 1)
                dve.tensor_tensor_scan(a_sum[c][:, 1:T + 1], ew[:, c:c + 1].to_broadcast([P, T]), ekv[c][:, :],
                                       0.0, ALU.mult, ALU.add).then_inc(scans_ready, 1)

            def gate(s, c):
                if not inside(s, SEQS):
                    return
                dve.wait_ge(exps_ready, 6 * s + 3 * c + 3)
                dve.wait_ge(bd_ready, 2 * s + c + 1)
                dve.scalar_tensor_tensor(out=den[c][:, :], in0=er[c][:, :], scalar=1.0, in1=den[c][:, :],
                                         op0=ALU.add, op1=ALU.mult).then_inc(den_ready, 1)
                dve.wait_ge(den_ready, 2 * s + c + 1)
                dve.reciprocal(den[c][:, :], den[c][:, :]).then_inc(rec_ready, 1)
                dve.wait_ge(rec_ready, 2 * s + c + 1)
                wait(dve, glo_ready, 2 * s + c - 1)
                dve.tensor_tensor(g[c][:, :], num[c][:, :], den[c][:, :], ALU.mult).then_inc(g_ready, 1)

            def moments_o(s, p):
                if inside(s, SEQS):
                    dve.wait_ge(o_done, s + 1)
                    moments(LN_O, s, p, o_ps)

            def normalise_o(s, p):
                if inside(s, SEQS):
                    wait(dve, x1_ready, s)
                    normalise(LN_O, s, p, on, o_ps).then_inc(on_ready, 1)

            def moments_x1(s, p):
                if inside(s, SEQS):
                    dve.wait_ge(x1_ready, s + 1)
                    moments(LN_X1, s, p, x1[p])

            def f_low(s, p, c):
                if inside(s, SEQS):
                    dve.wait_ge(fhi_ready, 2 * s + c + 1)
                    dve.tensor_tensor(f_lo[p][:, c, :], shared_ps[:, :], f_hi[p][:, c, :].bitcast(F32),
                                      ALU.subtract).then_inc(flo_ready, 1)

            def product(s, q):
                if not inside(s, SEQS):
                    return
                dve.wait_ge(silu_ready, s * Q + q + 1)
                wait(dve, hlo_ready, s * Q + q - 1)
                dve.scalar_tensor_tensor(out=h[q % 2][:, :], in0=h3_ps[:, :], scalar=bias[:, 1, q:q + 1],
                                         in1=act_h[q % 2][:, :], op0=ALU.add, op1=ALU.mult).then_inc(h_ready, 1)

            def read_logits(s):
                if inside(s, SEQS):
                    dve.wait_ge(logits_done, s + 1)
                    dve.tensor_copy(logits[:, bass.ds(s * SUBS, SUBS), :], logits_ps).then_inc(logits_read, 1)

            def body(i, par):
                product(i - 4, 3)
                f_low(i - 3, 1 - par, 1)
                moments_x(i + 1, 1 - par)
                moments_x1(i - 2, par)
                scans(i, 0)
                moments_o(i - 1, 1 - par)
                gate(i, 0)
                normalise_o(i - 1, 1 - par)
                scans(i, 1)
                product(i - 3, 0)
                normalise_x(i + 1, 1 - par)
                product(i - 3, 1)
                read_logits(i - 3)
                gate(i, 1)
                product(i - 3, 2)
                low(i + 1)
                f_low(i - 2, par, 0)

            steps(dve, body, -1, *LOOP, END)

        @block.gpsimd
        def _(pool):
            scale_constants(pool, scale_c, C, consts_done)
            pool.wait_ge(zs_cleared, 1)
            pool.memset(zeros[:, :, 0:C], 0.0).then_inc(zeros_ready, 1)
            pool.memset(zeros[:, :, C:ROW], NOBODY).then_inc(zeros_ready, 1)

            def inverse_std(k, s, p):
                if not inside(s, SEQS):
                    return
                pool.wait_ge(stats_ready[k], s + 1)
                if k == LN_X1:
                    wait(pool, xf_ready, s - 1)
                layernorm_scales(pool, scale_c, stats[k][p], sums[k][p], half_diff[k][p], var[k][p], mean[k][p],
                                 rstd[k][p], scales_ordered[k], s, rstd_ready[k], negative=(k == LN_X1))
                if k == LN_X1:
                    pool.wait_ge(rstd_ready[k], s + 1)
                    pool.tensor_tensor(offset[p][:, :], mean[k][p][:, :], rstd[k][p][:, :], ALU.mult)\
                        .then_inc(offset_ready, 1)

            def running_sums(s, c):
                if not inside(s, SEQS):
                    return
                pool.wait_ge(scans_ready, 2 * s + c + 1)
                pool.tensor_tensor(num[c][:, :], num[c][:, :], a_sum[c][:, 0:T], ALU.add)
                wait(pool, g_ready, 2 * s + c - 1)
                pool.tensor_tensor(den[c][:, :], b_sum[c][:, 0:T], eku[c][:, :], ALU.add).then_inc(bd_ready, 1)

            def g_low(s, c):
                if not inside(s, SEQS):
                    return
                pool.wait_ge(ghi_ready, 2 * s + c + 1)
                pool.tensor_tensor(g_lo[:, c, :], g[c][:, :], g_hi[:, c, :].bitcast(F32), ALU.subtract)\
                    .then_inc(glo_ready, 1)

            def add_x(s, p):
                if not inside(s, SEQS):
                    return
                pool.wait_ge(on_ready, s + 1)
                pool.wait_ge(res_loaded[p], landed(s, p))
                wait(pool, x1_stored[p], landed(s - 2, p))
                wait(pool, xf_ready, s - 1)
                pool.tensor_tensor(x1[p][:, :, :], on[:, :, :], x_res[p][:, :, :], ALU.add).then_inc(x1_ready, 1)

            def h_low(s, q):
                if not inside(s, SEQS):
                    return
                pool.wait_ge(hhi_ready, s * Q + q + 1)
                pool.tensor_tensor(h_lo[:, q, :], h[q % 2][:, :], h_hi[:, q, :].bitcast(F32), ALU.subtract)\
                    .then_inc(hlo_ready, 1)

            def body(i, par):
                h_low(i - 4, 3)
                inverse_std(LN_X, i + 1, 1 - par)
                inverse_std(LN_X1, i - 2, par)
                running_sums(i, 0)
                inverse_std(LN_O, i - 1, 1 - par)
                g_low(i, 0)
                running_sums(i, 1)
                add_x(i - 1, 1 - par)
                h_low(i - 3, 0)
                h_low(i - 3, 1)
                g_low(i, 1)
                h_low(i - 3, 2)

            steps(pool, body, -1, *LOOP, END)


def swiglu(nc, name, tiles, parts, src, dst, weights, biases, ident, route=None, expert_of=None):
    C = dst.shape[1]
    ROW = src.shape[1]
    CC, SUBS = C // P, 4
    T = SUBS * P
    INNER = parts * P
    W13, W2 = 2 * CC * INNER, parts * C
    WSETS = 2 if expert_of is not None else 1
    E = 8

    with ExitStack() as ctx:
        def sb(label, shape, dt=F32):
            return ctx.enter_context(nc.sbuf_tensor(f"{name}_{label}", shape, dt))

        def psum(label, shape):
            return ctx.enter_context(nc.psum_tensor(f"{name}_{label}", shape, F32))

        def sem(label):
            return ctx.enter_context(nc.semaphore(f"{name}_{label}"))

        eye = sb("eye", [P, P])
        w_raw = [sb(f"w_raw{p}", [P, W13 + W2]) for p in range(WSETS)]
        w13_hi = [sb(f"w13_hi{p}", [P, 2, CC, INNER], F32R) for p in range(WSETS)]
        w13_lo = [sb(f"w13_lo{p}", [P, 2, CC, INNER], F32R) for p in range(WSETS)]
        w2_hi = [sb(f"w2_hi{p}", [P, parts, C], F32R) for p in range(WSETS)]
        w2_lo = [sb(f"w2_lo{p}", [P, parts, C], F32R) for p in range(WSETS)]
        bias = [sb(f"bias{p}", [P, 2, parts]) for p in range(WSETS)]
        x_in = [sb(f"x_in{p}", [P, SUBS, ROW]) for p in range(2)]
        z_hi = [sb(f"z_hi{p}", [P, CC, T], F32R) for p in range(2)]
        z_lo = [sb(f"z_lo{p}", [P, CC, T], F32R) for p in range(2)]
        act_h = [sb(f"act_h{p}", [P, T]) for p in range(2)]
        h = [sb(f"h{p}", [P, T]) for p in range(2)]
        h_hi = [sb(f"h_hi{p}", [P, parts, T], F32R) for p in range(2)]
        h_lo = [sb(f"h_lo{p}", [P, parts, T], F32R) for p in range(2)]
        y = [sb(f"y{p}", [P, SUBS, C]) for p in range(2)]
        if expert_of is not None:
            row_next = [sb(f"row_next{p}", [P, SUBS], mybir.dt.uint32) for p in range(2)]
            row_at = [[sb(f"row_at{p}{j}", [P, 1], mybir.dt.uint32) for j in range(SUBS)] for p in range(2)]
            scratch = sb("scratch", [P, 2])
        turn_ps = psum("turn_ps", [P, CC, T])
        h1_ps = [psum(f"h1_ps{p}", [P, T]) for p in range(2)]
        h3_ps = [psum(f"h3_ps{p}", [P, T]) for p in range(2)]
        y_ps = psum("y_ps", [P, SUBS, C])
        if route:
            gw = sb("gw", [P, CC, E])
            gw_hi = sb("gw_hi", [P, CC, E], F32R)
            gw_lo = sb("gw_lo", [P, CC, E], F32R)
            gb = sb("gb", [P, E])
            logits_ps = turn_ps[:, 0, 0:SUBS * E].rearrange("p (j e) -> p j e", e=E)

        eye_in = sem("eye_in")
        w_loaded = [sem(f"w_loaded{p}") for p in range(WSETS)]
        bias_loaded = [sem(f"bias_loaded{p}") for p in range(WSETS)]
        w13_high = sem("w13_high")
        w13_split = sem("w13_split")
        w2_high = sem("w2_high")
        w2_split = sem("w2_split")
        x_loaded = [sem(f"x_loaded{p}") for p in range(2)]
        turned = sem("turned")
        zhi_ready = sem("zhi_ready")
        zlo_ready = sem("zlo_ready")
        h13_done = sem("h13_done")
        silu_ready = sem("silu_ready")
        h_ready = sem("h_ready")
        hhi_ready = sem("hhi_ready")
        hlo_ready = sem("hlo_ready")
        y_done = sem("y_done")
        y_read = sem("y_read")
        y_stored = [sem(f"y_stored{p}") for p in range(2)]
        Y_DMAS = 1 if expert_of is None else SUBS
        rows_read = sem("rows_read")
        rows_kept = sem("rows_kept")
        scratch_ready = sem("scratch_ready")
        held = sem("held")
        if route:
            gw_in = sem("gw_in")
            gw_ready = sem("gw_ready")
            logits_done = sem("logits_done")
            logits_read = sem("logits_read")
        block = ctx.enter_context(nc.Block())
        LOOP = (4, tiles - 2)

        def words(ap):
            return ap.bitcast(F32)

        def rows(dram, i):
            return dram[bass.ds(i * T, T), :].rearrange("(j p) c -> p j c", p=P)

        @block.sync
        def _(sp):
            sp.dma_start(eye[:, :], ident).then_inc(eye_in, 16)
            if route:
                sp.dma_start(gw[:, :, :], route["w"]).then_inc(gw_in, 16)
                sp.dma_start(gb[:, :], route["b"].to_broadcast([P, E])).then_inc(gw_in, 16)

            if expert_of is None:
                sp.dma_start(w_raw[0][:, :], weights).then_inc(w_loaded[0], 16)
                sp.dma_start(bias[0][:, :, :], biases).then_inc(bias_loaded[0], 16)

            def expert(n):
                return sp.value_load(expert_of[0:1, bass.ds(n, 1)], min_val=0, max_val=E - 1)

            def body(i, par):
                n = i + 2
                if inside(n, tiles):
                    wait(sp, turned, n - 1)
                    if expert_of is not None:
                        wait(sp, rows_read, n - 1)
                    sp.dma_start(x_in[par][:, :, :], rows(src, n)).then_inc(x_loaded[par], 16)
                if expert_of is not None and inside(n, tiles):
                    e = expert(n)
                    wait(sp, w2_split, n - 1)
                    sp.dma_start(w_raw[par][:, :], weights[:, bass.ds(e * (W13 + W2), W13 + W2)])\
                        .then_inc(w_loaded[par], 16)
                n = i + 1
                if expert_of is not None and inside(n, tiles):
                    p = 1 - par
                    e = expert(n)
                    wait(sp, h_ready, (n - 1) * parts)
                    sp.dma_start(bias[p][:, :, :], biases[bass.ds(e, 1), :, :, :]
                                 .rearrange("a p b c -> p (a b) c")).then_inc(bias_loaded[p], 16)
                s = i - 1
                if expert_of is None and inside(s, tiles):
                    sp.wait_ge(y_read, s + 1)
                    sp.dma_start(rows(dst, s), y[1 - par][:, :, :]).then_inc(y_stored[1 - par], 16)

            steps(sp, body, -2, *LOOP, tiles + 1)
            for p in range(2):
                sp.wait_ge(y_stored[p], 16 * Y_DMAS * (tiles // 2))

        @block.tensor
        def _(pe):
            pe.wait_ge(eye_in, 16)

            def turn(s, p):
                if not inside(s, tiles):
                    return
                pe.wait_ge(x_loaded[p], landed(s, p))
                wait(pe, zlo_ready, s)
                if route:
                    wait(pe, logits_read, s)
                for c in range(CC):
                    for j in range(SUBS):
                        last = pe.transpose(turn_ps[:, c, j * P:(j + 1) * P],
                                            x_in[p][:, j, c * P:(c + 1) * P], eye[:, :])
                last.then_inc(turned, 1)

            def logits(s, p):
                if not inside(s, tiles):
                    return
                if isinstance(s, int) and s == 0:
                    pe.wait_ge(gw_ready, 2)
                pe.wait_ge(zlo_ready, s + 1)
                for j in range(SUBS):
                    n = 0
                    for c in range(CC):
                        for a, w in ((z_hi, gw_hi), (z_lo, gw_hi), (z_hi, gw_lo)):
                            last = pe.matmul(logits_ps[:, j, :], a[p][:, c, j * P:(j + 1) * P], w[:, c, :],
                                             start=(n == 0), stop=(n == 5))
                            n += 1
                last.then_inc(logits_done, 1)

            def inner(s, p, q):
                if not inside(s, tiles):
                    return
                w = p % WSETS
                if q == 0:
                    pe.wait_ge(zlo_ready, s + 1)
                    if expert_of is not None:
                        pe.wait_ge(w13_split, s + 1)
                    elif isinstance(s, int) and s == 0:
                        pe.wait_ge(w13_split, 1)
                wait(pe, silu_ready, s * parts + q - 1)
                wait(pe, h_ready, s * parts + q - 1)
                for which, out in ((0, h1_ps[q % 2]), (1, h3_ps[q % 2])):
                    n = 0
                    for c in range(CC):
                        for a, b in ((w13_hi, z_hi), (w13_hi, z_lo), (w13_lo, z_hi)):
                            last = pe.matmul(out[:, :], a[w][:, which, c, q * P:(q + 1) * P], b[p][:, c, :],
                                             start=(n == 0), stop=(n == 5))
                            n += 1
                last.then_inc(h13_done, 1)

            def outer(s, p):
                if not inside(s, tiles):
                    return
                w = p % WSETS
                pe.wait_ge(hlo_ready, (s + 1) * parts)
                wait(pe, y_read, s)
                if expert_of is not None:
                    pe.wait_ge(w2_split, s + 1)
                elif isinstance(s, int) and s == 0:
                    pe.wait_ge(w2_split, 1)
                for j in range(SUBS):
                    n = 0
                    for q in range(parts):
                        for a, b in ((h_hi, w2_hi), (h_lo, w2_hi), (h_hi, w2_lo)):
                            last = pe.matmul(y_ps[:, j, :], a[p][:, q, j * P:(j + 1) * P], b[w][:, q, :],
                                             start=(n == 0), stop=(n == 3 * parts - 1))
                            n += 1
                last.then_inc(y_done, 1)

            def body(i, par):
                inner(i, par, 0)
                turn(i + 1, 1 - par)
                outer(i - 1, 1 - par)
                for q in range(1, parts):
                    inner(i, par, q)
                if route:
                    logits(i + 1, 1 - par)

            steps(pe, body, -1, *LOOP, tiles + 1)

        def flat(w):
            return w.rearrange("p a b n -> p (a b n)") if len(w.shape) == 4 else w.rearrange("p a n -> p (a n)")

        @block.scalar
        def _(act):
            def high_w13(s, p):
                if not inside(s, tiles) or (expert_of is None and not (isinstance(s, int) and s == 0)):
                    return
                w = p % WSETS
                act.wait_ge(w_loaded[w], landed(s, p))
                wait(act, h13_done, (s - 1) * parts)
                act.activation(flat(w13_hi[w][:, :, :, :]), w_raw[w][:, 0:W13], ACT.Copy).then_inc(w13_high, 1)

            def high_w2(s, p):
                if not inside(s, tiles) or (expert_of is None and not (isinstance(s, int) and s == 0)):
                    return
                w = p % WSETS
                wait(act, y_done, s - 1)
                act.activation(flat(w2_hi[w][:, :, :]), w_raw[w][:, W13:W13 + W2], ACT.Copy).then_inc(w2_high, 1)

            def high(s, p):
                if not inside(s, tiles):
                    return
                act.wait_ge(turned, s + 1)
                wait(act, h13_done, (s - 1) * parts)
                if route:
                    wait(act, logits_done, s - 1)
                act.activation(z_hi[p][:, :, :], turn_ps[:, :, :], ACT.Copy).then_inc(zhi_ready, 1)

            def silu(s, p, q):
                if not inside(s, tiles):
                    return
                w = p % WSETS
                act.wait_ge(h13_done, s * parts + q + 1)
                if expert_of is not None:
                    act.wait_ge(bias_loaded[w], landed(s, p))
                elif isinstance(s, int) and s == 0:
                    act.wait_ge(bias_loaded[w], 16)
                wait(act, h_ready, s * parts + q - 1)
                act.activation(act_h[q % 2][:, :], h1_ps[q % 2][:, :], ACT.Silu, bias=bias[w][:, 0, q:q + 1])\
                    .then_inc(silu_ready, 1)

            def h_high(s, p, q):
                if not inside(s, tiles):
                    return
                act.wait_ge(h_ready, s * parts + q + 1)
                wait(act, y_done, s - 1)
                act.activation(h_hi[p][:, q, :], h[q % 2][:, :], ACT.Copy).then_inc(hhi_ready, 1)

            def body(i, par):
                high_w13(i + 1, 1 - par)
                silu(i, par, 0)
                high(i + 1, 1 - par)
                for q in range(1, parts):
                    h_high(i, par, q - 1)
                    if q == 1:
                        high_w2(i + 1, 1 - par)
                    silu(i, par, q)
                h_high(i, par, parts - 1)

            steps(act, body, -1, *LOOP, tiles)

        @block.vector
        def _(dve):
            if route:
                dve.wait_ge(gw_in, 32)
                dve.tensor_copy(gw_hi[:, :, :], gw[:, :, :]).then_inc(gw_ready, 1)
                dve.wait_ge(gw_ready, 1)
                dve.tensor_tensor(gw_lo[:, :, :], gw[:, :, :], words(gw_hi[:, :, :]), ALU.subtract)\
                    .then_inc(gw_ready, 1)

            def low(s, p):
                if inside(s, tiles):
                    dve.wait_ge(zhi_ready, s + 1)
                    dve.tensor_tensor(z_lo[p][:, :, :], turn_ps[:, :, :], words(z_hi[p][:, :, :]), ALU.subtract)\
                        .then_inc(zlo_ready, 1)

            def low_w13(s, p):
                if not inside(s, tiles) or (expert_of is None and not (isinstance(s, int) and s == 0)):
                    return
                w = p % WSETS
                dve.wait_ge(w13_high, s + 1)
                dve.tensor_tensor(flat(w13_lo[w][:, :, :, :]), w_raw[w][:, 0:W13],
                                  words(flat(w13_hi[w][:, :, :, :])), ALU.subtract).then_inc(w13_split, 1)

            def low_w2(s, p):
                if not inside(s, tiles) or (expert_of is None and not (isinstance(s, int) and s == 0)):
                    return
                w = p % WSETS
                dve.wait_ge(w2_high, s + 1)
                dve.tensor_tensor(flat(w2_lo[w][:, :, :]), w_raw[w][:, W13:W13 + W2],
                                  words(flat(w2_hi[w][:, :, :])), ALU.subtract).then_inc(w2_split, 1)

            def read_logits(s, p):
                if inside(s, tiles):
                    dve.wait_ge(logits_done, s + 1)
                    to = route["logits"][:, bass.ds(s * SUBS, SUBS), :]
                    dve.tensor_tensor(to, logits_ps, gb[:, None, :].to_broadcast([P, SUBS, E]), ALU.add)\
                        .then_inc(logits_read, 1)

            def product(s, p, q):
                if not inside(s, tiles):
                    return
                w = p % WSETS
                dve.wait_ge(silu_ready, s * parts + q + 1)
                wait(dve, hlo_ready, s * parts + q - 1)
                dve.scalar_tensor_tensor(out=h[q % 2][:, :], in0=h3_ps[q % 2][:, :], scalar=bias[w][:, 1, q:q + 1],
                                         in1=act_h[q % 2][:, :], op0=ALU.add, op1=ALU.mult).then_inc(h_ready, 1)

            def read_y(s, p):
                if inside(s, tiles):
                    dve.wait_ge(y_done, s + 1)
                    wait(dve, y_stored[p], landed(s - 2, p, Y_DMAS))
                    dve.tensor_copy(y[p][:, :, :], y_ps[:, :, :]).then_inc(y_read, 1)

            def read_rows(s, p):
                if expert_of is not None and inside(s, tiles):
                    dve.wait_ge(x_loaded[p], landed(s, p))
                    wait(dve, rows_kept, s - 1)
                    dve.tensor_copy(row_next[p][:, :], x_in[p][:, :, C]).then_inc(rows_read, 1)

            def keep_rows(s, p):
                if expert_of is not None and inside(s, tiles):
                    dve.wait_ge(rows_read, s + 1)
                    wait(dve, y_stored[p], landed(s - 2, p, Y_DMAS))
                    for j in range(SUBS):
                        last = dve.tensor_copy(row_at[p][j][:, :], row_next[p][:, j:j + 1])
                    last.then_inc(rows_kept, 1)

            def low_w13(s, p):
                if not inside(s, tiles) or (expert_of is None and not (isinstance(s, int) and s == 0)):
                    return
                w = p % WSETS
                dve.wait_ge(w13_high, s + 1)
                dve.tensor_tensor(flat(w13_lo[w][:, :, :, :]), w_raw[w][:, 0:W13],
                                  words(flat(w13_hi[w][:, :, :, :])), ALU.subtract).then_inc(w13_split, 1)

            def low_w2(s, p):
                if not inside(s, tiles) or (expert_of is None and not (isinstance(s, int) and s == 0)):
                    return
                w = p % WSETS
                dve.wait_ge(w2_high, s + 1)
                dve.tensor_tensor(flat(w2_lo[w][:, :, :]), w_raw[w][:, W13:W13 + W2],
                                  words(flat(w2_hi[w][:, :, :])), ALU.subtract).then_inc(w2_split, 1)

            def read_logits(s, p):
                if inside(s, tiles):
                    dve.wait_ge(logits_done, s + 1)
                    to = route["logits"][:, bass.ds(s * SUBS, SUBS), :]
                    dve.tensor_tensor(to, logits_ps, gb[:, None, :].to_broadcast([P, SUBS, E]), ALU.add)\
                        .then_inc(logits_read, 1)

            def product(s, p, q):
                if not inside(s, tiles):
                    return
                w = p % WSETS
                dve.wait_ge(silu_ready, s * parts + q + 1)
                wait(dve, hlo_ready, s * parts + q - 1)
                dve.scalar_tensor_tensor(out=h[q % 2][:, :], in0=h3_ps[q % 2][:, :], scalar=bias[w][:, 1, q:q + 1],
                                         in1=act_h[q % 2][:, :], op0=ALU.add, op1=ALU.mult).then_inc(h_ready, 1)

            def read_y(s, p):
                if inside(s, tiles):
                    dve.wait_ge(y_done, s + 1)
                    wait(dve, y_stored[p], landed(s - 2, p, Y_DMAS))
                    dve.tensor_copy(y[p][:, :, :], y_ps[:, :, :]).then_inc(y_read, 1)

            def body(i, par):
                product(i, par, 0)
                read_rows(i + 1, 1 - par)
                low_w13(i + 1, 1 - par)
                low(i + 1, 1 - par)
                read_y(i - 1, 1 - par)
                low_w2(i + 1, 1 - par)
                keep_rows(i, par)
                for q in range(1, parts):
                    product(i, par, q)
                if route:
                    read_logits(i + 1, 1 - par)

            steps(dve, body, -1, *LOOP, tiles + 1)

        @block.gpsimd
        def _(pool):
            def h_low(s, p, q):
                if not inside(s, tiles):
                    return
                pool.wait_ge(hhi_ready, s * parts + q + 1)
                pool.tensor_tensor(h_lo[p][:, q, :], h[q % 2][:, :], words(h_hi[p][:, q, :]), ALU.subtract)\
                    .then_inc(hlo_ready, 1)

            def send(s, p):
                if expert_of is None or not inside(s, tiles):
                    return
                hold(pool, scratch, held, s, (y_read, s + 1), (rows_kept, s + 1))
                for j in range(SUBS):
                    pool.indirect_dma_start(out=dst[:, :], out_offset=bass.IndirectOffsetOnAxis(ap=row_at[p][j][:, :], axis=0),
                                            in_=y[p][:, j, :], in_offset=None, bounds_check=dst.shape[0] - 1,
                                            oob_is_err=False).then_inc(y_stored[p], 16)

            if expert_of is not None:
                pool.memset(scratch[:, :], 0.0).then_inc(scratch_ready, 1)
                pool.wait_ge(scratch_ready, 1)

            def body(i, par):
                for q in range(parts):
                    h_low(i, par, q)
                send(i - 1, 1 - par)

            steps(pool, body, 0, *LOOP, tiles + 1)


def routing(nc, logits, gate_b, gates, slot, expert_of, tri, ones, limits, rank_start, SLOT_TILE):
    _, NT, E = logits.shape
    TILES = expert_of.shape[1]
    STEPS = limits.shape[1]

    with ExitStack() as ctx:
        def sb(label, shape, dt=F32):
            return ctx.enter_context(nc.sbuf_tensor(f"r_{label}", shape, dt))

        def sem(label):
            return ctx.enter_context(nc.semaphore(f"r_{label}"))

        tri_s = sb("tri", [P, P])
        ones_s = sb("ones", [P, P])
        gate_bias = sb("gate_bias", [P, E])
        limits_s = sb("limits", [P, STEPS])
        start_s = sb("rank_start", [P, E])
        top = sb("top", [P, NT])
        prob = sb("prob", [P, NT, E])
        ge = sb("ge", [P, NT, E])
        rank = sb("rank", [P, NT, E])
        mask = sb("mask", [P, NT, E])
        before = sb("before", [P, E, NT + 1])
        over = sb("over", [P, E, STEPS])
        used = sb("used", [P, E])
        ends = sb("ends", [P, E + 1])
        pos = sb("pos", [P, NT, E])
        chosen = sb("chosen", [P, NT, E])
        picked = sb("picked", [P, NT, E])
        slot_f = sb("slot_f", [P, NT])
        past = sb("past", [1, TILES, E])
        number = sb("number", [1, TILES])
        rank_ps = ctx.enter_context(nc.psum_tensor("r_rank_ps", [P, NT, E], F32))
        total_ps = ctx.enter_context(nc.psum_tensor("r_total_ps", [P, NT, E], F32))

        in_ready = sem("in_ready")
        mask_ready = sem("mask_ready")
        counted = sem("counted")
        shifted_ready = sem("shifted_ready")
        exp_ready = sem("exp_ready")
        chain = sem("chain")
        block = ctx.enter_context(nc.Block())

        @block.sync
        def _(sp):
            sp.dma_start(tri_s[:, :], tri).then_inc(in_ready, 16)
            sp.dma_start(ones_s[:, :], ones).then_inc(in_ready, 16)
            sp.dma_start(gate_bias[:, :], gate_b.to_broadcast([P, E])).then_inc(in_ready, 16)
            sp.dma_start(limits_s[:, :], limits.to_broadcast([P, STEPS])).then_inc(in_ready, 16)
            sp.dma_start(start_s[:, :], rank_start.to_broadcast([P, E])).then_inc(in_ready, 16)

        @block.scalar
        def _(act):
            act.wait_ge(shifted_ready, 1)
            act.activation(prob[:, :, :], prob[:, :, :], ACT.Exp).then_inc(exp_ready, 1)

        @block.tensor
        def _(pe):
            pe.wait_ge(in_ready, 80)
            pe.wait_ge(mask_ready, 1)
            flat = mask[:, :, :].rearrange("p t e -> p (t e)")
            pe.matmul(rank_ps[:, :, :].rearrange("p t e -> p (t e)"), tri_s[:, :], flat, start=True, stop=True)
            pe.matmul(total_ps[:, :, :].rearrange("p t e -> p (t e)"), ones_s[:, :], flat, start=True, stop=True)\
                .then_inc(counted, 1)

        @block.vector
        def _(dve):
            count = [0]

            def then(ins):
                count[0] += 1
                ins.then_inc(chain, 1)
                dve.wait_ge(chain, count[0])

            def wide(v):
                return v[:, :, None].to_broadcast([P, NT, E])

            dve.wait_ge(in_ready, 80)
            then(dve.tensor_tensor(logits[:, :, :], logits[:, :, :], gate_bias[:, None, :].to_broadcast([P, NT, E]),
                                   ALU.add))
            then(dve.tensor_reduce(top[:, :], logits[:, :, :], mybir.AxisListType.X, ALU.max))
            dve.tensor_tensor(prob[:, :, :], logits[:, :, :], wide(top), ALU.subtract).then_inc(shifted_ready, 1)
            dve.wait_ge(exp_ready, 1)
            then(dve.tensor_reduce(top[:, :], prob[:, :, :], mybir.AxisListType.X, ALU.add))
            then(dve.reciprocal(top[:, :], top[:, :]))
            then(dve.tensor_tensor(prob[:, :, :], prob[:, :, :], wide(top), ALU.mult))
            then(dve.tensor_copy(rank[:, :, :], start_s[:, None, :].to_broadcast([P, NT, E])))
            for d in range(1, E):
                then(dve.tensor_tensor(ge[:, :, 0:E - d], prob[:, :, 0:E - d], prob[:, :, d:E], ALU.is_ge))
                then(dve.tensor_tensor(rank[:, :, d:E], rank[:, :, d:E], ge[:, :, 0:E - d], ALU.add))
                then(dve.tensor_tensor(rank[:, :, 0:E - d], rank[:, :, 0:E - d], ge[:, :, 0:E - d], ALU.subtract))
            dve.tensor_scalar(mask[:, :, :], rank[:, :, :], 2.0, None, ALU.is_lt).then_inc(mask_ready, 1)
            dve.wait_ge(mask_ready, 1)
            dve.memset(before[:, :, 0:1], 0.0)
            dve.memset(ends[:, 0:1], 0.0)
            dve.memset(gates["all"][:, :, E:E + 1], 1.0)
            then(dve.tensor_tensor(gates["all"][:, :, 0:E], mask[:, :, :], prob[:, :, :], ALU.mult))
            dve.wait_ge(counted, 1)
            then(dve.tensor_copy(ge[:, :, :], total_ps[:, :, :]))
            for e in range(E):
                last = dve.tensor_tensor_scan(before[:, e, 1:NT + 1], ones_s[:, 0:1].to_broadcast([P, NT]),
                                              ge[:, :, e], 0.0, ALU.mult, ALU.add)
            then(last)
            then(dve.tensor_tensor(over[:, :, :], before[:, :, NT:NT + 1].to_broadcast([P, E, STEPS]),
                                   limits_s[:, None, :].to_broadcast([P, E, STEPS]), ALU.is_gt))
            then(dve.tensor_reduce(used[:, :], over[:, :, :], mybir.AxisListType.X, ALU.add))
            then(dve.tensor_tensor_scan(ends[:, 1:E + 1], ones_s[:, 0:E], used[:, :], 0.0, ALU.mult, ALU.add))
            for t in range(TILES):
                last = dve.tensor_scalar(past[:, t, :], ends[0:1, 1:E + 1], float(t), None, ALU.is_le)
            then(last)
            then(dve.tensor_reduce(number[:, :], past[:, :, :], mybir.AxisListType.X, ALU.add))
            then(dve.tensor_scalar(expert_of[:, :], number[:, :], float(E - 1), None, ALU.min))
            then(dve.tensor_tensor(pos[:, :, :], rank_ps[:, :, :],
                                   before[:, :, 0:NT].rearrange("p e t -> p t e"), ALU.add))
            then(dve.tensor_scalar(used[:, :], ends[:, 0:E], float(SLOT_TILE), None, ALU.mult))
            then(dve.tensor_tensor(pos[:, :, :], pos[:, :, :], used[:, None, :].to_broadcast([P, NT, E]), ALU.add))
            for k in range(2):
                then(dve.tensor_scalar(chosen[:, :, :], rank[:, :, :], float(k), None, ALU.is_equal))
                then(dve.tensor_tensor(picked[:, :, :], chosen[:, :, :], pos[:, :, :], ALU.mult))
                then(dve.tensor_reduce(slot_f[:, :], picked[:, :, :], mybir.AxisListType.X, ALU.add))
                then(dve.tensor_copy(slot[k][:, :], slot_f[:, :]))
                then(dve.tensor_tensor(picked[:, :, :], chosen[:, :, :], prob[:, :, :], ALU.mult))
                then(dve.tensor_reduce(gates[k][:, :], picked[:, :, :], mybir.AxisListType.X, ALU.add))


def dispatch(nc, xf_dram, slot, numbers, slots_x):
    C = xf_dram.shape[1]
    NT = xf_dram.shape[0] // P
    SUBS = 4
    T = SUBS * P
    tiles = xf_dram.shape[0] // T
    with ExitStack() as ctx:
        def sem(label):
            return ctx.enter_context(nc.semaphore(f"d_{label}"))

        x_in = [[[ctx.enter_context(nc.sbuf_tensor(f"d_x_in{p}{j}{k}", [P, C + 1], F32)) for k in range(2)]
                 for j in range(SUBS)] for p in range(2)]
        row_no = ctx.enter_context(nc.sbuf_tensor("d_row_no", [P, NT, 2], F32))
        row_no_in = sem("row_no_in")
        at = [[[ctx.enter_context(nc.sbuf_tensor(f"d_at{p}{j}{k}", [P, 1], mybir.dt.uint32)) for k in range(2)]
               for j in range(SUBS)] for p in range(2)]
        scratch = ctx.enter_context(nc.sbuf_tensor("d_scratch", [P, 2], F32))
        x_loaded = [sem(f"x_loaded{p}") for p in range(2)]
        at_ready = sem("at_ready")
        scratch_ready = sem("scratch_ready")
        held = sem("held")
        sent = [sem(f"sent{p}") for p in range(2)]
        block = ctx.enter_context(nc.Block())
        LOOP = (2, tiles)

        @block.sync
        def _(sp):
            sp.dma_start(row_no[:, :, :], numbers).then_inc(row_no_in, 16)

            def body(i, par):
                wait(sp, sent[par], landed(i - 2, par, 2 * SUBS))
                for j in range(SUBS):
                    for k in range(2):
                        sp.dma_start(x_in[par][j][k][:, 0:C], xf_dram[bass.ds(i * T + j * P, P), :])\
                            .then_inc(x_loaded[par], 16)

            steps(sp, body, 0, *LOOP, tiles)

        @block.vector
        def _(dve):
            dve.wait_ge(row_no_in, 16)

            def body(i, par):
                wait(dve, sent[par], landed(i - 2, par, 2 * SUBS))
                for j in range(SUBS):
                    for k in range(2):
                        dve.tensor_copy(x_in[par][j][k][:, C:C + 1], row_no[:, bass.ds(i * SUBS + j, 1), k])
                        last = dve.tensor_copy(at[par][j][k][:, :], slot[k][:, bass.ds(i * SUBS + j, 1)])
                last.then_inc(at_ready, 1)

            steps(dve, body, 0, *LOOP, tiles)

        @block.gpsimd
        def _(pool):
            pool.memset(scratch[:, :], 0.0).then_inc(scratch_ready, 1)
            pool.wait_ge(scratch_ready, 1)

            def body(i, par):
                hold(pool, scratch, held, i, (x_loaded[par], landed(i, par, 2 * SUBS)), (at_ready, i + 1))
                for j in range(SUBS):
                    for k in range(2):
                        pool.indirect_dma_start(out=slots_x[:, :], out_offset=bass.IndirectOffsetOnAxis(ap=at[par][j][k][:, :], axis=0),
                                                in_=x_in[par][j][k][:, :], in_offset=None).then_inc(sent[par], 16)

            steps(pool, body, 0, *LOOP, tiles)
            for p in range(2):
                pool.wait_ge(sent[p], landed(tiles - 2 + p, p, 2 * SUBS))


def combine(nc, x1_dram, shared, expert_y, gates, out_biases, ident, out):
    C = x1_dram.shape[1]
    SUBS = 4
    T = SUBS * P
    tiles = x1_dram.shape[0] // T
    G = gates["all"].shape[2]
    with ExitStack() as ctx:
        def sb(label, shape, dt=F32):
            return ctx.enter_context(nc.sbuf_tensor(f"c_{label}", shape, dt))

        def sem(label):
            return ctx.enter_context(nc.semaphore(f"c_{label}"))

        eye = sb("eye", [P, P])
        b_out = sb("b_out", [G, C])
        scale_c = sb("scale_c", [P, 4, SUBS])
        ye = [sb(f"ye{p}", [P, SUBS, 2, C]) for p in range(2)]
        ys = [sb(f"ys{p}", [P, SUBS, C]) for p in range(2)]
        x1 = [sb(f"x1{p}", [P, SUBS, C]) for p in range(2)]
        gt = [sb(f"gt{p}", [G, T]) for p in range(2)]
        gate_now = [sb(f"gate_now{p}", [P, 2, SUBS]) for p in range(2)]
        acc = [sb(f"acc{p}", [P, SUBS, C]) for p in range(2)]
        normal = [sb(f"normal{p}", [P, SUBS, C]) for p in range(2)]
        stats = [sb(f"stats{p}", [P, SUBS, 6]) for p in range(2)]
        sums = [sb(f"sums{p}", [P, SUBS, 2]) for p in range(2)]
        half_diff = [sb(f"half_diff{p}", [P, SUBS]) for p in range(2)]
        var = [sb(f"var{p}", [P, SUBS]) for p in range(2)]
        mean = [sb(f"mean{p}", [P, SUBS]) for p in range(2)]
        rstd = [sb(f"rstd{p}", [P, SUBS]) for p in range(2)]
        res = [sb(f"res{p}", [P, SUBS, C]) for p in range(2)]
        gt_ps = [ctx.enter_context(nc.psum_tensor(f"c_gt_ps{p}", [P, T], F32)) for p in range(2)]
        b_ps = [ctx.enter_context(nc.psum_tensor(f"c_b_ps{p}", [P, SUBS, C], F32)) for p in range(2)]

        consts_in = sem("consts_in")
        scale_c_ready = sem("scale_c_ready")
        at_ready = sem("at_ready")
        loaded = [sem(f"loaded{p}") for p in range(2)]
        x1_loaded = [sem(f"x1_loaded{p}") for p in range(2)]
        gt_turned = sem("gt_turned")
        gt_ready = sem("gt_ready")
        b_done = sem("b_done")
        sum_b = sem("sum_b")
        sum_0 = sem("sum_0")
        sum_1 = sem("sum_1")
        stats_ready = sem("stats_ready")
        scales_ordered = sem("scales_ordered")
        rstd_ready = sem("rstd_ready")
        normed = sem("normed")
        res_ready = sem("res_ready")
        stored = [sem(f"stored{p}") for p in range(2)]
        block = ctx.enter_context(nc.Block())
        LOOP = (4, tiles - 2)

        def rows(dram, i):
            return dram[bass.ds(i * T, T), :].rearrange("(j p) c -> p j c", p=P)

        @block.sync
        def _(sp):
            sp.dma_start(eye[:, :], ident).then_inc(consts_in, 16)
            sp.dma_start(b_out[:, :], out_biases).then_inc(consts_in, 16)

            def body(i, par):
                if inside(i, tiles):
                    wait(sp, sum_1, i - 1)
                    sp.dma_start(ys[par][:, :, :], rows(shared, i)).then_inc(loaded[par], 16)
                    sp.dma_start(ye[par][:, :, :, :], expert_y[bass.ds(i * (2 * T), 2 * T), :]
                                 .rearrange("(j p k) c -> p j k c", p=P, k=2)).then_inc(loaded[par], 16)

            steps(sp, body, 0, *LOOP, tiles)
            for p in range(2):
                sp.wait_ge(stored[p], 16 * (tiles // 2))

        @block.tensor
        def _(pe):
            pe.wait_ge(consts_in, 32)

            def turn(s, p):
                if not inside(s, tiles):
                    return
                pe.wait_ge(at_ready, s + 1)
                wait(pe, gt_ready, s - 1)
                for j in range(SUBS):
                    last = pe.transpose(gt_ps[p][0:G, j * P:(j + 1) * P], gates["now"][p][:, j, :], eye[:, :])
                last.then_inc(gt_turned, 1)

            def bias(s, p):
                if not inside(s, tiles):
                    return
                pe.wait_ge(gt_ready, s + 1)
                wait(pe, sum_b, s - 1)
                for j in range(SUBS):
                    last = pe.matmul(b_ps[p][:, j, :], gt[p][:, j * P:(j + 1) * P], b_out[:, :],
                                     start=True, stop=True)
                last.then_inc(b_done, 1)

            def body(i, par):
                turn(i, par)
                bias(i, par)

            steps(pe, body, 0, *LOOP, tiles)

        @block.scalar
        def _(act):
            def body(i, par):
                if inside(i, tiles):
                    act.wait_ge(gt_turned, i + 1)
                    wait(act, b_done, i - 1)
                    act.activation(gt[par][:, :], gt_ps[par][0:G, :], ACT.Copy).then_inc(gt_ready, 1)
                if inside(i, tiles):
                    wait(act, res_ready, i - 1)
                    act.dma_start(x1[par][:, :, :], rows(x1_dram, i)).then_inc(x1_loaded[par], 16)
                s = i - 2
                if inside(s, tiles):
                    act.wait_ge(res_ready, s + 1)
                    act.dma_start(rows(out, s), res[par][:, :, :]).then_inc(stored[par], 16)

            steps(act, body, 0, *LOOP, tiles + 2)

        @block.vector
        def _(dve):
            def fetch(s, p):
                if not inside(s, tiles):
                    return
                wait(dve, gt_turned, s - 1)
                for k in range(2):
                    dve.tensor_copy(gate_now[p][:, k, :], gates[k][:, bass.ds(s * SUBS, SUBS)])
                dve.tensor_copy(gates["now"][p][:, :, :], gates["all"][:, bass.ds(s * SUBS, SUBS), :])\
                    .then_inc(at_ready, 1)

            def add(s, p):
                if not inside(s, tiles):
                    return
                dve.wait_ge(b_done, s + 1)
                dve.wait_ge(loaded[p], landed(s, p, 2))
                wait(dve, normed, s - 1)
                dve.tensor_tensor(acc[p][:, :, :], b_ps[p][:, :, :], ys[p][:, :, :], ALU.add).then_inc(sum_b, 1)
                dve.wait_ge(sum_b, s + 1)
                dve.wait_ge(at_ready, s + 1)
                for k, done in ((0, sum_0), (1, sum_1)):
                    for j in range(SUBS):
                        last = dve.scalar_tensor_tensor(out=acc[p][:, j, :], in0=ye[p][:, j, k, :],
                                                        scalar=gate_now[p][:, k, j:j + 1], in1=acc[p][:, j, :],
                                                        op0=ALU.mult, op1=ALU.add)
                    last.then_inc(done, 1)
                    dve.wait_ge(done, s + 1)
                for j in range(SUBS):
                    last = dve.bn_stats(stats[p][:, j, :], acc[p][:, j, :])
                last.then_inc(stats_ready, 1)

            def finish(s, p):
                if not inside(s, tiles):
                    return
                dve.wait_ge(rstd_ready, s + 1)
                wait(dve, res_ready, s - 1)
                for j in range(SUBS):
                    last = dve.tensor_scalar(normal[p][:, j, :], acc[p][:, j, :], mean[p][:, j:j + 1],
                                             rstd[p][:, j:j + 1], ALU.subtract, ALU.mult)
                last.then_inc(normed, 1)

            def body(i, par):
                fetch(i + 1, 1 - par)
                add(i, par)
                finish(i - 1, 1 - par)

            steps(dve, body, -1, *LOOP, tiles + 1)

        @block.gpsimd
        def _(pool):
            scale_constants(pool, scale_c, C, scale_c_ready)

            def inverse_std(s, p):
                if not inside(s, tiles):
                    return
                pool.wait_ge(stats_ready, s + 1)
                layernorm_scales(pool, scale_c, stats[p], sums[p], half_diff[p], var[p], mean[p], rstd[p],
                                 scales_ordered, s, rstd_ready)

            def add_x1(s, p):
                if not inside(s, tiles):
                    return
                pool.wait_ge(normed, s + 1)
                wait(pool, stored[p], landed(s - 2, p))
                pool.wait_ge(x1_loaded[p], landed(s, p))
                pool.tensor_tensor(res[p][:, :, :], normal[p][:, :, :], x1[p][:, :, :], ALU.add).then_inc(res_ready, 1)

            def body(i, par):
                inverse_std(i, par)
                add_x1(i - 1, 1 - par)

            steps(pool, body, 0, *LOOP, tiles + 1)


SLOT_TILE = 512


def sandwich(nc, x, attn_w, mix, decay, first, ident, tri, ones, limits, rank_start, ffn_w, expert_biases,
             shared_biases, gate_w, gate_b, out_biases, numbers, out):
    B, T, C = x.shape
    TOKENS = B * T
    E = gate_w.shape[2]
    EXPERTS_W = 6 * C * (C // P) // 2
    MAX_TILES = (2 * TOKENS + E * (SLOT_TILE - 1)) // SLOT_TILE
    TILES = MAX_TILES + MAX_TILES % 2
    COLS = ffn_w.shape[1]

    x1_dram = nc.dram_tensor("x1_dram", (B, T, C), F32, kind="Internal").ap()
    xf_dram = nc.dram_tensor("xf_dram", (B, T, C), F32, kind="Internal").ap()
    slots_x = nc.dram_tensor("slots_x", (TILES * SLOT_TILE, C + 1), F32, kind="Internal").ap()
    expert_y = nc.dram_tensor("expert_y", (2 * TOKENS, C), F32, kind="Internal").ap()
    shared_y = nc.dram_tensor("shared_y", (TOKENS, C), F32, kind="Internal").ap()
    tokens = "b t c -> (b t) c"

    with ExitStack() as ctx:
        def sb(label, shape, dt=F32):
            return ctx.enter_context(nc.sbuf_tensor(label, shape, dt))

        NT = TOKENS // P
        logits = sb("logits", [P, NT, E])
        gates = {0: sb("gate0", [P, NT]), 1: sb("gate1", [P, NT]), "all": sb("gates_all", [P, NT, E + 1]),
                 "now": [sb(f"gates_now{p}", [P, 4, E + 1]) for p in range(2)]}
        slot = [sb(f"slot{k}", [P, NT], mybir.dt.uint32) for k in range(2)]
        expert_of = sb("expert_of", [1, TILES], mybir.dt.int32)
        shared_at = E * EXPERTS_W
        first_pass(nc, x, attn_w, mix, decay, first, ident, ffn_w[:, shared_at:COLS], shared_biases, gate_w, logits,
                   x1_dram, xf_dram, shared_y, slots_x)
        routing(nc, logits, gate_b, gates, slot, expert_of, tri, ones, limits, rank_start, SLOT_TILE)
        dispatch(nc, xf_dram.rearrange(tokens), slot, numbers, slots_x)
        swiglu(nc, "ex", TILES, 2, slots_x, expert_y, ffn_w[:, 0:shared_at],
               expert_biases, ident, expert_of=expert_of)
        combine(nc, x1_dram.rearrange(tokens), shared_y, expert_y, gates, out_biases, ident,
                out.rearrange(tokens))


def kernel(**inputs):
    import numpy as _np
    import concourse.bacc as _bacc
    from concourse import mybir as _mybir
    from concourse.bass_utils import run_bass_kernel_spmd as _run

    def get(name):
        return _np.asarray(inputs["L0_" + name])

    def chunked(w):
        n, m = w.shape
        return w.T.reshape(m // 128, 128, n).transpose(1, 0, 2)

    def columns(v):
        return v.reshape(-1, 128).T

    w1, w3, w2 = get("ffn_w1"), get("ffn_w3"), get("ffn_w2")
    ffn = [chunked(w[e]).reshape(128, -1) for e in range(w1.shape[0]) for w in (w1, w3, w2)]
    ffn += [chunked(get(n)).reshape(128, -1) for n in ("ffn_ws1", "ffn_ws3", "ffn_ws2")]
    tokens, slot_tile = get("attn_x").shape[0] * get("attn_x").shape[1], 512
    arrays = {
        "x": get("attn_x"),
        "attn_w": _np.stack([chunked(get(n)) for n in ("attn_Wk", "attn_Wv", "attn_Wr", "attn_Wo")], 1),
        "mix": _np.stack([columns(get(n)) for n in ("attn_mix_k", "attn_mix_v", "attn_mix_r")], 1),
        "decay": columns(get("attn_spatial_decay")),
        "first": columns(get("attn_spatial_first")),
        "ident": _np.eye(128, dtype=_np.float32),
        "tri": _np.triu(_np.ones((128, 128), _np.float32), 1),
        "ones": _np.ones((128, 128), _np.float32),
        "limits": _np.arange(0, tokens, slot_tile, dtype=_np.float32)[None],
        "rank_start": _np.arange(7, -1, -1, dtype=_np.float32)[None],
        "ffn_w": _np.concatenate(ffn, 1),
        "expert_biases": _np.stack([_np.stack([columns(b[e]) for b in (get("ffn_b1"), get("ffn_b3"))], 1)
                                    for e in range(w1.shape[0])], 0),
        "shared_biases": _np.stack([columns(get("ffn_bs1")), columns(get("ffn_bs3"))], 1),
        "gate_w": chunked(get("ffn_gate_w")),
        "gate_b": get("ffn_gate_b")[None],
        "numbers": _np.arange(2 * tokens, dtype=_np.float32).reshape(-1, 128, 2).transpose(1, 0, 2),
        "out_biases": _np.concatenate([get("ffn_b2"), get("ffn_bs2")[None]], 0),
    }
    nc = _bacc.Bacc("TRN2", target_bir_lowering=False, num_devices=1)
    args = {}
    for name in arrays:
        a = arrays[name] = _np.ascontiguousarray(arrays[name])
        args[name] = nc.dram_tensor(name, a.shape, _mybir.dt.from_np(a.dtype), kind="ExternalInput").ap()
    args["out"] = nc.dram_tensor("out", arrays["x"].shape, _mybir.dt.float32, kind="ExternalOutput").ap()
    sandwich(nc, **args)
    r = _run(nc, [arrays], core_ids=[0])
    return r.results[0]["out"]
```

```python
from contextlib import ExitStack

import concourse.bass as bass
from concourse import mybir

F32 = mybir.dt.float32
F32R = mybir.dt.float32r
ALU = mybir.AluOpType
ACT = mybir.ActivationFunctionType

P = 128
EPS = 1e-5
NOBODY = 1e9


def inside(s, n):
    return not isinstance(s, int) or 0 <= s < n


def wait(eng, sem, count):
    if not isinstance(count, int) or count > 0:
        eng.wait_ge(sem, count)


def hold(pool, scratch, held, step, *waits):
    for sem, count in waits:
        wait(pool, sem, count)
    wait(pool, held, step)
    pool.tensor_tensor(scratch[:, 0:1], scratch[:, 1:2], scratch[:, 1:2], ALU.add).then_inc(held, 1)


SCALES = 4
HALF, PER_ROW, EPSILON, MINUS_HALF = range(4)


def scale_constants(pool, consts, row, ready):
    for k, v in ((HALF, 0.5), (PER_ROW, 1.0 / row), (EPSILON, EPS), (MINUS_HALF, -0.5)):
        pool.memset(consts[:, k, :], v).then_inc(ready, 1)
    pool.wait_ge(ready, 4)


def layernorm_scales(pool, consts, stats, sums, half_diff, var, mean, rstd, ordered, s, ready, negative=False):
    pool.tensor_tensor(sums[:, :, :], stats[:, :, 1:3], stats[:, :, 4:6], ALU.add)
    pool.tensor_tensor(half_diff[:, :], stats[:, :, 1], stats[:, :, 4], ALU.subtract).then_inc(ordered, 1)
    pool.wait_ge(ordered, s * SCALES + 1)
    pool.tensor_tensor(mean[:, :], sums[:, :, 0], consts[:, MINUS_HALF if negative else HALF, :], ALU.mult)
    pool.tensor_tensor(half_diff[:, :], half_diff[:, :], consts[:, HALF, :], ALU.mult)
    pool.tensor_tensor(var[:, :], sums[:, :, 1], consts[:, PER_ROW, :], ALU.mult).then_inc(ordered, 1)
    pool.wait_ge(ordered, s * SCALES + 2)
    pool.tensor_tensor(half_diff[:, :], half_diff[:, :], half_diff[:, :], ALU.mult)
    pool.tensor_tensor(var[:, :], var[:, :], consts[:, EPSILON, :], ALU.add).then_inc(ordered, 1)
    pool.wait_ge(ordered, s * SCALES + 3)
    pool.tensor_tensor(var[:, :], var[:, :], half_diff[:, :], ALU.add).then_inc(ordered, 1)
    pool.wait_ge(ordered, s * SCALES + 4)
    pool.tensor_tensor(rstd[:, :], var[:, :], consts[:, MINUS_HALF, :], ALU.pow).then_inc(ready, 1)


def landed(s, parity, dmas=1):
    return (s - parity + 2) * (8 * dmas)


def steps(eng, body, first, loop_first, loop_end, end):
    for i in range(first, loop_first):
        body(i, i % 2)
    with eng.Fori(loop_first // 2, loop_end // 2) as pair:
        body(pair * 2, 0)
        body(pair * 2 + 1, 1)
    for i in range(loop_end, end):
        body(i, i % 2)


def split_weights(nc, attn_w, mix, ffn_w, gate_w, w_hi, w_lo, wo_hi, wo_lo, w13, w2, gw, load_ahead):
    K, V, R = range(3)
    HERE, SHIFT, REST = range(3)
    CC, C = attn_w.shape[2:]
    W13 = w13["hi"].shape[1] * w13["hi"].shape[2] * w13["hi"].shape[3]

    with ExitStack() as ctx:
        def sb(name, shape, dt=F32):
            return ctx.enter_context(nc.sbuf_tensor(f"w_{name}", shape, dt))

        def sem(name):
            return ctx.enter_context(nc.semaphore(f"w_{name}"))

        w_raw = sb("raw", [P, 4, CC, C])
        w_mixed = sb("mixed", [P, 3, 3, C])
        ffn_raw = sb("ffn_raw", [P, ffn_w.shape[1]])
        gw_raw = sb("gw_raw", list(gate_w.shape))
        mix_c = sb("mix_c", [P, 3, CC])
        unmix = sb("unmix", [P, 3, CC])
        both = sb("both", [P, 3, CC])
        mix_in = sem("mix_in")
        w_in = sem("w_in")
        ffn_in = sem("ffn_in")
        mixes_ready = sem("mixes_ready")
        mixed_ready = sem("mixed_ready")
        hi_ready = sem("hi_ready")
        ffn_hi_ready = sem("ffn_hi_ready")
        block = ctx.enter_context(nc.Block())

        def words(ap):
            return ap.bitcast(F32)

        def flat(w):
            return w.rearrange("p a b n -> p (a b n)") if len(w.shape) == 4 else w.rearrange("p a n -> p (a n)")

        @block.sync
        def _(sp):
            sp.dma_start(mix_c[:, :, :], mix).then_inc(mix_in, 16)
            sp.dma_start(w_raw[:, :, :, :], attn_w).then_inc(w_in, 16)
            sp.dma_start(ffn_raw[:, :], ffn_w).then_inc(ffn_in, 16)
            sp.dma_start(gw_raw[:, :, :], gate_w).then_inc(ffn_in, 16)
            load_ahead(sp)

        @block.scalar
        def _(act):
            act.wait_ge(ffn_in, 32)
            act.activation(flat(w13["hi"][:, :, :, :]), ffn_raw[:, 0:W13], ACT.Copy).then_inc(ffn_hi_ready, 1)
            act.activation(flat(w2["hi"][:, :, :]), ffn_raw[:, W13:], ACT.Copy).then_inc(ffn_hi_ready, 1)
            act.activation(gw["hi"][:, :, :], gw_raw[:, :, :], ACT.Copy).then_inc(ffn_hi_ready, 1)
            act.wait_ge(mixed_ready, 1)
            act.activation(w_hi[:, :, :, :], w_mixed[:, :, :, :], ACT.Copy).then_inc(hi_ready, 1)
            act.activation(wo_hi[:, :, :], w_raw[:, 3, :, :], ACT.Copy).then_inc(hi_ready, 1)

        @block.gpsimd
        def _(pool):
            pool.wait_ge(ffn_hi_ready, 3)
            pool.tensor_tensor(flat(w2["lo"][:, :, :]), ffn_raw[:, W13:], words(flat(w2["hi"][:, :, :])), ALU.subtract)
            pool.tensor_tensor(gw["lo"][:, :, :], gw_raw[:, :, :], words(gw["hi"][:, :, :]), ALU.subtract)

        @block.vector
        def _(dve):
            dve.wait_ge(mix_in, 16)
            dve.tensor_scalar(unmix[:, :, :], mix_c[:, :, :], -1.0, 1.0, ALU.mult, ALU.add).then_inc(mixes_ready, 1)
            dve.wait_ge(mixes_ready, 1)
            dve.tensor_tensor(both[:, :, :], mix_c[:, :, :], unmix[:, :, :], ALU.add).then_inc(mixes_ready, 1)
            dve.wait_ge(mixes_ready, 2)
            dve.wait_ge(w_in, 16)
            for which in (K, V, R):
                for part, c, by in ((HERE, 0, mix_c), (SHIFT, 0, unmix), (REST, 1, both)):
                    last = dve.tensor_scalar(w_mixed[:, which, part, :], w_raw[:, which, c, :],
                                             by[:, which, c:c + 1], None, ALU.mult)
            last.then_inc(mixed_ready, 1)
            dve.wait_ge(ffn_hi_ready, 1)
            dve.tensor_tensor(flat(w13["lo"][:, :, :, :]), ffn_raw[:, 0:W13], words(flat(w13["hi"][:, :, :, :])),
                              ALU.subtract)
            dve.wait_ge(hi_ready, 2)
            dve.tensor_tensor(w_lo[:, :, :, :], w_mixed[:, :, :, :], words(w_hi[:, :, :, :]), ALU.subtract)
            dve.tensor_tensor(wo_lo[:, :, :], w_raw[:, 3, :, :], words(wo_hi[:, :, :]), ALU.subtract)


def first_pass(nc, x, attn_w, mix, decay, first, ident, tri, ones, ffn_w, shared_biases, gate_w, gate_b, rank_start,
               earlier, region_start, numbers, limits, tile_slots, logits, rank, count, tile_of, x1_dram, shared_y,
               slots_x):
    SEQS, T, C = x.shape
    SUBS = T // P
    ROW = slots_x.shape[1]
    CC = C // P
    SHIFTED = C // 4
    Q = shared_biases.shape[2]
    E = gate_w.shape[2]
    TILES = tile_slots.shape[1]
    LIMITS = limits.shape[1]
    REGION = slots_x.shape[0] // (E + 1)
    TILE = SUBS * P
    assert CC == 2 and SUBS == 4 and 2 * SHIFTED == P and T == 512 and SEQS % 2 == 0 and Q == 4
    K, V, R = range(3)
    HERE, SHIFT, REST = range(3)

    with ExitStack() as ctx:
        def sb(name, shape, dt=F32):
            return ctx.enter_context(nc.sbuf_tensor(f"f_{name}", shape, dt))

        def psum(name, shape):
            return ctx.enter_context(nc.psum_tensor(f"f_{name}", shape, F32))

        def sem(name):
            return ctx.enter_context(nc.semaphore(f"f_{name}"))

        w_hi = sb("w_hi", [P, 3, 3, C], F32R)
        w_lo = sb("w_lo", [P, 3, 3, C], F32R)
        wo_hi = sb("wo_hi", [P, CC, C], F32R)
        wo_lo = sb("wo_lo", [P, CC, C], F32R)
        w13 = {h: sb(f"w13_{h}", [P, 2, CC, Q * P], F32R) for h in ("hi", "lo")}
        w2 = {h: sb(f"w2_{h}", [P, Q, C], F32R) for h in ("hi", "lo")}
        gw = {h: sb(f"gw_{h}", [P, CC, E], F32R) for h in ("hi", "lo")}

        eye = sb("eye", [P, P])
        bias = sb("bias", [P, 2, Q])
        decay_c = sb("decay_c", [P, CC])
        first_c = sb("first_c", [P, CC])
        x_in = [sb(f"x_in{p}", [P, SUBS, C]) for p in range(2)]
        tri_in = sb("tri_in", [P, P])
        ones_in = sb("ones_in", [P, P])
        gate_bias = sb("gate_bias", [P, E])
        start_s = sb("rank_start", [P, E])
        earlier_s = sb("earlier", [P, 1, E, E])
        number_s = sb("numbers", [P, SEQS * SUBS])
        limits_s = sb("limits", [P, LIMITS])
        region_s = sb("region_start", [P, E])
        tile_no = sb("tile_no", [P, TILES])
        consts_in = sem("consts_in")
        x_loaded = [sem(f"x_loaded{p}") for p in range(2)]

        def by_tiles(rows):
            return rows.rearrange("(j p) c -> p j c", p=P)

        def load_ahead(sp):
            sp.dma_start(eye[:, :], ident).then_inc(consts_in, 16)
            sp.dma_start(decay_c[:, :], decay).then_inc(consts_in, 16)
            sp.dma_start(first_c[:, :], first).then_inc(consts_in, 16)
            sp.dma_start(bias[:, :, :], shared_biases).then_inc(consts_in, 16)
            sp.dma_start(tri_in[:, :], tri).then_inc(consts_in, 16)
            sp.dma_start(ones_in[:, :], ones).then_inc(consts_in, 16)
            sp.dma_start(gate_bias[:, :], gate_b.to_broadcast([P, E])).then_inc(consts_in, 16)
            sp.dma_start(start_s[:, :], rank_start.to_broadcast([P, E])).then_inc(consts_in, 16)
            sp.dma_start(earlier_s[:, 0, :, :].rearrange("p a b -> p (a b)"), earlier.to_broadcast([P, E * E]))\
                .then_inc(consts_in, 16)
            sp.dma_start(count[:, :], region_start.to_broadcast([P, E])).then_inc(consts_in, 16)
            sp.dma_start(number_s[:, :], numbers).then_inc(consts_in, 16)
            sp.dma_start(limits_s[:, :], limits.to_broadcast([P, LIMITS])).then_inc(consts_in, 16)
            sp.dma_start(region_s[:, :], region_start.to_broadcast([P, E])).then_inc(consts_in, 16)
            sp.dma_start(tile_no[:, :], tile_slots.to_broadcast([P, TILES])).then_inc(consts_in, 16)
            for n in range(2):
                sp.dma_start(x_in[n][:, :, :], by_tiles(x[n, :, :])).then_inc(x_loaded[n], 16)

        split_weights(nc, attn_w, mix, ffn_w, gate_w, w_hi, w_lo, wo_hi, wo_lo, w13, w2, gw, load_ahead)

        ew = sb("ew", [P, CC])
        u = sb("u", [P, CC])
        scale_c = sb("scale_c", [P, 4, SUBS])

        x_res = [sb(f"x_res{p}", [P, SUBS, C]) for p in range(2)]
        xn = sb("xn", [P, SUBS, C])
        z_hi = sb("z_hi", [P, CC, T], F32R)
        z_lo = sb("z_lo", [P, CC, T], F32R)
        zs_hi = sb("zs_hi", [P, T], F32R)
        zs_lo = sb("zs_lo", [P, T], F32R)
        ek = [sb(f"ek{c}", [P, T]) for c in range(CC)]
        eku = [sb(f"eku{c}", [P, T]) for c in range(CC)]
        er = [sb(f"er{c}", [P, T]) for c in range(CC)]
        ekv = [sb(f"ekv{c}", [P, T]) for c in range(CC)]
        a_sum = [sb(f"a_sum{c}", [P, T + 1]) for c in range(CC)]
        b_sum = [sb(f"b_sum{c}", [P, T + 1]) for c in range(CC)]
        num = [sb(f"num{c}", [P, T]) for c in range(CC)]
        den = [sb(f"den{c}", [P, T]) for c in range(CC)]
        g = [sb(f"g{c}", [P, T]) for c in range(CC)]
        g_hi = sb("g_hi", [P, CC, T], F32R)
        g_lo = sb("g_lo", [P, CC, T], F32R)
        on = sb("on", [P, SUBS, C])
        x1 = [sb(f"x1{p}", [P, SUBS, C]) for p in range(2)]
        xf = [sb(f"xf{p}", [P, SUBS, ROW]) for p in range(2)]
        f_hi = [sb(f"f_hi{p}", [P, CC, T], F32R) for p in range(2)]
        f_lo = [sb(f"f_lo{p}", [P, CC, T], F32R) for p in range(2)]
        act_h = [sb(f"act_h{p}", [P, T]) for p in range(2)]
        h = [sb(f"h{q}", [P, T]) for q in range(Q)]
        h_hi = sb("h_hi", [P, Q, T], F32R)
        h_lo = sb("h_lo", [P, Q, T], F32R)
        y = [sb(f"y{half}", [P, SUBS // 2, C]) for half in range(2)]
        tri_s = sb("tri", [P, P], F32R)
        ones_s = sb("ones", [P, P], F32R)
        lg = sb("lg", [P, SUBS, E])
        as_high = sb("as_high", [P, SUBS, E, E])
        before_it = sb("before_it", [P, SUBS, E])
        after_it = sb("after_it", [P, SUBS, E])
        rank_now = sb("rank_now", [P, SUBS, E])
        mask = sb("mask", [P, SUBS, E], F32R)
        pos = sb("pos", [P, SUBS, E])
        picked = [sb(f"picked{k}", [P, SUBS, E]) for k in range(2)]
        slot = [sb(f"slot{k}", [P, SUBS]) for k in range(2)]
        at = [[sb(f"at{p}{k}", [P, SUBS], mybir.dt.uint32) for k in range(2)] for p in range(2)]
        warm = sb("warm", [P, 2])
        nobody = sb("nobody", [P, 1, ROW])
        free_slot = sb("free_slot", [1, E], mybir.dt.int32)
        tokens_of = sb("tokens_of", [P, E])
        over = sb("over", [P, E, LIMITS])
        used = sb("used", [P, E])
        ends = sb("ends", [P, E + 1])
        shift = sb("shift", [P, E])
        began, ended, at_tile = (xn[:, :, :].rearrange("p j c -> p (j c)")[:, k * TILES * E:(k + 1) * TILES * E]
                                 .rearrange("p (t e) -> p t e", e=E) for k in range(3))
        number = sb("number", [P, TILES])
        unused = sb("unused", [P, TILES])
        one = sb("one", [P, 1])
        scratch = sb("scratch", [P, 2])
        LN_X, LN_O, LN_X1 = range(3)
        stats = [[sb(f"stats{k}{p}", [P, SUBS, 6]) for p in range(2)] for k in range(3)]
        sums = [[sb(f"sums{k}{p}", [P, SUBS, 2]) for p in range(2)] for k in range(3)]
        half_diff = [[sb(f"half_diff{k}{p}", [P, SUBS]) for p in range(2)] for k in range(3)]
        var = [[sb(f"var{k}{p}", [P, SUBS]) for p in range(2)] for k in range(3)]
        mean = [[sb(f"mean{k}{p}", [P, SUBS]) for p in range(2)] for k in range(3)]
        rstd = [[sb(f"rstd{k}{p}", [P, SUBS]) for p in range(2)] for k in range(3)]
        offset = [sb(f"offset{p}", [P, SUBS]) for p in range(2)]

        k_ps = psum("k_ps", [P, T])
        v_ps = psum("v_ps", [P, T])
        r_ps = psum("r_ps", [P, T])
        h1_ps = psum("h1_ps", [P, T])
        h3_ps = psum("h3_ps", [P, T])
        turn_ps = psum("turn_ps", [P, CC, T])
        o_ps = turn_ps[:, :, :].rearrange("p a (b n) -> p (a b) n", n=C)
        shared_ps = psum("shared_ps", [P, T])
        y_ps = shared_ps[:, :].rearrange("p (j n) -> p j n", n=C)
        logits_ps = shared_ps[:, 0:SUBS * E].rearrange("p (j e) -> p j e", e=E)
        rank_ps = logits_ps
        total_ps = shared_ps[:, SUBS * E:(SUBS + 1) * E]

        consts_done = sem("consts_done")
        zs_cleared = sem("zs_cleared")
        u_ready = sem("u_ready")
        ew_ready = sem("ew_ready")
        res_loaded = [sem(f"res_loaded{p}") for p in range(2)]
        stats_ready = [sem(f"stats_ready{k}") for k in range(3)]
        scales_ordered = [sem(f"scales_ordered{k}") for k in range(3)]
        rstd_ready = [sem(f"rstd_ready{k}") for k in range(3)]
        offset_ready = sem("offset_ready")
        xn_ready = sem("xn_ready")
        turned = sem("turned")
        zhi_ready = sem("zhi_ready")
        zlo_ready = sem("zlo_ready")
        zs_ready = sem("zs_ready")
        kvr_done = sem("kvr_done")
        exps_ready = sem("exps_ready")
        ekv_ready = sem("ekv_ready")
        v_used = sem("v_used")
        scans_ready = sem("scans_ready")
        bd_ready = sem("bd_ready")
        den_ready = sem("den_ready")
        rec_ready = sem("rec_ready")
        g_ready = sem("g_ready")
        ghi_ready = sem("ghi_ready")
        glo_ready = sem("glo_ready")
        o_done = sem("o_done")
        on_ready = sem("on_ready")
        x1_ready = sem("x1_ready")
        xf_ready = sem("xf_ready")
        x1_stored = [sem(f"x1_stored{p}") for p in range(2)]
        f_turned = sem("f_turned")
        fhi_ready = sem("fhi_ready")
        flo_ready = sem("flo_ready")
        inner_done = sem("inner_done")
        silu_ready = sem("silu_ready")
        h_ready = sem("h_ready")
        hhi_ready = sem("hhi_ready")
        hlo_ready = sem("hlo_ready")
        y_done = sem("y_done")
        y_read = sem("y_read")
        y_stored = [sem(f"y_stored{half}") for half in range(2)]
        logits_done = sem("logits_done")
        logits_read = sem("logits_read")
        ranking = sem("ranking")
        nobody_ready = sem("nobody_ready")
        free_ready = sem("free_ready")
        cleared = sem("cleared")
        tiling = sem("tiling")
        warmed = sem("warmed")
        mask_ready = sem("mask_ready")
        counted = sem("counted")
        counts_read = sem("counts_read")
        placing = sem("placing")
        at_ready = sem("at_ready")
        scratch_ready = sem("scratch_ready")
        held = sem("held")
        sent = [sem(f"sent{p}") for p in range(2)]
        CONSTS = 14
        RANK_STEPS, PLACE_STEPS = 6, 3
        block = ctx.enter_context(nc.Block())

        LOOP = (4, SEQS - 2)
        END = SEQS + 3

        @block.sync
        def _(sp):
            def clear(at):
                sp.dma_start(by_tiles(slots_x[bass.ds(at, TILE), :]), nobody[:, :, :].to_broadcast([P, SUBS, ROW]))\
                    .then_inc(cleared, 16)

            def clear_tails():
                sp.wait_ge(nobody_ready, 2)
                clear(E * REGION)
                sp.wait_ge(free_ready, 1)
                for e in range(E):
                    clear(sp.value_load(free_slot[0:1, e:e + 1], min_val=e * REGION, max_val=(e + 1) * REGION - TILE))

            def body(i, par):
                if isinstance(i, int) and i == END - 1:
                    clear_tails()
                s = i - 3
                if inside(s, SEQS):
                    for half in range(2):
                        sp.wait_ge(y_read, 2 * s + half + 1)
                        at = (s * 2 + half) * (T // 2)
                        sp.dma_start(by_tiles(shared_y[bass.ds(at, T // 2), :]), y[half][:, :, :])\
                            .then_inc(y_stored[half], 16)
                n = i + 2
                if inside(n, SEQS) and not (isinstance(n, int) and n < 2):
                    wait(sp, xn_ready, n - 1)
                    sp.dma_start(x_in[par][:, :, :], by_tiles(x[n, :, :])).then_inc(x_loaded[par], 16)
                if inside(i, SEQS):
                    wait(sp, x1_ready, i - 1)
                    sp.dma_start(x_res[par][:, :, :], by_tiles(x[i, :, :])).then_inc(res_loaded[par], 16)
                s = i - 1
                if inside(s, SEQS):
                    sp.wait_ge(x1_ready, s + 1)
                    sp.dma_start(by_tiles(x1_dram[s, :, :]), x1[1 - par][:, :, :]).then_inc(x1_stored[1 - par], 16)
                s = i + 1
                if inside(s, SEQS):
                    for ready, z, zs in ((zhi_ready, z_hi[:, 0, :].bitcast(F32), zs_hi[:, :].bitcast(F32)),
                                         (zlo_ready, z_lo[:, 0, :].bitcast(F32), zs_lo[:, :].bitcast(F32))):
                        sp.wait_ge(ready, s + 1)
                        sp.dma_start(zs[0:SHIFTED, 1:T], z[0:SHIFTED, 0:T - 1]).then_inc(zs_ready, 16)
                        sp.dma_start(zs[SHIFTED:P, 0:T - 1], z[SHIFTED:P, 1:T]).then_inc(zs_ready, 16)

            steps(sp, body, -2, *LOOP, END)
            sp.wait_ge(cleared, 16 * (E + 1))
            for p in range(2):
                sp.wait_ge(x1_stored[p], 16 * (SEQS // 2))
                sp.wait_ge(y_stored[p], 16 * SEQS)
                sp.wait_ge(sent[p], 16 * 2 * SUBS * (SEQS // 2))

        @block.tensor
        def _(pe):
            pe.wait_ge(consts_in, 16 * CONSTS)

            def turn(s):
                if not inside(s, SEQS):
                    return
                pe.wait_ge(xn_ready, s + 1)
                wait(pe, on_ready, min(s - 1, SEQS) if isinstance(s, int) else s - 1)
                for c in range(CC):
                    for j in range(SUBS):
                        last = pe.transpose(turn_ps[:, c, j * P:(j + 1) * P], xn[:, j, c * P:(c + 1) * P], eye[:, :])
                last.then_inc(turned, 1)

            def kvr(s, c):
                if not inside(s, SEQS):
                    return
                if c == 0:
                    pe.wait_ge(zhi_ready, s + 1)
                    pe.wait_ge(zlo_ready, s + 1)
                wait(pe, exps_ready, 6 * s + 3 * c)
                wait(pe, v_used, 2 * s + c)
                for part, hi, lo in ((HERE, z_hi[:, 0, :], z_lo[:, 0, :]),
                                     (REST, z_hi[:, 1, :], z_lo[:, 1, :]),
                                     (SHIFT, zs_hi[:, :], zs_lo[:, :])):
                    if c == 0 and part == SHIFT:
                        pe.wait_ge(zs_ready, 64 * (s + 1))
                    for which, out in ((K, k_ps), (V, v_ps), (R, r_ps)):
                        for n, (w, z) in enumerate(((w_hi, hi), (w_hi, lo), (w_lo, hi))):
                            last = pe.matmul(out[:, :], w[:, which, part, c * P:(c + 1) * P], z,
                                             start=(part == HERE and n == 0), stop=(part == SHIFT and n == 2))
                last.then_inc(kvr_done, 1)

            def project(s):
                if not inside(s, SEQS):
                    return
                pe.wait_ge(glo_ready, 2 * s + 2)
                wait(pe, zlo_ready, min(s + 2, SEQS) if isinstance(s, int) else s + 2)
                for j in range(SUBS):
                    n = 0
                    for c in range(CC):
                        for a, w in ((g_hi, wo_hi), (g_lo, wo_hi), (g_hi, wo_lo)):
                            last = pe.matmul(o_ps[:, j, :], a[:, c, j * P:(j + 1) * P], w[:, c, :],
                                             start=(n == 0), stop=(n == 5))
                            n += 1
                last.then_inc(o_done, 1)

            def turn_xf(s, p, c):
                if not inside(s, SEQS):
                    return
                if c == 0:
                    pe.wait_ge(xf_ready, s + 1)
                    wait(pe, counts_read, s)
                    wait(pe, y_read, 2 * s - 2)
                else:
                    pe.wait_ge(flo_ready, 2 * s + 1)
                for j in range(SUBS):
                    last = pe.transpose(shared_ps[:, j * P:(j + 1) * P], xf[p][:, j, c * P:(c + 1) * P], eye[:, :])
                last.then_inc(f_turned, 1)

            def route(s, p):
                if not inside(s, SEQS):
                    return
                pe.wait_ge(flo_ready, 2 * s + 2)
                for j in range(SUBS):
                    n = 0
                    for c in range(CC):
                        for a, w in ((f_hi, gw["hi"]), (f_lo, gw["hi"]), (f_hi, gw["lo"])):
                            last = pe.matmul(logits_ps[:, j, :], a[p][:, c, j * P:(j + 1) * P], w[:, c, :],
                                             start=(n == 0), stop=(n == 5))
                            n += 1
                last.then_inc(logits_done, 1)

            def count_tokens(s):
                if not inside(s, SEQS):
                    return
                pe.wait_ge(mask_ready, s + 1)
                for j in range(SUBS):
                    for n in range(j):
                        pe.matmul(rank_ps[:, j, :], ones_s[:, :], mask[:, n, :], start=(n == 0), stop=False)
                    pe.matmul(rank_ps[:, j, :], tri_s[:, :], mask[:, j, :], start=(j == 0), stop=True)
                for n in range(SUBS):
                    last = pe.matmul(total_ps, ones_s[:, :], mask[:, n, :], start=(n == 0), stop=(n == SUBS - 1))
                last.then_inc(counted, 1)

            def inner(s, p, q):
                if not inside(s, SEQS):
                    return
                if q == 0:
                    pe.wait_ge(flo_ready, 2 * s + 2)
                for which, out, read in ((0, h1_ps, silu_ready), (1, h3_ps, h_ready)):
                    wait(pe, read, s * Q + q)
                    n = 0
                    for c in range(CC):
                        for a, b in ((w13["hi"], f_hi), (w13["hi"], f_lo), (w13["lo"], f_hi)):
                            last = pe.matmul(out[:, :], a[:, which, c, q * P:(q + 1) * P], b[p][:, c, :],
                                             start=(n == 0), stop=(n == 5))
                            n += 1
                last.then_inc(inner_done, 1)

            def outer(s, half):
                if not inside(s, SEQS):
                    return
                if half == 0:
                    pe.wait_ge(hlo_ready, (s + 1) * Q)
                    pe.wait_ge(counts_read, min(s + 2, SEQS) if isinstance(s, int) else s + 2)
                else:
                    pe.wait_ge(y_read, 2 * s + 1)
                for j in range(SUBS // 2):
                    n = 0
                    at = (half * (SUBS // 2) + j) * P
                    for q in range(Q):
                        for a, b in ((h_hi, w2["hi"]), (h_lo, w2["hi"]), (h_hi, w2["lo"])):
                            last = pe.matmul(y_ps[:, j, :], a[:, q, at:at + P], b[:, q, :],
                                             start=(n == 0), stop=(n == 3 * Q - 1))
                            n += 1
                last.then_inc(y_done, 1)

            def body(i, par):
                kvr(i, 0)
                turn_xf(i - 2, par, 1)
                project(i - 1)
                route(i - 2, par)
                kvr(i, 1)
                count_tokens(i - 2)
                inner(i - 2, par, 0)
                outer(i - 3, 0)
                inner(i - 2, par, 1)
                outer(i - 3, 1)
                inner(i - 2, par, 2)
                turn(i + 1)
                inner(i - 2, par, 3)
                turn_xf(i - 1, 1 - par, 0)

            steps(pe, body, -1, *LOOP, END)

        @block.scalar
        def _(act):
            act.wait_ge(consts_in, 16 * CONSTS)
            act.activation(ew[:, :], decay_c[:, :], ACT.Exp, scale=1.0 / T).then_inc(ew_ready, 1)
            act.wait_ge(u_ready, 1)
            act.wait_ge(scratch_ready, 2)

            def exps(s, c):
                if not inside(s, SEQS):
                    return
                act.wait_ge(kvr_done, 2 * s + c + 1)
                wait(act, den_ready, 2 * s + c - 1)
                act.activation(ek[c][:, :], k_ps[:, :], ACT.Exp).then_inc(exps_ready, 1)
                act.activation(eku[c][:, :], k_ps[:, :], ACT.Exp, bias=u[:, c:c + 1]).then_inc(exps_ready, 1)
                act.activation(er[c][:, :], r_ps[:, :], ACT.Exp, scale=-1.0).then_inc(exps_ready, 1)

            def prepare(i, which, function):
                wait(act, warmed, 2 * (i + 1) + which)
                act.activation(warm[:, 1:2], warm[:, 0:1], function).then_inc(warmed, 1)

            def high(s):
                if not inside(s, SEQS):
                    return
                act.wait_ge(turned, s + 1)
                wait(act, kvr_done, 2 * s)
                if not isinstance(s, int) or s > 0:
                    act.wait_ge(zs_ready, 64 * s)
                act.activation(z_hi[:, :, :], turn_ps[:, :, :], ACT.Copy).then_inc(zhi_ready, 1)

            def g_high(s, c):
                if not inside(s, SEQS):
                    return
                act.wait_ge(g_ready, 2 * s + c + 1)
                wait(act, o_done, s)
                act.activation(g_hi[:, c, :], g[c][:, :], ACT.Copy).then_inc(ghi_ready, 1)

            def normalise_x1(s, p):
                if not inside(s, SEQS):
                    return
                act.wait_ge(offset_ready, s + 1)
                wait(act, sent[p], landed(s - 2, p, 2 * SUBS))
                wait(act, f_turned, 2 * s - 2)
                for j in range(SUBS):
                    last = act.activation(xf[p][:, j, 0:C], x1[p][:, j, :], ACT.Identity, bias=offset[p][:, j:j + 1],
                                          scale=rstd[LN_X1][p][:, j:j + 1])
                last.then_inc(xf_ready, 1)

            def f_high(s, p, c):
                if not inside(s, SEQS):
                    return
                act.wait_ge(f_turned, 2 * s + c + 1)
                wait(act, inner_done, (s - 1) * Q)
                wait(act, logits_done, s - 1)
                act.activation(f_hi[p][:, c, :], shared_ps[:, :], ACT.Copy).then_inc(fhi_ready, 1)

            def silu(s, q):
                if not inside(s, SEQS):
                    return
                act.wait_ge(inner_done, s * Q + q + 1)
                wait(act, h_ready, s * Q + q - 1)
                act.activation(act_h[q % 2][:, :], h1_ps[:, :], ACT.Silu, bias=bias[:, 0, q:q + 1])\
                    .then_inc(silu_ready, 1)

            def h_high(s, q):
                if not inside(s, SEQS):
                    return
                act.wait_ge(h_ready, s * Q + q + 1)
                wait(act, y_done, 2 * s)
                act.activation(h_hi[:, q, :], h[q][:, :], ACT.Copy).then_inc(hhi_ready, 1)

            def read_y(s, half):
                if not inside(s, SEQS):
                    return
                act.wait_ge(y_done, 2 * s + half + 1)
                if not isinstance(s, int) or s > 0:
                    act.wait_ge(y_stored[half], 16 * s)
                act.activation(y[half][:, :, :], y_ps, ACT.Copy).then_inc(y_read, 1)

            def body(i, par):
                h_high(i - 3, 3)
                exps(i, 0)
                f_high(i - 2, par, 1)
                exps(i, 1)
                prepare(i, 0, ACT.Silu)
                silu(i - 2, 0)
                g_high(i, 0)
                read_y(i - 3, 0)
                silu(i - 2, 1)
                read_y(i - 3, 1)
                h_high(i - 2, 0)
                h_high(i - 2, 1)
                silu(i - 2, 2)
                high(i + 1)
                normalise_x1(i - 1, 1 - par)
                h_high(i - 2, 2)
                silu(i - 2, 3)
                prepare(i, 1, ACT.Exp)
                f_high(i - 1, 1 - par, 0)
                g_high(i, 1)

            steps(act, body, -1, *LOOP, END)

        @block.vector
        def _(dve):
            dve.memset(zs_hi[0:SHIFTED, 0:1].bitcast(F32), 0.0)
            dve.memset(zs_hi[SHIFTED:P, T - 1:T].bitcast(F32), 0.0)
            dve.memset(zs_lo[0:SHIFTED, 0:1].bitcast(F32), 0.0)
            dve.memset(zs_lo[SHIFTED:P, T - 1:T].bitcast(F32), 0.0)
            for c in range(CC):
                dve.memset(a_sum[c][:, 0:1], 0.0)
                last = dve.memset(b_sum[c][:, 0:1], 0.0)
            last.then_inc(zs_cleared, 1)
            dve.wait_ge(consts_in, 16 * CONSTS)
            dve.tensor_copy(tri_s[:, :], tri_in[:, :])
            dve.tensor_copy(ones_s[:, :], ones_in[:, :])
            dve.tensor_scalar(u[:, :], first_c[:, :], 1.0 / T, None, ALU.mult).then_inc(u_ready, 1)
            dve.wait_ge(ew_ready, 1)

            def moments(k, s, p, src):
                for j in range(SUBS):
                    last = dve.bn_stats(stats[k][p][:, j, :], src[:, j, :])
                last.then_inc(stats_ready[k], 1)

            def normalise(k, s, p, out, src):
                dve.wait_ge(rstd_ready[k], s + 1)
                for j in range(SUBS):
                    last = dve.tensor_scalar(out[:, j, :], src[:, j, :], mean[k][p][:, j:j + 1],
                                             rstd[k][p][:, j:j + 1], ALU.subtract, ALU.mult)
                return last

            def moments_x(s, p):
                if inside(s, SEQS):
                    dve.wait_ge(x_loaded[p], landed(s, p))
                    moments(LN_X, s, p, x_in[p])

            def normalise_x(s, p):
                if inside(s, SEQS):
                    wait(dve, turned, s)
                    normalise(LN_X, s, p, xn, x_in[p]).then_inc(xn_ready, 1)

            def low(s):
                if inside(s, SEQS):
                    dve.wait_ge(zhi_ready, s + 1)
                    dve.tensor_tensor(z_lo[:, :, :], turn_ps[:, :, :], z_hi[:, :, :].bitcast(F32),
                                      ALU.subtract).then_inc(zlo_ready, 1)

            def scans(s, c):
                if not inside(s, SEQS):
                    return
                dve.wait_ge(exps_ready, 6 * s + 3 * c + 2)
                dve.tensor_tensor(ekv[c][:, :], ek[c][:, :], v_ps[:, :], ALU.mult).then_inc(ekv_ready, 1)
                dve.tensor_tensor(num[c][:, :], eku[c][:, :], v_ps[:, :], ALU.mult).then_inc(v_used, 1)
                wait(dve, bd_ready, 2 * s + c - 1)
                dve.tensor_tensor_scan(b_sum[c][:, 1:T + 1], ew[:, c:c + 1].to_broadcast([P, T]), ek[c][:, :],
                                       0.0, ALU.mult, ALU.add)
                dve.wait_ge(ekv_ready, 2 * s + c + 1)
                dve.tensor_tensor_scan(a_sum[c][:, 1:T + 1], ew[:, c:c + 1].to_broadcast([P, T]), ekv[c][:, :],
                                       0.0, ALU.mult, ALU.add).then_inc(scans_ready, 1)

            def denominator(s, c):
                if not inside(s, SEQS):
                    return
                dve.wait_ge(exps_ready, 6 * s + 3 * c + 3)
                dve.wait_ge(bd_ready, 2 * s + c + 1)
                dve.scalar_tensor_tensor(out=den[c][:, :], in0=er[c][:, :], scalar=1.0, in1=den[c][:, :],
                                         op0=ALU.add, op1=ALU.mult).then_inc(den_ready, 1)

            def invert(s, c, at):
                if not inside(s, SEQS):
                    return
                dve.wait_ge(den_ready, 2 * s + c + 1)
                dve.reciprocal(den[c][:, at], den[c][:, at]).then_inc(rec_ready, 1)

            def gate(s, c, n):
                if not inside(s, SEQS):
                    return
                dve.wait_ge(rec_ready, 3 * s + n)
                wait(dve, glo_ready, 2 * s + c - 1)
                dve.tensor_tensor(g[c][:, :], num[c][:, :], den[c][:, :], ALU.mult).then_inc(g_ready, 1)

            def moments_o(s, p):
                if inside(s, SEQS):
                    dve.wait_ge(o_done, s + 1)
                    moments(LN_O, s, p, o_ps)

            def normalise_o(s, p):
                if inside(s, SEQS):
                    wait(dve, x1_ready, s)
                    normalise(LN_O, s, p, on, o_ps).then_inc(on_ready, 1)

            def moments_x1(s, p):
                if inside(s, SEQS):
                    dve.wait_ge(x1_ready, s + 1)
                    moments(LN_X1, s, p, x1[p])

            def f_low(s, p, c):
                if inside(s, SEQS):
                    dve.wait_ge(fhi_ready, 2 * s + c + 1)
                    dve.tensor_tensor(f_lo[p][:, c, :], shared_ps[:, :], f_hi[p][:, c, :].bitcast(F32),
                                      ALU.subtract).then_inc(flo_ready, 1)

            def product(s, q):
                if not inside(s, SEQS):
                    return
                dve.wait_ge(silu_ready, s * Q + q + 1)
                wait(dve, hlo_ready, (s - 1) * Q + q + 1)
                dve.scalar_tensor_tensor(out=h[q][:, :], in0=h3_ps[:, :], scalar=bias[:, 1, q:q + 1],
                                         in1=act_h[q % 2][:, :], op0=ALU.add, op1=ALU.mult).then_inc(h_ready, 1)

            def by_rows(v, n):
                return v[:, None, :].to_broadcast([P, SUBS, n])

            def rank_experts(s):
                if not inside(s, SEQS):
                    return
                tiles = bass.ds(s * SUBS, SUBS)

                def then(ins, n):
                    ins.then_inc(ranking, 1)
                    dve.wait_ge(ranking, s * RANK_STEPS + n)

                dve.wait_ge(logits_done, s + 1)
                dve.tensor_tensor(lg[:, :, :], logits_ps, by_rows(gate_bias, E), ALU.add).then_inc(logits_read, 1)
                dve.wait_ge(logits_read, s + 1)
                then(dve.tensor_tensor(as_high[:, :, :, :], lg[:, :, None, :].to_broadcast([P, SUBS, E, E]),
                                       lg[:, :, :, None].to_broadcast([P, SUBS, E, E]), ALU.is_ge), 1)
                then(dve.tensor_tensor(as_high[:, :, :, :], as_high[:, :, :, :],
                                       earlier_s[:, :, :, :].to_broadcast([P, SUBS, E, E]), ALU.mult), 2)
                dve.tensor_reduce(before_it[:, :, :], as_high[:, :, :, :], mybir.AxisListType.X, ALU.add)
                then(dve.tensor_reduce(after_it[:, :, :], as_high[:, :, :, :].rearrange("p j a b -> p j b a"),
                                       mybir.AxisListType.X, ALU.add), 3)
                then(dve.tensor_tensor(before_it[:, :, :], before_it[:, :, :], after_it[:, :, :], ALU.subtract), 4)
                then(dve.tensor_tensor(rank_now[:, :, :], before_it[:, :, :], by_rows(start_s, E), ALU.add), 5)
                dve.tensor_scalar(mask[:, :, :], rank_now[:, :, :], 2.0, None, ALU.is_lt).then_inc(mask_ready, 1)
                dve.tensor_copy(rank[:, tiles, :], rank_now[:, :, :])
                then(dve.tensor_copy(logits[:, tiles, :], lg[:, :, :]), 6)

            def place(s, p):
                if not inside(s, SEQS):
                    return

                def then(ins, n):
                    ins.then_inc(placing, 1)
                    dve.wait_ge(placing, s * PLACE_STEPS + n)

                dve.wait_ge(counted, s + 1)
                then(dve.tensor_tensor(pos[:, :, :], rank_ps, by_rows(count, E), ALU.add), 1)
                dve.tensor_tensor(count[:, :], count[:, :], total_ps, ALU.add).then_inc(counts_read, 1)
                for k in range(2):
                    last = dve.scalar_tensor_tensor(out=picked[k][:, :, :], in0=rank_now[:, :, :], scalar=float(k),
                                                    in1=pos[:, :, :], op0=ALU.is_equal, op1=ALU.mult)
                then(last, 2)
                for k in range(2):
                    last = dve.tensor_reduce(slot[k][:, :], picked[k][:, :, :], mybir.AxisListType.X, ALU.add)
                then(last, 3)
                wait(dve, sent[p], landed(s - 2, p, 2 * SUBS))
                for k in range(2):
                    dve.tensor_copy(at[p][k][:, :], slot[k][:, :])
                dve.tensor_copy(xf[p][:, :, C + 1], slot[0][:, :])
                dve.tensor_copy(xf[p][:, :, C], number_s[:, bass.ds(s * SUBS, SUBS)]).then_inc(at_ready, 1)

            def tile_slots_out():
                done = [0]

                def then(ins):
                    done[0] += 1
                    ins.then_inc(tiling, 1)
                    dve.wait_ge(tiling, done[0])

                dve.wait_ge(turned, SEQS)
                dve.memset(ends[:, 0:1], 0.0)
                dve.memset(one[:, :], 1.0)
                then(dve.tensor_tensor(tokens_of[:, :], count[:, :], region_s[:, :], ALU.subtract))
                then(dve.tensor_tensor(over[:, :, :], tokens_of[:, :, None].to_broadcast([P, E, LIMITS]),
                                       limits_s[:, None, :].to_broadcast([P, E, LIMITS]), ALU.is_gt))
                then(dve.tensor_reduce(used[:, :], over[:, :, :], mybir.AxisListType.X, ALU.add))
                then(dve.tensor_scalar(used[:, :], used[:, :], float(TILE), None, ALU.mult))
                then(dve.tensor_tensor_scan(ends[:, 1:E + 1], one[:, :].to_broadcast([P, E]), used[:, :], 0.0, ALU.mult,
                                            ALU.add))
                slots_at = tile_no[:, :, None].to_broadcast([P, TILES, E])
                dve.tensor_tensor(began[:, :, :], slots_at, ends[:, None, 0:E].to_broadcast([P, TILES, E]), ALU.is_ge)
                then(dve.tensor_tensor(ended[:, :, :], slots_at, ends[:, None, 1:E + 1].to_broadcast([P, TILES, E]),
                                       ALU.is_ge))
                then(dve.tensor_tensor(at_tile[:, :, :], began[:, :, :], ended[:, :, :], ALU.subtract))
                then(dve.tensor_tensor(shift[:, :], region_s[:, :], ends[:, 0:E], ALU.subtract))
                then(dve.tensor_tensor(began[:, :, :], shift[:, None, :].to_broadcast([P, TILES, E]),
                                       tile_no[:, :, None].to_broadcast([P, TILES, E]), ALU.add))
                then(dve.tensor_tensor(at_tile[:, :, :], at_tile[:, :, :], began[:, :, :], ALU.mult))
                dve.tensor_reduce(number[:, :], at_tile[:, :, :], mybir.AxisListType.X, ALU.add)
                then(dve.tensor_scalar(unused[:, :], ended[:, :, E - 1], float(E * REGION), None, ALU.mult))
                then(dve.tensor_tensor(tile_of["start"][:, :], number[:, :], unused[:, :], ALU.add))
                then(dve.tensor_reduce(number[:, :], ended[:, :, :], mybir.AxisListType.X, ALU.add))
                dve.tensor_scalar(tile_of["expert"][:, :], number[0:1, :], float(E - 1), None, ALU.min)
                dve.tensor_copy(tile_of["slot"][:, :], tile_of["start"][0:1, :])

            def body(i, par):
                product(i - 3, 3)
                moments_x(i + 1, 1 - par)
                f_low(i - 2, par, 1)
                scans(i, 0)
                rank_experts(i - 2)
                moments_o(i - 1, 1 - par)
                denominator(i, 0)
                invert(i, 0, slice(0, T))
                gate(i, 0, 1)
                place(i - 2, par)
                normalise_o(i - 1, 1 - par)
                product(i - 2, 0)
                scans(i, 1)
                normalise_x(i + 1, 1 - par)
                moments_x1(i - 1, 1 - par)
                product(i - 2, 1)
                denominator(i, 1)
                invert(i, 1, slice(0, T // 2))
                product(i - 2, 2)
                low(i + 1)
                invert(i, 1, slice(T // 2, T))
                gate(i, 1, 3)
                f_low(i - 1, 1 - par, 0)
                if isinstance(i, int) and i == SEQS + 1:
                    dve.wait_ge(counts_read, SEQS)
                    dve.tensor_copy(free_slot[:, :], count[0:1, :]).then_inc(free_ready, 1)

            steps(dve, body, -1, *LOOP, END)
            tile_slots_out()

        @block.gpsimd
        def _(pool):
            scale_constants(pool, scale_c, C, consts_done)
            pool.wait_ge(zs_cleared, 1)
            pool.memset(scratch[:, :], 0.0).then_inc(scratch_ready, 1)
            pool.memset(warm[:, :], 0.0).then_inc(scratch_ready, 1)
            pool.memset(nobody[:, :, 0:C], 0.0).then_inc(nobody_ready, 1)
            pool.memset(nobody[:, :, C:ROW], NOBODY).then_inc(nobody_ready, 1)
            pool.wait_ge(scratch_ready, 1)

            def inverse_std(k, s, p):
                if not inside(s, SEQS):
                    return
                pool.wait_ge(stats_ready[k], s + 1)
                if k == LN_X1:
                    wait(pool, xf_ready, s - 1)
                layernorm_scales(pool, scale_c, stats[k][p], sums[k][p], half_diff[k][p], var[k][p], mean[k][p],
                                 rstd[k][p], scales_ordered[k], s, rstd_ready[k], negative=(k == LN_X1))
                if k == LN_X1:
                    pool.wait_ge(rstd_ready[k], s + 1)
                    pool.tensor_tensor(offset[p][:, :], mean[k][p][:, :], rstd[k][p][:, :], ALU.mult)\
                        .then_inc(offset_ready, 1)

            def running_sums(s, c):
                if not inside(s, SEQS):
                    return
                pool.wait_ge(scans_ready, 2 * s + c + 1)
                pool.tensor_tensor(num[c][:, :], num[c][:, :], a_sum[c][:, 0:T], ALU.add)
                wait(pool, g_ready, 2 * s + c - 1)
                pool.tensor_tensor(den[c][:, :], b_sum[c][:, 0:T], eku[c][:, :], ALU.add).then_inc(bd_ready, 1)

            def g_low(s, c):
                if not inside(s, SEQS):
                    return
                pool.wait_ge(ghi_ready, 2 * s + c + 1)
                pool.tensor_tensor(g_lo[:, c, :], g[c][:, :], g_hi[:, c, :].bitcast(F32), ALU.subtract)\
                    .then_inc(glo_ready, 1)

            def add_x(s, p):
                if not inside(s, SEQS):
                    return
                pool.wait_ge(on_ready, s + 1)
                pool.wait_ge(res_loaded[p], landed(s, p))
                wait(pool, x1_stored[p], landed(s - 2, p))
                wait(pool, xf_ready, s - 1)
                pool.tensor_tensor(x1[p][:, :, :], on[:, :, :], x_res[p][:, :, :], ALU.add).then_inc(x1_ready, 1)

            def h_low(s, q):
                if not inside(s, SEQS):
                    return
                pool.wait_ge(hhi_ready, s * Q + q + 1)
                pool.tensor_tensor(h_lo[:, q, :], h[q][:, :], h_hi[:, q, :].bitcast(F32), ALU.subtract)\
                    .then_inc(hlo_ready, 1)

            def send(s, p, k, tiles):
                if not inside(s, SEQS):
                    return
                for j in tiles:
                    pool.indirect_dma_start(out=slots_x[:, :],
                                            out_offset=bass.IndirectOffsetOnAxis(ap=at[p][k][:, j:j + 1], axis=0),
                                            in_=xf[p][:, j, :], in_offset=None).then_inc(sent[p], 16)

            def body(i, par):
                h_low(i - 3, 3)
                send(i - 3, 1 - par, 1, (0, 1, 2, 3))
                running_sums(i, 0)
                inverse_std(LN_O, i - 1, 1 - par)
                inverse_std(LN_X, i + 1, 1 - par)
                add_x(i - 1, 1 - par)
                if inside(i - 2, SEQS):
                    hold(pool, scratch, held, i - 2, (at_ready, i - 1))
                send(i - 2, par, 0, (0, 1))
                running_sums(i, 1)
                inverse_std(LN_X1, i - 1, 1 - par)
                h_low(i - 2, 0)
                h_low(i - 2, 1)
                g_low(i, 0)
                send(i - 2, par, 0, (2, 3))
                h_low(i - 2, 2)
                g_low(i, 1)

            steps(pool, body, -1, *LOOP, END)


def expert_tiles(nc, tiles, parts, slots, dst, weights, biases, ident, own_rows, tile_of, logits, rank, gates,
                 load_ahead):
    C = dst.shape[1]
    ROW = slots.shape[1]
    CC, SUBS = C // P, 4
    T = SUBS * P
    INNER = parts * P
    W13, W2 = 2 * CC * INNER, parts * C
    E = biases.shape[0]

    with ExitStack() as ctx:
        def sb(label, shape, dt=F32):
            return ctx.enter_context(nc.sbuf_tensor(f"e_{label}", shape, dt))

        def psum(label, shape):
            return ctx.enter_context(nc.psum_tensor(f"e_{label}", shape, F32))

        def sem(label):
            return ctx.enter_context(nc.semaphore(f"e_{label}"))

        eye = sb("eye", [P, P])
        w_raw = [sb(f"w_raw{p}", [P, W13 + W2]) for p in range(2)]
        w13_hi = [sb(f"w13_hi{p}", [P, 2, CC, INNER], F32R) for p in range(2)]
        w13_lo = [sb(f"w13_lo{p}", [P, 2, CC, INNER], F32R) for p in range(2)]
        w2_hi = [sb(f"w2_hi{p}", [P, parts, C], F32R) for p in range(2)]
        w2_lo = [sb(f"w2_lo{p}", [P, parts, C], F32R) for p in range(2)]
        bias = [sb(f"bias{p}", [P, 2, parts]) for p in range(2)]
        x_in = [sb(f"x_in{p}", [P, SUBS, ROW]) for p in range(2)]
        z_hi = [sb(f"z_hi{p}", [P, CC, T], F32R) for p in range(2)]
        z_lo = [sb(f"z_lo{p}", [P, CC, T], F32R) for p in range(2)]
        act_h = [sb(f"act_h{p}", [P, T]) for p in range(2)]
        h = [sb(f"h{p}", [P, T]) for p in range(2)]
        h_hi = [sb(f"h_hi{p}", [P, parts, T], F32R) for p in range(2)]
        h_lo = [sb(f"h_lo{p}", [P, parts, T], F32R) for p in range(2)]
        y = [sb(f"y{p}", [P, SUBS, C]) for p in range(2)]
        NT = logits.shape[1]
        top = sb("top", [P, NT])
        prob = sb("prob", [P, NT, E])
        picked = sb("picked", [P, NT, E])
        own_s = sb("own_rows", [P, SUBS])
        start_now = sb("start_now", [P, 1])
        own = sb("own", [P, SUBS])
        second = sb("second", [P, SUBS])
        row_next = [sb(f"row_next{p}", [P, SUBS]) for p in range(2)]
        row_at = [sb(f"row_at{p}", [P, SUBS], mybir.dt.uint32) for p in range(2)]
        scratch = sb("scratch", [P, 2])
        turn_ps = psum("turn_ps", [P, CC, T])
        h1_ps = [psum(f"h1_ps{p}", [P, T]) for p in range(2)]
        h3_ps = [psum(f"h3_ps{p}", [P, T]) for p in range(2)]
        y_ps = psum("y_ps", [P, SUBS, C])

        shifted_ready = sem("shifted_ready")
        exp_ready = sem("exp_ready")
        gates_ordered = sem("gates_ordered")
        consts_in = sem("consts_in")
        w_loaded = [sem(f"w_loaded{p}") for p in range(2)]
        bias_loaded = [sem(f"bias_loaded{p}") for p in range(2)]
        w13_high = sem("w13_high")
        w13_split = sem("w13_split")
        w2_high = sem("w2_high")
        w2_split = sem("w2_split")
        x_loaded = [sem(f"x_loaded{p}") for p in range(2)]
        turned = sem("turned")
        zhi_ready = sem("zhi_ready")
        zlo_ready = sem("zlo_ready")
        h13_done = sem("h13_done")
        silu_ready = sem("silu_ready")
        h_ready = sem("h_ready")
        hhi_ready = sem("hhi_ready")
        hlo_ready = sem("hlo_ready")
        y_done = sem("y_done")
        y_read = sem("y_read")
        y_stored = [sem(f"y_stored{p}") for p in range(2)]
        rows_ordered = sem("rows_ordered")
        rows_read = sem("rows_read")
        rows_kept = sem("rows_kept")
        scratch_ready = sem("scratch_ready")
        held = sem("held")
        block = ctx.enter_context(nc.Block())
        LOOP = (4, tiles - tiles % 2 - 2)

        def words(ap):
            return ap.bitcast(F32)

        @block.sync
        def _(sp):
            sp.dma_start(eye[:, :], ident).then_inc(consts_in, 16)
            sp.dma_start(own_s[:, :], own_rows).then_inc(consts_in, 16)

            def body(i, par):
                if isinstance(i, int) and i == 2:
                    load_ahead(sp)
                n = i + 2
                if inside(n, tiles):
                    at = sp.value_load(tile_of["slot"][0:1, bass.ds(n, 1)], min_val=0, max_val=slots.shape[0] - T)
                    wait(sp, turned, n - 1)
                    wait(sp, rows_read, n - 1)
                    sp.dma_start(x_in[par][:, :, :], slots[bass.ds(at, T), :].rearrange("(j p) c -> p j c", p=P))\
                        .then_inc(x_loaded[par], 16)
                    e = sp.value_load(tile_of["expert"][0:1, bass.ds(n, 1)], min_val=0, max_val=E - 1)
                    wait(sp, w2_split, n - 1)
                    sp.dma_start(w_raw[par][:, :], weights[:, bass.ds(e * (W13 + W2), W13 + W2)])\
                        .then_inc(w_loaded[par], 16)
                n = i + 1
                if inside(n, tiles):
                    p = 1 - par
                    e = sp.value_load(tile_of["expert"][0:1, bass.ds(n, 1)], min_val=0, max_val=E - 1)
                    wait(sp, h_ready, (n - 1) * parts)
                    sp.dma_start(bias[p][:, :, :], biases[bass.ds(e, 1), :, :, :]
                                 .rearrange("a p b c -> p (a b) c")).then_inc(bias_loaded[p], 16)

            steps(sp, body, -2, *LOOP, tiles)
            for p in range(2):
                sp.wait_ge(y_stored[p], 16 * SUBS * ((tiles + 1 - p) // 2))

        @block.tensor
        def _(pe):
            pe.wait_ge(consts_in, 32)

            def turn(s, p):
                if not inside(s, tiles):
                    return
                pe.wait_ge(x_loaded[p], landed(s, p))
                wait(pe, zlo_ready, s)
                for c in range(CC):
                    for j in range(SUBS):
                        last = pe.transpose(turn_ps[:, c, j * P:(j + 1) * P],
                                            x_in[p][:, j, c * P:(c + 1) * P], eye[:, :])
                last.then_inc(turned, 1)

            def inner(s, p, q):
                if not inside(s, tiles):
                    return
                if q == 0:
                    pe.wait_ge(zlo_ready, s + 1)
                    pe.wait_ge(w13_split, s + 1)
                wait(pe, silu_ready, s * parts + q - 1)
                wait(pe, h_ready, s * parts + q - 1)
                for which, out in ((0, h1_ps[q % 2]), (1, h3_ps[q % 2])):
                    n = 0
                    for c in range(CC):
                        for a, b in ((w13_hi, z_hi), (w13_hi, z_lo), (w13_lo, z_hi)):
                            last = pe.matmul(out[:, :], a[p][:, which, c, q * P:(q + 1) * P], b[p][:, c, :],
                                             start=(n == 0), stop=(n == 5))
                            n += 1
                last.then_inc(h13_done, 1)

            def outer(s, p):
                if not inside(s, tiles):
                    return
                pe.wait_ge(hlo_ready, (s + 1) * parts)
                wait(pe, y_read, s)
                pe.wait_ge(w2_split, s + 1)
                for j in range(SUBS):
                    n = 0
                    for q in range(parts):
                        for a, b in ((h_hi, w2_hi), (h_lo, w2_hi), (h_hi, w2_lo)):
                            last = pe.matmul(y_ps[:, j, :], a[p][:, q, j * P:(j + 1) * P], b[p][:, q, :],
                                             start=(n == 0), stop=(n == 3 * parts - 1))
                            n += 1
                last.then_inc(y_done, 1)

            def body(i, par):
                inner(i, par, 0)
                turn(i + 1, 1 - par)
                outer(i - 1, 1 - par)
                for q in range(1, parts):
                    inner(i, par, q)

            steps(pe, body, -1, *LOOP, tiles + 1)

        def flat(w):
            return w.rearrange("p a b n -> p (a b n)") if len(w.shape) == 4 else w.rearrange("p a n -> p (a n)")

        @block.scalar
        def _(act):
            def high_w13(s, p):
                if not inside(s, tiles):
                    return
                act.wait_ge(w_loaded[p], landed(s, p))
                wait(act, h13_done, (s - 1) * parts)
                act.activation(flat(w13_hi[p][:, :, :, :]), w_raw[p][:, 0:W13], ACT.Copy).then_inc(w13_high, 1)

            def high_w2(s, p):
                if not inside(s, tiles):
                    return
                wait(act, y_done, s - 1)
                act.activation(flat(w2_hi[p][:, :, :]), w_raw[p][:, W13:W13 + W2], ACT.Copy).then_inc(w2_high, 1)

            def high(s, p):
                if not inside(s, tiles):
                    return
                act.wait_ge(turned, s + 1)
                wait(act, h13_done, (s - 1) * parts)
                act.activation(z_hi[p][:, :, :], turn_ps[:, :, :], ACT.Copy).then_inc(zhi_ready, 1)

            def silu(s, p, q):
                if not inside(s, tiles):
                    return
                act.wait_ge(h13_done, s * parts + q + 1)
                act.wait_ge(bias_loaded[p], landed(s, p))
                wait(act, h_ready, s * parts + q - 1)
                act.activation(act_h[q % 2][:, :], h1_ps[q % 2][:, :], ACT.Silu, bias=bias[p][:, 0, q:q + 1])\
                    .then_inc(silu_ready, 1)

            def h_high(s, p, q):
                if not inside(s, tiles):
                    return
                act.wait_ge(h_ready, s * parts + q + 1)
                wait(act, y_done, s - 1)
                act.activation(h_hi[p][:, q, :], h[q % 2][:, :], ACT.Copy).then_inc(hhi_ready, 1)

            def body(i, par):
                if isinstance(i, int) and i == 1:
                    act.wait_ge(shifted_ready, 2)
                    act.activation(prob[:, :, :], prob[:, :, :], ACT.Exp).then_inc(exp_ready, 1)
                high_w13(i + 1, 1 - par)
                silu(i, par, 0)
                high(i + 1, 1 - par)
                for q in range(1, parts):
                    h_high(i, par, q - 1)
                    if q == 1:
                        high_w2(i + 1, 1 - par)
                    silu(i, par, q)
                h_high(i, par, parts - 1)

            steps(act, body, -1, *LOOP, tiles)

        @block.vector
        def _(dve):
            dve.wait_ge(consts_in, 32)

            def low(s, p):
                if inside(s, tiles):
                    dve.wait_ge(zhi_ready, s + 1)
                    dve.tensor_tensor(z_lo[p][:, :, :], turn_ps[:, :, :], words(z_hi[p][:, :, :]), ALU.subtract)\
                        .then_inc(zlo_ready, 1)

            def low_w13(s, p):
                if not inside(s, tiles):
                    return
                dve.wait_ge(w13_high, s + 1)
                dve.tensor_tensor(flat(w13_lo[p][:, :, :, :]), w_raw[p][:, 0:W13],
                                  words(flat(w13_hi[p][:, :, :, :])), ALU.subtract).then_inc(w13_split, 1)

            def low_w2(s, p):
                if not inside(s, tiles):
                    return
                dve.wait_ge(w2_high, s + 1)
                dve.tensor_tensor(flat(w2_lo[p][:, :, :]), w_raw[p][:, W13:W13 + W2],
                                  words(flat(w2_hi[p][:, :, :])), ALU.subtract).then_inc(w2_split, 1)

            def product(s, p, q):
                if not inside(s, tiles):
                    return
                dve.wait_ge(silu_ready, s * parts + q + 1)
                wait(dve, hlo_ready, s * parts + q - 1)
                dve.scalar_tensor_tensor(out=h[q % 2][:, :], in0=h3_ps[q % 2][:, :], scalar=bias[p][:, 1, q:q + 1],
                                         in1=act_h[q % 2][:, :], op0=ALU.add, op1=ALU.mult).then_inc(h_ready, 1)

            def read_y(s, p):
                if inside(s, tiles):
                    dve.wait_ge(y_done, s + 1)
                    wait(dve, y_stored[p], landed(s - 2, p, SUBS))
                    dve.tensor_copy(y[p][:, :, :], y_ps[:, :, :]).then_inc(y_read, 1)

            def make_gates():
                done = [0]

                def then(ins):
                    done[0] += 1
                    ins.then_inc(gates_ordered, 1)
                    dve.wait_ge(gates_ordered, done[0])

                wide = top[:, :, None].to_broadcast([P, NT, E])
                dve.wait_ge(exp_ready, 1)
                then(dve.tensor_reduce(top[:, :], prob[:, :, :], mybir.AxisListType.X, ALU.add))
                then(dve.reciprocal(top[:, :], top[:, :]))
                then(dve.tensor_tensor(prob[:, :, :], prob[:, :, :], wide, ALU.mult))
                dve.memset(gates["all"][:, :, E:E + 1], 1.0)
                dve.scalar_tensor_tensor(out=gates["all"][:, :, 0:E], in0=rank[:, :, :], scalar=2.0,
                                         in1=prob[:, :, :], op0=ALU.is_lt, op1=ALU.mult)
                for k in range(2):
                    then(dve.scalar_tensor_tensor(out=picked[:, :, :], in0=rank[:, :, :], scalar=float(k),
                                                  in1=prob[:, :, :], op0=ALU.is_equal, op1=ALU.mult))
                    then(dve.tensor_reduce(gates[k][:, :], picked[:, :, :], mybir.AxisListType.X, ALU.add))

            def shift_logits():
                dve.tensor_reduce(top[:, :], logits[:, :, :], mybir.AxisListType.X, ALU.max).then_inc(shifted_ready, 1)
                dve.wait_ge(shifted_ready, 1)
                dve.tensor_tensor(prob[:, :, :], logits[:, :, :], top[:, :, None].to_broadcast([P, NT, E]),
                                  ALU.subtract).then_inc(shifted_ready, 1)

            def read_rows(s, p):
                if not inside(s, tiles):
                    return

                def then(ins, n):
                    ins.then_inc(rows_ordered, 1)
                    dve.wait_ge(rows_ordered, s * 3 + n)

                then(dve.tensor_copy(start_now[:, :], tile_of["start"][:, bass.ds(s, 1)]), 1)
                then(dve.tensor_scalar(own[:, :], own_s[:, :], start_now[:, 0:1], None, ALU.add), 2)
                dve.wait_ge(x_loaded[p], landed(s, p))
                then(dve.tensor_tensor(second[:, :], own[:, :], x_in[p][:, :, C + 1], ALU.not_equal), 3)
                wait(dve, rows_kept, s - 1)
                dve.tensor_tensor(row_next[p][:, :], second[:, :], x_in[p][:, :, C], ALU.add).then_inc(rows_read, 1)

            def keep_rows(s, p):
                if inside(s, tiles):
                    dve.wait_ge(rows_read, s + 1)
                    wait(dve, y_stored[p], landed(s - 2, p, SUBS))
                    dve.tensor_copy(row_at[p][:, :], row_next[p][:, :]).then_inc(rows_kept, 1)

            def body(i, par):
                product(i, par, 0)
                read_rows(i + 1, 1 - par)
                low_w13(i + 1, 1 - par)
                low(i + 1, 1 - par)
                read_y(i - 1, 1 - par)
                low_w2(i + 1, 1 - par)
                for q in range(1, parts):
                    product(i, par, q)
                keep_rows(i, par)
                if isinstance(i, int) and i == 0:
                    shift_logits()
                if isinstance(i, int) and i == 2:
                    make_gates()

            steps(dve, body, -1, *LOOP, tiles + 1)

        @block.gpsimd
        def _(pool):
            def h_low(s, p, q):
                if not inside(s, tiles):
                    return
                pool.wait_ge(hhi_ready, s * parts + q + 1)
                pool.tensor_tensor(h_lo[p][:, q, :], h[q % 2][:, :], words(h_hi[p][:, q, :]), ALU.subtract)\
                    .then_inc(hlo_ready, 1)

            def send(s, p):
                if not inside(s, tiles):
                    return
                hold(pool, scratch, held, s, (y_read, s + 1), (rows_kept, s + 1))
                for j in range(SUBS):
                    pool.indirect_dma_start(out=dst[:, :], out_offset=bass.IndirectOffsetOnAxis(ap=row_at[p][:, j:j + 1], axis=0),
                                            in_=y[p][:, j, :], in_offset=None, bounds_check=dst.shape[0] - 1,
                                            oob_is_err=False).then_inc(y_stored[p], 16)

            pool.memset(scratch[:, :], 0.0).then_inc(scratch_ready, 1)
            pool.wait_ge(scratch_ready, 1)

            def body(i, par):
                for q in range(parts):
                    h_low(i, par, q)
                send(i - 1, 1 - par)

            steps(pool, body, 0, *LOOP, tiles + 1)


def combine(nc, x1_dram, expert_y, shared, gates, ahead, out):
    C = x1_dram.shape[1]
    SUBS = 4
    T = SUBS * P
    tiles = x1_dram.shape[0] // T
    G = gates["all"].shape[2]
    with ExitStack() as ctx:
        def sb(label, shape, dt=F32):
            return ctx.enter_context(nc.sbuf_tensor(f"c_{label}", shape, dt))

        def sem(label):
            return ctx.enter_context(nc.semaphore(f"c_{label}"))

        eye, b_out, ys, x1 = (ahead[n] for n in ("eye", "b_out", "ys", "x1"))
        scale_c = sb("scale_c", [P, 4, SUBS])
        ye = [sb(f"ye{p}", [P, SUBS, 2, C]) for p in range(2)]
        gt = [sb(f"gt{p}", [G, T]) for p in range(2)]
        gate_now = [sb(f"gate_now{p}", [P, 2, SUBS]) for p in range(2)]
        acc = [sb(f"acc{p}", [P, SUBS, C]) for p in range(2)]
        offset = [sb(f"offset{p}", [P, SUBS]) for p in range(2)]
        normal = [sb(f"normal{p}", [P, SUBS, C]) for p in range(2)]
        stats = [sb(f"stats{p}", [P, SUBS, 6]) for p in range(2)]
        sums = [sb(f"sums{p}", [P, SUBS, 2]) for p in range(2)]
        half_diff = [sb(f"half_diff{p}", [P, SUBS]) for p in range(2)]
        var = [sb(f"var{p}", [P, SUBS]) for p in range(2)]
        mean = [sb(f"mean{p}", [P, SUBS]) for p in range(2)]
        rstd = [sb(f"rstd{p}", [P, SUBS]) for p in range(2)]
        res = [sb(f"res{p}", [P, SUBS, C]) for p in range(2)]
        gt_ps = [ctx.enter_context(nc.psum_tensor(f"c_gt_ps{p}", [P, T], F32)) for p in range(2)]
        b_ps = [ctx.enter_context(nc.psum_tensor(f"c_b_ps{p}", [P, SUBS, C], F32)) for p in range(2)]

        consts_in, ys_loaded, x1_loaded = (ahead[n] for n in ("consts_in", "ys_loaded", "x1_loaded"))
        scale_c_ready = sem("scale_c_ready")
        at_ready = sem("at_ready")
        ye_loaded = [sem(f"ye_loaded{p}") for p in range(2)]
        gt_turned = sem("gt_turned")
        gt_ready = sem("gt_ready")
        b_done = sem("b_done")
        sum_b = sem("sum_b")
        sum_0 = sem("sum_0")
        sum_1 = sem("sum_1")
        stats_ready = sem("stats_ready")
        scales_ordered = sem("scales_ordered")
        rstd_ready = sem("rstd_ready")
        offset_ready = sem("offset_ready")
        normed = sem("normed")
        res_ready = sem("res_ready")
        stored = [sem(f"stored{p}") for p in range(2)]
        block = ctx.enter_context(nc.Block())
        LOOP = (4, tiles - 2)

        def rows(dram, i):
            return dram[bass.ds(i * T, T), :].rearrange("(j p) c -> p j c", p=P)

        @block.sync
        def _(sp):
            def body(i, par):
                if inside(i, tiles):
                    wait(sp, sum_1, i - 1)
                    if not (isinstance(i, int) and i < 2):
                        sp.dma_start(ys[par][:, :, :], rows(shared, i)).then_inc(ys_loaded[par], 16)
                    sp.dma_start(ye[par][:, :, :, :], expert_y[bass.ds(i * (2 * T), 2 * T), :]
                                 .rearrange("(j p k) c -> p j k c", p=P, k=2)).then_inc(ye_loaded[par], 16)

            steps(sp, body, 0, *LOOP, tiles)
            for p in range(2):
                sp.wait_ge(stored[p], 16 * (tiles // 2))

        @block.tensor
        def _(pe):
            pe.wait_ge(consts_in, 32)

            def turn(s, p):
                if not inside(s, tiles):
                    return
                pe.wait_ge(at_ready, s + 1)
                wait(pe, gt_ready, s - 1)
                for j in range(SUBS):
                    last = pe.transpose(gt_ps[p][0:G, j * P:(j + 1) * P], gates["now"][p][:, j, :], eye[:, :])
                last.then_inc(gt_turned, 1)

            def bias(s, p):
                if not inside(s, tiles):
                    return
                pe.wait_ge(gt_ready, s + 1)
                wait(pe, sum_b, s - 1)
                for j in range(SUBS):
                    last = pe.matmul(b_ps[p][:, j, :], gt[p][:, j * P:(j + 1) * P], b_out[:, :],
                                     start=True, stop=True)
                last.then_inc(b_done, 1)

            def body(i, par):
                turn(i, par)
                bias(i, par)

            steps(pe, body, 0, *LOOP, tiles)

        @block.scalar
        def _(act):
            def body(i, par):
                n = i + 1
                if inside(n, tiles):
                    act.wait_ge(gt_turned, n + 1)
                    wait(act, b_done, n - 1)
                    act.activation(gt[1 - par][:, :], gt_ps[1 - par][0:G, :], ACT.Copy).then_inc(gt_ready, 1)
                if inside(i, tiles) and not (isinstance(i, int) and i < 2):
                    wait(act, res_ready, i - 1)
                    act.dma_start(x1[par][:, :, :], rows(x1_dram, i)).then_inc(x1_loaded[par], 16)
                s = i - 1
                if inside(s, tiles):
                    act.wait_ge(offset_ready, s + 1)
                    wait(act, res_ready, s - 1)
                    for j in range(SUBS):
                        last = act.activation(normal[1 - par][:, j, :], acc[1 - par][:, j, :], ACT.Identity,
                                              bias=offset[1 - par][:, j:j + 1], scale=rstd[1 - par][:, j:j + 1])
                    last.then_inc(normed, 1)
                s = i - 2
                if inside(s, tiles):
                    act.wait_ge(res_ready, s + 1)
                    act.dma_start(rows(out, s), res[par][:, :, :]).then_inc(stored[par], 16)

            steps(act, body, -1, *LOOP, tiles + 2)

        @block.vector
        def _(dve):
            def fetch(s, p):
                if not inside(s, tiles):
                    return
                wait(dve, gt_turned, s - 1)
                for k in range(2):
                    dve.tensor_copy(gate_now[p][:, k, :], gates[k][:, bass.ds(s * SUBS, SUBS)])
                dve.tensor_copy(gates["now"][p][:, :, :], gates["all"][:, bass.ds(s * SUBS, SUBS), :])\
                    .then_inc(at_ready, 1)

            def add(s, p):
                if not inside(s, tiles):
                    return
                dve.wait_ge(b_done, s + 1)
                dve.wait_ge(ys_loaded[p], landed(s, p))
                wait(dve, normed, s - 1)
                dve.tensor_tensor(acc[p][:, :, :], b_ps[p][:, :, :], ys[p][:, :, :], ALU.add).then_inc(sum_b, 1)
                dve.wait_ge(sum_b, s + 1)
                dve.wait_ge(ye_loaded[p], landed(s, p))
                dve.wait_ge(at_ready, s + 1)
                for k, done in ((0, sum_0), (1, sum_1)):
                    for j in range(SUBS):
                        last = dve.scalar_tensor_tensor(out=acc[p][:, j, :], in0=ye[p][:, j, k, :],
                                                        scalar=gate_now[p][:, k, j:j + 1], in1=acc[p][:, j, :],
                                                        op0=ALU.mult, op1=ALU.add)
                    last.then_inc(done, 1)
                    dve.wait_ge(done, s + 1)
                for j in range(SUBS):
                    last = dve.bn_stats(stats[p][:, j, :], acc[p][:, j, :])
                last.then_inc(stats_ready, 1)

            def body(i, par):
                fetch(i + 1, 1 - par)
                add(i, par)

            steps(dve, body, -1, *LOOP, tiles)

        @block.gpsimd
        def _(pool):
            scale_constants(pool, scale_c, C, scale_c_ready)

            def inverse_std(s, p):
                if not inside(s, tiles):
                    return
                pool.wait_ge(stats_ready, s + 1)
                layernorm_scales(pool, scale_c, stats[p], sums[p], half_diff[p], var[p], mean[p], rstd[p],
                                 scales_ordered, s, rstd_ready, negative=True)
                pool.wait_ge(rstd_ready, s + 1)
                wait(pool, normed, s - 1)
                pool.tensor_tensor(offset[p][:, :], mean[p][:, :], rstd[p][:, :], ALU.mult).then_inc(offset_ready, 1)

            def add_x1(s, p):
                if not inside(s, tiles):
                    return
                pool.wait_ge(normed, s + 1)
                wait(pool, stored[p], landed(s - 2, p))
                pool.wait_ge(x1_loaded[p], landed(s, p))
                pool.tensor_tensor(res[p][:, :, :], normal[p][:, :, :], x1[p][:, :, :], ALU.add).then_inc(res_ready, 1)

            def body(i, par):
                inverse_std(i, par)
                add_x1(i - 1, 1 - par)

            steps(pool, body, 0, *LOOP, tiles + 1)


SLOT_TILE = 512


def sandwich(nc, x, attn_w, mix, decay, first, ident, tri, ones, limits, rank_start, earlier, region_start,
             tile_slots, own_rows, ffn_w, expert_biases, shared_biases, gate_w, gate_b, out_biases, numbers, out):
    B, T, C = x.shape
    TOKENS = B * T
    E = gate_w.shape[2]
    EXPERTS_W = 6 * C * (C // P) // 2
    TILES = (2 * TOKENS + E * (SLOT_TILE - 1)) // SLOT_TILE
    assert TILES == tile_slots.shape[1]
    COLS = ffn_w.shape[1]

    x1_dram = nc.dram_tensor("x1_dram", (B, T, C), F32, kind="Internal").ap()
    slots_x = nc.dram_tensor("slots_x", ((E + 1) * (TOKENS + SLOT_TILE), C + 2), F32, kind="Internal").ap()
    expert_y = nc.dram_tensor("expert_y", (2 * TOKENS, C), F32, kind="Internal").ap()
    shared_y = nc.dram_tensor("shared_y", (TOKENS, C), F32, kind="Internal").ap()
    tokens = "b t c -> (b t) c"

    with ExitStack() as ctx:
        def sb(label, shape, dt=F32):
            return ctx.enter_context(nc.sbuf_tensor(label, shape, dt))

        NT = TOKENS // P
        logits = sb("logits", [P, NT, E])
        gates = {0: sb("gate0", [P, NT]), 1: sb("gate1", [P, NT]), "all": sb("gates_all", [P, NT, E + 1]),
                 "now": [sb(f"gates_now{p}", [P, 4, E + 1]) for p in range(2)]}
        rank = sb("rank", [P, NT, E])
        count = sb("count", [P, E])
        tile_of = {"expert": sb("tile_expert", [1, TILES], mybir.dt.int32),
                   "slot": sb("tile_slot", [1, TILES], mybir.dt.int32), "start": sb("tile_start", [P, TILES])}
        shared_at = E * EXPERTS_W
        first_pass(nc, x, attn_w, mix, decay, first, ident, tri, ones, ffn_w[:, shared_at:COLS], shared_biases,
                   gate_w, gate_b, rank_start, earlier, region_start, numbers, limits, tile_slots, logits, rank,
                   count, tile_of, x1_dram, shared_y, slots_x)
        ahead = {"eye": sb("c_eye", [P, P]), "b_out": sb("c_b_out", [E + 1, C]),
                 "ys": [sb(f"c_ys{p}", [P, SLOT_TILE // P, C]) for p in range(2)],
                 "x1": [sb(f"c_x1{p}", [P, SLOT_TILE // P, C]) for p in range(2)]}
        ahead["consts_in"] = ctx.enter_context(nc.semaphore("c_consts_in"))
        for name in ("ys_loaded", "x1_loaded"):
            ahead[name] = [ctx.enter_context(nc.semaphore(f"c_{name}{p}")) for p in range(2)]
        x1_rows = x1_dram.rearrange(tokens)

        def load_ahead(sp):
            sp.dma_start(ahead["eye"][:, :], ident).then_inc(ahead["consts_in"], 16)
            sp.dma_start(ahead["b_out"][:, :], out_biases).then_inc(ahead["consts_in"], 16)
            for p in range(2):
                for to, rows, done in ((ahead["ys"], shared_y, ahead["ys_loaded"]),
                                       (ahead["x1"], x1_rows, ahead["x1_loaded"])):
                    sp.dma_start(to[p][:, :, :], rows[p * SLOT_TILE:(p + 1) * SLOT_TILE, :]
                                 .rearrange("(j p) c -> p j c", p=P)).then_inc(done[p], 16)

        expert_tiles(nc, TILES, 2, slots_x, expert_y, ffn_w[:, 0:shared_at], expert_biases, ident, own_rows, tile_of,
                     logits, rank, gates, load_ahead)
        combine(nc, x1_rows, expert_y, shared_y, gates, ahead, out.rearrange(tokens))


def kernel(**inputs):
    import numpy as _np
    import concourse.bacc as _bacc
    from concourse import mybir as _mybir
    from concourse.bass_utils import run_bass_kernel_spmd as _run

    def get(name):
        return _np.asarray(inputs["L0_" + name])

    def chunked(w):
        n, m = w.shape
        return w.T.reshape(m // 128, 128, n).transpose(1, 0, 2)

    def columns(v):
        return v.reshape(-1, 128).T

    w1, w3, w2 = get("ffn_w1"), get("ffn_w3"), get("ffn_w2")
    ffn = [chunked(w[e]).reshape(128, -1) for e in range(w1.shape[0]) for w in (w1, w3, w2)]
    ffn += [chunked(get(n)).reshape(128, -1) for n in ("ffn_ws1", "ffn_ws3", "ffn_ws2")]
    tokens, slot_tile, experts = get("attn_x").shape[0] * get("attn_x").shape[1], 512, w1.shape[0]
    arrays = {
        "x": get("attn_x"),
        "attn_w": _np.stack([chunked(get(n)) for n in ("attn_Wk", "attn_Wv", "attn_Wr", "attn_Wo")], 1),
        "mix": _np.stack([columns(get(n)) for n in ("attn_mix_k", "attn_mix_v", "attn_mix_r")], 1),
        "decay": columns(get("attn_spatial_decay")),
        "first": columns(get("attn_spatial_first")),
        "ident": _np.eye(128, dtype=_np.float32),
        "tri": _np.triu(_np.ones((128, 128), _np.float32), 1),
        "ones": _np.ones((128, 128), _np.float32),
        "limits": _np.arange(0, tokens, slot_tile, dtype=_np.float32)[None],
        "rank_start": _np.arange(experts - 1, -1, -1, dtype=_np.float32)[None],
        "ffn_w": _np.concatenate(ffn, 1),
        "expert_biases": _np.stack([_np.stack([columns(b[e]) for b in (get("ffn_b1"), get("ffn_b3"))], 1)
                                    for e in range(w1.shape[0])], 0),
        "shared_biases": _np.stack([columns(get("ffn_bs1")), columns(get("ffn_bs3"))], 1),
        "gate_w": chunked(get("ffn_gate_w")),
        "gate_b": get("ffn_gate_b")[None],
        "numbers": _np.arange(0, 2 * tokens, 2, dtype=_np.float32).reshape(-1, 128).T,
        "tile_slots": _np.arange((2 * tokens + experts * (slot_tile - 1)) // slot_tile, dtype=_np.float32)[None] * slot_tile,
        "own_rows": _np.arange(slot_tile, dtype=_np.float32).reshape(-1, 128).T,
        "region_start": _np.arange(experts, dtype=_np.float32)[None] * (tokens + slot_tile),
        "earlier": _np.tril(_np.ones((experts, experts), _np.float32), -1).reshape(1, -1),
        "out_biases": _np.concatenate([get("ffn_b2"), get("ffn_bs2")[None]], 0),
    }
    nc = _bacc.Bacc("TRN2", target_bir_lowering=False, num_devices=1)
    args = {}
    for name in arrays:
        a = arrays[name] = _np.ascontiguousarray(arrays[name])
        args[name] = nc.dram_tensor(name, a.shape, _mybir.dt.from_np(a.dtype), kind="ExternalInput").ap()
    args["out"] = nc.dram_tensor("out", arrays["x"].shape, _mybir.dt.float32, kind="ExternalOutput").ap()
    sandwich(nc, **args)
    r = _run(nc, [arrays], core_ids=[0])
    return r.results[0]["out"]
```
